# Optimizing a Trainium2 kernel written in Bass

```python
import numpy as np
import jax
import jax.numpy as jnp

def _softmax(x, axis=-1):
    return jax.nn.softmax(x, axis=axis)

def _gelu(x):
    return jax.nn.gelu(x, approximate=True)

def _silu(x):
    return jax.nn.silu(x)

def _sigmoid(x):
    return jax.nn.sigmoid(x)

def _layernorm(x, axis=-1, eps=1e-05):
    m = jnp.mean(x, axis=axis, keepdims=True)
    v = jnp.var(x, axis=axis, keepdims=True)
    return (x - m) / jnp.sqrt(v + eps)

def _scatter_add(tgt, idx, src, axis=0):
    return tgt.at[idx].add(src)

def _segment_sum(src, seg, n):
    return jax.ops.segment_sum(src, seg, n)
kernel_name = 'mk_adj_preln_d2_adj_r2_3f9fc4'

def setup_inputs(seed: int=0):
    np.random.seed(seed)
    _w = jnp.asarray

    def _rec_inputs():
        import jax
        import jax.numpy as jnp
        _gk = jax.random.key(seed)
        x = -0.0002928 + 1 * jax.random.normal(jax.random.fold_in(_gk, 1), (4096, 256), jnp.float32)
        _w = (1.0 + jnp.arange(4096, dtype=jnp.float32)) ** (-0.5)
        _w = _w / _w.mean()
        _pij = jnp.clip(0.000976562 * _w[:, None] * _w[None, :], 0.0, 1.0)
        _a = jax.random.uniform(jax.random.fold_in(_gk, 2), (4096, 4096)) < _pij
        _a = jnp.logical_or(_a, jnp.eye(4096, dtype=bool))
        _af = _a.astype(jnp.float32)
        _af = _af * jax.random.uniform(jax.random.fold_in(_gk, 3), (4096, 4096), jnp.float32, 0.05, 1)
        adj = _af
        return (x, adj)
    x, adj = _rec_inputs()

    def _L0_gnn_setup():
        import jax, jax.numpy as jnp
        import numpy as np
        EPS = 1e-08
        key = jax.random.key(seed)
        k1, k2, k3, k4 = jax.random.split(key, 4)
        N, IN, OUT = (4096, 256, 256)
        x = jax.random.normal(k1, (N, IN), dtype=jnp.float32)
        adj = jax.random.uniform(k2, (N, N), dtype=jnp.float32)
        W = jax.random.normal(k3, (OUT, IN), dtype=jnp.float32) * (1.0 / np.sqrt(IN))
        b = jax.random.normal(k4, (OUT,), dtype=jnp.float32) * 0.01
        return {'x': x, 'adj': adj, 'W': W, 'b': b}
    _L0_gnn_all = _L0_gnn_setup()
    _L0_gnn_in = {k: v for k, v in _L0_gnn_all.items() if k in ('W', 'b')}
    del _L0_gnn_all

    def _L1_gnn_setup():
        import jax, jax.numpy as jnp
        import numpy as np
        N = 2048
        DIM_IN = 256
        DIM_Q = 256
        DIM_K = 256
        N_GRAPHS = 32
        key = jax.random.key(seed)
        ks = jax.random.split(key, 9)
        x = jax.random.normal(ks[0], (N, DIM_IN), dtype=jnp.float32)
        b = jax.random.normal(ks[1], (N, N), dtype=jnp.float32)
        edge_encoding = jax.random.normal(ks[2], (N, N), dtype=jnp.float32)
        ptr = jnp.arange(N_GRAPHS + 1, dtype=jnp.int64) * (N // N_GRAPHS)
        s_in = 1.0 / np.sqrt(DIM_IN)
        Wq = jax.random.normal(ks[3], (DIM_Q, DIM_IN), dtype=jnp.float32) * s_in
        bq = jnp.zeros((DIM_Q,), dtype=jnp.float32)
        Wk = jax.random.normal(ks[4], (DIM_K, DIM_IN), dtype=jnp.float32) * s_in
        bk = jnp.zeros((DIM_K,), dtype=jnp.float32)
        Wv = jax.random.normal(ks[5], (DIM_K, DIM_IN), dtype=jnp.float32) * s_in
        bv = jnp.zeros((DIM_K,), dtype=jnp.float32)
        return {'x': x, 'b': b, 'edge_encoding': edge_encoding, 'ptr': ptr, 'Wq': Wq, 'bq': bq, 'Wk': Wk, 'bk': bk, 'Wv': Wv, 'bv': bv}
    _L1_gnn_all = _L1_gnn_setup()
    _L1_gnn_in = {k: v for k, v in _L1_gnn_all.items() if k in ('ptr', 'Wq', 'bq', 'Wk', 'bk', 'Wv', 'bv')}
    del _L1_gnn_all
    return {'x': x, 'adj': adj, 'L0_gnn_W': _L0_gnn_in['W'], 'L0_gnn_b': _L0_gnn_in['b'], 'L1_gnn_ptr': _L1_gnn_in['ptr'], 'L1_gnn_Wq': _L1_gnn_in['Wq'], 'L1_gnn_bq': _L1_gnn_in['bq'], 'L1_gnn_Wk': _L1_gnn_in['Wk'], 'L1_gnn_bk': _L1_gnn_in['bk'], 'L1_gnn_Wv': _L1_gnn_in['Wv'], 'L1_gnn_bv': _L1_gnn_in['bv']}

def reference(x, adj, L0_gnn_W, L0_gnn_b, L1_gnn_ptr, L1_gnn_Wq, L1_gnn_bq, L1_gnn_Wk, L1_gnn_bk, L1_gnn_Wv, L1_gnn_bv):
    import jax
    import jax.numpy as jnp

    def _L0_gnn_ref(x, adj, W, b):
        import jax, jax.numpy as jnp
        import numpy as np
        EPS = 1e-08
        deg = adj.sum(axis=1)
        dis = (deg + EPS) ** (-0.5)
        a_norm = dis[:, None] * adj * dis[None, :]
        h = a_norm @ x
        return h @ W.T + b

    def _L1_gnn_ref(x, b, edge_encoding, ptr, Wq, bq, Wk, bk, Wv, bv):
        import jax, jax.numpy as jnp
        import numpy as np
        N = 2048
        DIM_IN = 256
        DIM_Q = 256
        DIM_K = 256
        N_GRAPHS = 32
        n = x.shape[0]
        graph_id = jnp.searchsorted(ptr, jnp.arange(n), side='right') - 1
        mask = graph_id[:, None] == graph_id[None, :]
        query = x @ Wq.T + bq
        key = x @ Wk.T + bk
        value = x @ Wv.T + bv
        scale = 1.0 / jnp.sqrt(jnp.float32(query.shape[-1]))
        a = jnp.where(mask, query @ key.T * scale, 0.0)
        scores = (a + b + edge_encoding) * jnp.where(mask, 1.0, -1000000.0)
        softmax = jax.nn.softmax(scores, axis=-1) * mask
        return softmax @ value
    h = jnp.maximum(_layernorm(x, axis=-1), 0.0)
    x = x + _L0_gnn_ref(h, adj, L0_gnn_W, L0_gnn_b)
    h = jnp.maximum(_layernorm(x, axis=-1), 0.0)
    x = x + _L1_gnn_ref(h, adj, adj, L1_gnn_ptr, L1_gnn_Wq, L1_gnn_bq, L1_gnn_Wk, L1_gnn_bk, L1_gnn_Wv, L1_gnn_bv)
    return x

_drawn_inputs = setup_inputs


def setup_inputs(seed=0):
    import zlib

    import numpy as np

    out = dict(_drawn_inputs(seed))
    spreads = {'L1_gnn_bq': (0.0, 2.0), 'L1_gnn_bk': (0.0, 0.8), 'L1_gnn_bv': (0.0, 0.1)}
    factors = {'L0_gnn_b': 7.009, 'L1_gnn_Wq': 3.278}
    for name, (base, spread) in spreads.items():
        noise = np.random.default_rng([zlib.crc32(name.encode()), seed]).standard_normal(out[name].shape)
        drawn = base * np.exp(spread * noise) if base else spread * noise
        out[name] = jnp.asarray(drawn.astype(out[name].dtype))
    for name, factor in factors.items():
        out[name] = (out[name] * factor).astype(out[name].dtype)
    return out
```

```python
from contextlib import ExitStack

import concourse.bass as bass
from concourse import mybir

F32 = mybir.dt.float32
F32R = mybir.dt.float32r
BF16 = mybir.dt.bfloat16
I32 = mybir.dt.int32
U8 = mybir.dt.uint8
ALU = mybir.AluOpType
ACT = mybir.ActivationFunctionType
AX_X = mybir.AxisListType.X

P = 128
N = 4096
D = 256
KD = D // P
TILES = N // P
GRP = 4
GROUPS = TILES // GRP
CW = 512
CHUNKS = N // CW
STEPS = GROUPS * CHUNKS
CT = CW // P
HALF = N // 2
HCH = CHUNKS // 2
HT = TILES // 2
BANKS = 8
NPTR = 33
BIG = 2.0 ** 100
OFF = 2e6
EPS_DEG = 1e-8
EPS_LN = 1e-5


def gnn_kernel(nc, x, adj, adjT, W0T, b0, ptr, WqT, bq, WkT, bk, WvT, bv, out):
    with ExitStack() as ctx:
        cursor = [nc.sbuf_base + (-nc.sbuf_base) % 32]

        def at(name, shape, dt, offset=None):
            size = {F32: 4, F32R: 4, I32: 4, BF16: 2, U8: 1}[dt]
            for n in shape[1:]:
                size *= n
            size += -size % 32
            if offset is None:
                offset = cursor[0]
                cursor[0] += size
            assert offset + size <= nc.sbuf_usable_end, (name, offset + size, nc.sbuf_usable_end)
            return nc.alloc_sbuf_tensor_at(name, shape, dt, offset=offset), offset

        def sb(name, shape, dt, offset=None):
            return at(name, shape, dt, offset)[0]

        def sem(name):
            return ctx.enter_context(nc.semaphore(name))

        penn = sb("penn", [P, HT, P], BF16)
        gidrow = sb("gidrow", [P, N], U8)
        gidcol = sb("gidcol", [P, TILES], F32)
        deg = sb("deg", [P, TILES], F32)
        dis = sb("dis", [P, TILES], F32)
        mn = sb("mn", [P, TILES], F32)
        nboff = sb("nboff", [P, TILES], F32)
        zz = sb("zz", [P, 2, TILES], F32)
        nmx = sb("nmx", [P, TILES], F32)
        nm = sb("nm", [P, TILES], F32)
        dd = sb("dd", [P, 2, TILES], F32)
        ee = sb("ee", [P, 2, TILES], F32)
        coef = sb("coef", [P, TILES], F32)
        ident = sb("ident", [P, P], F32)
        bcols = sb("bcols", [P, 2, KD], F32)
        b0row = sb("b0row", [P, D], F32)
        bvrow = sb("bvrow", [P, D], F32)
        ptri = sb("ptri", [NPTR, 1], I32)
        ptrf = sb("ptrf", [NPTR, 1], F32)
        ones33 = sb("ones33", [NPTR, P], BF16)
        flagw = sb("flagw", [1, 32], F32)
        flag = sb("flag", [1, 1], I32)
        mhalf = sb("mhalf", [P, GRP], F32)
        epsdeg = sb("epsdeg", [P, GRP], F32)
        bnst = sb("bnst", [P, GRP, 6], F32)
        mv = sb("mv", [P, GRP, 2], F32)
        pw = sb("pw", [P, 4, GRP], F32)
        hs = [sb(f"hs{i}", [P, 2, GRP], F32) for i in range(2)]
        mx4 = sb("mx4", [P, CT], F32)

        regK = cursor[0]
        QTh = sb("QTh", [P, KD, HALF], F32R)
        QTl = sb("QTl", [P, KD, HALF], F32R)
        KTh = sb("KTh", [P, KD, HALF], F32R)
        KTl = sb("KTl", [P, KD, HALF], F32R)
        Vh = sb("Vh", [P, HT, D], F32R)
        Vl = sb("Vl", [P, HT, D], F32R)
        endK = cursor[0]
        cursor[0] = regK
        raw = [sb(f"raw{i}", [P, GRP, CW], F32) for i in range(4)]
        regS = cursor[0]
        ahi = [sb(f"ahi{i}", [P, GRP, CW], F32R) for i in range(2)]
        alo = [sb(f"alo{i}", [P, GRP, CW], F32R) for i in range(2)]
        Ghi = [sb(f"Ghi{i}", [P, GRP, D], F32R) for i in range(2)]
        Glo = [sb(f"Glo{i}", [P, GRP, D], F32R) for i in range(2)]
        gf = sb("gf", [P, GRP, D], F32)
        xg = [sb(f"xg{i}", [P, GRP, D], F32) for i in range(2)]
        masktmp = sb("masktmp", [P, 1024], BF16)
        assert cursor[0] <= endK
        iota = sb("iota", [NPTR, N], I32, regS)
        cmp = sb("cmp", [NPTR, N], BF16, regS + 4 * N)
        cursor[0] = endK

        regA = cursor[0]
        aggT = sb("aggT", [P, KD, N], F32)
        adjr = [sb(f"adjr{i}", [P, HALF], F32, regA + 4 * HALF * i) for i in range(2)]
        SE = [sb(f"SE{i}", [P, HALF], F32, regA + 4 * HALF * (2 + i)) for i in range(2)]

        regR = cursor[0]
        row = [sb(f"row{i}", [P, N], F32) for i in range(4)]
        endR = cursor[0]
        cursor[0] = regR
        Whi = sb("Whi", [P, 4, KD, D], F32R)
        Wlo = sb("Wlo", [P, 4, KD, D], F32R)
        regPT = cursor[0]
        Ahi = sb("Ahi", [P, KD, CW], F32R)
        Alo = sb("Alo", [P, KD, CW], F32R)
        regH = cursor[0]
        hTh = sb("hTh", [P, KD, CW], F32R)
        hTl = sb("hTl", [P, KD, CW], F32R)
        hn = sb("hn", [P, CT, D], F32)
        xc = sb("xc", [P, CT, D], F32)
        regX = cursor[0]
        x1 = [sb(f"x1_{i}", [P, CT, D], F32) for i in range(3)]
        Wraw = sb("Wraw", [P, 4, KD, D], F32, regX)
        vf = [sb(f"vf{i}", [P, CW], F32) for i in range(2)]
        adjd = sb("adjd", [P, CT, P], F32)
        Sd = sb("Sd", [P, CT, P], F32)
        Ed = sb("Ed", [P, CT, P], F32)
        PTdh = sb("PTdh", [P, CW], F32R)
        PTdl = sb("PTdl", [P, CW], F32R)
        cursor[0] = max(cursor[0], endR)
        PTh = [sb(f"PTh{i}", [P, CW], F32R, regPT + 4 * CW * i) for i in range(2)]
        PTl = [sb(f"PTl{i}", [P, CW], F32R, regPT + 4 * CW * (2 + i)) for i in range(2)]
        x1t = [sb(f"x1t{i}", [P, D], F32, regH + 4 * D * i) for i in range(2)]
        outb = [sb(f"outb{i}", [P, D], F32, regH + 4 * D * (2 + i)) for i in range(2)]
        Og = sb("Og", [P, D], F32, regH + 4 * D * 4)

        ps = [ctx.enter_context(nc.psum_tensor(f"ps{i}", [P, CW], F32)) for i in range(BANKS)]

        x1_d = nc.dram_tensor("x1_scratch", (N, D), F32, kind="Internal").ap()
        qh_d = nc.dram_tensor("qh_scratch", (P, KD, N), F32, kind="Internal").ap()
        ql_d = nc.dram_tensor("ql_scratch", (P, KD, N), F32, kind="Internal").ap()
        kh_d = nc.dram_tensor("kh_scratch", (P, KD, N), F32, kind="Internal").ap()
        kl_d = nc.dram_tensor("kl_scratch", (P, KD, N), F32, kind="Internal").ap()
        vh_d = nc.dram_tensor("vh_scratch", (P, TILES, D), F32, kind="Internal").ap()
        vl_d = nc.dram_tensor("vl_scratch", (P, TILES, D), F32, kind="Internal").ap()

        ptr_loaded = sem("ptr_loaded")
        bias_loaded = sem("bias_loaded")
        row_first = [sem(f"row_first{i}") for i in range(4)]
        row_loaded = [sem(f"row_loaded{i}") for i in range(4)]
        raw_loaded = [sem(f"raw_loaded{i}") for i in range(4)]
        xg_loaded = [sem(f"xg_loaded{i}") for i in range(2)]
        iota_done = sem("iota_done")
        const_done = sem("const_done")
        cmp_done = sem("cmp_done")
        gid_full = sem("gid_full")
        gid_copied = sem("gid_copied")
        setup_link = sem("setup_link")
        flag_ready = sem("flag_ready")
        rowsum_done = sem("rowsum_done")
        mask_link = sem("mask_link")
        masked = sem("masked")
        mn_done = sem("mn_done")
        nb_done = sem("nb_done")
        exp_done = sem("exp_done")
        bns_done = sem("bns_done")
        bn_done = sem("bn_done")
        pool_link = sem("pool_link")
        gscale_done = sem("gscale_done")
        gf_done = sem("gf_done")
        g_hi = sem("g_hi")
        g_lo = sem("g_lo")
        split_hi = sem("split_hi")
        split_lo = sem("split_lo")
        units = sem("units")
        acc_done = sem("acc_done")

        w_loaded = sem("w_loaded")
        w_hi = sem("w_hi")
        w_done = sem("w_done")
        x_loaded = sem("x_loaded")
        xb_done = sem("xb_done")
        a_hi = sem("a_hi")
        a_lo = sem("a_lo")
        z_full = sem("z_full")
        x1_done = sem("x1_done")
        x1_stored = [sem(f"x1_stored{i}") for i in range(3)]
        bns2_done = sem("bns2_done")
        bn2_done = sem("bn2_done")
        hscale_done = sem("hscale_done")
        h_done = sem("h_done")
        tr_full = sem("tr_full")
        ht_hi = sem("ht_hi")
        ht_lo = sem("ht_lo")
        ring_full = sem("ring_full")
        ring_free = sem("ring_free")
        proj_hi = sem("proj_hi")
        proj_lo = sem("proj_lo")
        adjd_loaded = sem("adjd_loaded")
        d_link = sem("d_link")
        nmx_done = sem("nmx_done")
        dd_done = sem("dd_done")
        dexp_done = sem("dexp_done")
        ee_done = sem("ee_done")
        ptd_hi = sem("ptd_hi")
        ptd_lo = sem("ptd_lo")
        dout_done = sem("dout_done")
        out_stored = sem("out_stored")
        spilled = sem("spilled")

        adjr_loaded = [sem(f"adjr_loaded{i}") for i in range(2)]
        x1t_loaded = [sem(f"x1t_loaded{i}") for i in range(2)]
        s_full = sem("s_full")
        s_read = sem("s_read")
        m_done = sem("m_done")
        ddt_done = sem("ddt_done")
        e_done = sem("e_done")
        eet_done = sem("eet_done")
        pt_full = sem("pt_full")
        pt_hi = sem("pt_hi")
        pt_lo = sem("pt_lo")
        o_full = sem("o_full")
        f_link = sem("f_link")
        o_read = sem("o_read")
        outt_stored = [sem(f"outt_stored{i}") for i in range(2)]

        g_load = sem("g_load")
        g_score = sem("g_score")
        g_link = sem("g_link")
        g_sd = sem("g_sd")
        g_exp = sem("g_exp")
        g_tr = sem("g_tr")
        g_phi = sem("g_phi")
        g_plo = sem("g_plo")
        g_pv = sem("g_pv")
        g_end = sem("g_end")
        g_out = sem("g_out")
        g_fin = sem("g_fin")
        nmm = sem("nmm")
        nmt = sem("nmt")

        def rows_of(t, n=1):
            return bass.ds(t * P, n * P)

        def tiles_of(a, t):
            return a[bass.ds(t * P, GRP * P), :].rearrange("(b p) d -> p b d", p=P)

        def ring_plan(fast):
            order = []
            for c in range(CHUNKS + 1):
                diag = fast and 1 <= c <= HCH
                if diag:
                    order.append(("PT", c - 1))
                if c < CHUNKS:
                    order += [("q", c, 0), ("q", c, 1), ("k", c, 0), ("k", c, 1)]
                if diag:
                    order += [("O", c - 1, 0), ("O", c - 1, 1)]
                if c < CHUNKS:
                    order += [("v", c, 0), ("v", c, 1)]
                if fast and c < HCH:
                    order.append(("S", c))
            return {k: i for i, k in enumerate(order)}

        RING = {True: ring_plan(True), False: ring_plan(False)}

        def mm3(e, o, lh, ll, rh, rl, first, last):
            e.matmul(o, lh, rh, start=first, stop=False)
            e.matmul(o, lh, rl, start=False, stop=False)
            return e.matmul(o, ll, rh, start=False, stop=last)

        unread = {e.engine: sem(f"unread_{k}") for k, e in enumerate((nc.sync, nc.vector, nc.gpsimd))}

        def wait_alone(e, semaphore, value):
            e.wait_ge(semaphore, value)
            e.sem_inc(unread[e.engine], 1)

        block = ctx.enter_context(nc.Block())

        @block.sync
        def _(sp):
            sp.dma_start(ptri[:, :], ptr).then_inc(ptr_loaded, 16)
            for t in range(4):
                sp.dma_start(row[t][:, :], adj[rows_of(t), :]).then_inc(row_first[t], 16)
                if t < 2:
                    sp.dma_start(xg[t][:, :, :], tiles_of(x, GRP * t)).then_inc(xg_loaded[t], 16)
            for s in range(4):
                sp.dma_start(raw[s][:, :, :], adjT[rows_of(s), :].rearrange("p (t i) -> p t i", t=GRP))\
                  .then_inc(raw_loaded[s], 16)
            sp.dma_start(bcols[:, 0, :], bq).then_inc(bias_loaded, 16)
            sp.dma_start(bcols[:, 1, :], bk).then_inc(bias_loaded, 16)
            sp.dma_start(b0row[:, :], b0.rearrange("(a d) -> a d", a=1).partition_broadcast(P))\
              .then_inc(bias_loaded, 16)
            sp.dma_start(bvrow[:, :], bv.rearrange("(a d) -> a d", a=1).partition_broadcast(P))\
              .then_inc(bias_loaded, 16)

            def group(g, par):
                if not isinstance(g, int) or g + 2 < GROUPS:
                    wait_alone(sp, gf_done, GRP * g + GRP)
                    sp.dma_start(xg[par][:, :, :], tiles_of(x, GRP * g + 2 * GRP)).then_inc(xg_loaded[par], 16)
                for c in range(CHUNKS):
                    s = CHUNKS * g + c
                    if not isinstance(g, int) or s + 4 < STEPS:
                        wait_alone(sp, split_lo, s + 1)
                        sp.dma_start(raw[c % 4][:, :, :],
                                     adjT[bass.ds(s * P + 4 * P, P), :].rearrange("p (t i) -> p t i", t=GRP))\
                          .then_inc(raw_loaded[c % 4], 16)

            with sp.Fori(0, 3) as u:
                group(u * 2, 0)
                group(u * 2 + 1, 1)
            group(6, 0)
            group(7, 1)

            sp.wait_ge(exp_done, TILES)
            for i, w in enumerate((W0T, WqT, WkT, WvT)):
                sp.dma_start(Wraw[:, i, :, :], w.rearrange("(k p) o -> p k o", p=P)).then_inc(w_loaded, 16)
            sp.dma_start(xc[:, :, :], tiles_of(x, 0)).then_inc(x_loaded, 16)
            sp.wait_ge(flag_ready, 1)
            fast_reg = sp.value_load(flag[0:1, 0:1], min_val=0, max_val=1)

            def load_adjd(c):
                for b in range(CT):
                    t = CT * c + b
                    sp.dma_start(adjd[:, b, :], adj[t * P:t * P + P, t * P:t * P + P]).then_inc(adjd_loaded, 16)

            def chunks(fast):
                if fast:
                    load_adjd(0)
                for c in range(-1, CHUNKS + 1):
                    if c + 1 < CHUNKS:
                        sp.wait_ge(x1_done, CT * (c + 2))
                        if c + 2 < CHUNKS:
                            sp.dma_start(xc[:, :, :], tiles_of(x, CT * (c + 2))).then_inc(x_loaded, 16)
                        if not fast or c + 1 >= HCH:
                            sp.dma_start(tiles_of(x1_d, CT * (c + 1)), x1[(c + 1) % 3][:, :, :])\
                              .then_inc(x1_stored[(c + 1) % 3], 16)
                    if fast and 1 <= c <= HCH:
                        sp.wait_ge(dout_done, CT * c)
                        sp.dma_start(tiles_of(out, CT * (c - 1)), x1[(c - 1) % 3][:, :, :])\
                          .then_inc(x1_stored[(c - 1) % 3], 16)
                    if fast and 0 <= c < HCH - 1:
                        sp.wait_ge(d_link, 2 * c + 1)
                        load_adjd(c + 1)
                    if not fast and 0 <= c < CHUNKS:
                        sp.wait_ge(proj_lo, 6 * c + 6)
                        k = c % HCH
                        for d_, s_ in ((qh_d, QTh), (ql_d, QTl), (kh_d, KTh), (kl_d, KTl)):
                            sp.dma_start(d_[:, :, CW * c:CW * c + CW], s_[:, :, CW * k:CW * k + CW].bitcast(F32))\
                              .then_inc(spilled, 16)
                        for d_, s_ in ((vh_d, Vh), (vl_d, Vl)):
                            sp.dma_start(d_[:, CT * c:CT * c + CT, :], s_[:, CT * k:CT * k + CT, :].bitcast(F32))\
                              .then_inc(spilled, 16)
                for i in range(3):
                    sp.wait_ge(x1_stored[i], 16 * len(range(i, CHUNKS, 3)))

            def rows_for(i, par):
                sp.dma_start(adjr[par][:, :], adj[bass.ds(i * P + HALF, P), HALF:N]).then_inc(adjr_loaded[par], 16)
                sp.dma_start(x1t[par][:, :], x1_d[bass.ds(i * P + HALF, P), :]).then_inc(x1t_loaded[par], 16)

            def store_rows(i, par):
                wait_alone(sp, o_read, i + 1)
                sp.dma_start(out[bass.ds(i * P + HALF, P), :], outb[par][:, :]).then_inc(outt_stored[par], 16)

            with sp.If(fast_reg == 1):
                chunks(True)
                sp.wait_ge(a_lo, CHUNKS)
                sp.wait_ge(ring_full, RING[True][("v", CHUNKS - 1, 1)] + 1)
                rows_for(0, 0)
                rows_for(1, 1)
                with sp.Fori(0, HT // 2 - 1) as v:
                    for par in range(2):
                        i = v * 2 + par
                        wait_alone(sp, s_read, i * CT + CT)
                        sp.dma_start(adjr[par][:, :], adj[bass.ds(i * P + 2 * P + HALF, P), HALF:N])\
                          .then_inc(adjr_loaded[par], 16)
                        store_rows(i, par)
                        sp.dma_start(x1t[par][:, :], x1_d[bass.ds(i * P + 2 * P + HALF, P), :])\
                          .then_inc(x1t_loaded[par], 16)
                store_rows(HT - 2, 0)
                store_rows(HT - 1, 1)
                sp.wait_ge(outt_stored[0], 16 * HT // 2)
                sp.wait_ge(outt_stored[1], 16 * HT // 2)
            with sp.Else():
                chunks(False)
                sp.wait_ge(spilled, 16 * 6 * CHUNKS)
                with sp.Fori(0, TILES) as t:
                    with sp.Fori(0, CHUNKS) as c:
                        wait_alone(sp, g_end, t * CHUNKS + c + 1)
                        for d_, s_ in ((qh_d, QTh), (ql_d, QTl)):
                            sp.dma_start(s_[:, :, 0:P].bitcast(F32), d_[:, :, rows_of(t)]).then_inc(g_load, 16)
                        for d_, s_ in ((kh_d, KTh), (kl_d, KTl)):
                            sp.dma_start(s_[:, :, 0:CW].bitcast(F32), d_[:, :, bass.ds(c * CW, CW)]).then_inc(g_load, 16)
                        for d_, s_ in ((vh_d, Vh), (vl_d, Vl)):
                            sp.dma_start(s_[:, 0:CT, :].bitcast(F32), d_[:, bass.ds(c * CT, CT), :]).then_inc(g_load, 16)
                        sp.dma_start(adjr[0][:, 0:CW], adj[rows_of(t), bass.ds(c * CW, CW)]).then_inc(g_load, 16)
                        sp.dma_start(x1t[0][:, :], x1_d[rows_of(t), :]).then_inc(g_load, 16)
                    wait_alone(sp, g_out, t + 1)
                    sp.dma_start(out[rows_of(t), :], outb[0][:, :]).then_inc(outt_stored[0], 16)
                    wait_alone(sp, outt_stored[0], t * 16 + 16)
                sp.nop()

        @block.gpsimd
        def _(pool):
            pool.iota(iota[:, :], pattern=[[1, N]], base=0, channel_multiplier=0).then_inc(iota_done, 1)
            pool.memset(ident[:, :], 0.0).then_inc(pool_link, 1)
            pool.memset(mhalf[:, :], -0.5).then_inc(const_done, 1)
            pool.memset(epsdeg[:, :], EPS_DEG).then_inc(const_done, 1)
            pool.memset(ones33[:, :], 1.0).then_inc(const_done, 1)
            pool.wait_ge(pool_link, 1)
            pool.affine_select(out=ident[:, :], in_=ident[:, :], compare_op=ALU.not_equal, fill=1.0, base=0,
                               pattern=[[-1, P]], channel_multiplier=1).then_inc(const_done, 1)
            pool.wait_ge(const_done, 4)
            LINKS = 3

            def scales(gs, par):
                n = gs * LINKS + 1
                r = gs * GRP
                pool.wait_ge(rowsum_done, r + GRP)
                pool.wait_ge(bn_done, r + GRP)
                pool.wait_ge(const_done, 4)
                pool.tensor_tensor(pw[:, 0, :], deg[:, bass.ds(r, GRP)], epsdeg[:, :], ALU.add)
                pool.tensor_scalar(pw[:, 1, :], mv[:, :, 1], EPS_LN, None, ALU.add).then_inc(pool_link, 1)
                wait_alone(pool, pool_link, n + 1)
                pool.tensor_tensor(dis[:, bass.ds(r, GRP)], pw[:, 0, :], mhalf[:, :], ALU.pow)
                pool.tensor_tensor(pw[:, 2, :], pw[:, 1, :], mhalf[:, :], ALU.pow)
                pool.tensor_scalar(pw[:, 3, :], mv[:, :, 0], -1.0, None, ALU.mult).then_inc(pool_link, 1)
                wait_alone(pool, pool_link, n + 2)
                pool.tensor_tensor(hs[par][:, 0, :], pw[:, 2, :], dis[:, bass.ds(r, GRP)], ALU.mult)\
                    .then_inc(pool_link, 1)
                pool.wait_ge(pool_link, n + 3)
                pool.tensor_tensor(hs[par][:, 1, :], hs[par][:, 0, :], pw[:, 3, :], ALU.mult)\
                    .then_inc(gscale_done, 1)

            def next_row(r, slot):
                pool.wait_ge(exp_done, r + 1)
                pool.dma_start(row[slot][:, :], adj[bass.ds(r * P + 4 * P, P), :]).then_inc(row_loaded[slot], 16)

            for r in range(4):
                next_row(r, r)
            scales(0, 0)
            next_row(4, 0)

            def group(g, par):
                for c in range(1, CHUNKS, 2):
                    r = GRP * g + 5 + c // 2
                    if not isinstance(g, int) or r + 4 < TILES:
                        next_row(r, (1 + c // 2) % 4)
                    if c == 3 and (not isinstance(g, int) or g + 1 < GROUPS):
                        scales(g + 1, 1 - par)

            with pool.Fori(0, 2) as u:
                group(u * 2, 0)
                group(u * 2 + 1, 1)
            for g in range(4, GROUPS):
                group(g, g % 2)

            pool.wait_ge(bias_loaded, 16 * 4)
            for c in range(CHUNKS):
                pool.wait_ge(x_loaded, 16 * (c + 1))
                b0wide = b0row[:, :].rearrange("p (a d) -> p a d", a=1).to_broadcast([P, CT, D])
                pool.tensor_tensor(xc[:, :, :], xc[:, :, :], b0wide, ALU.add).then_inc(xb_done, 1)
                n = GROUPS * LINKS + 1 + 3 * c
                pool.wait_ge(bn2_done, CT * (c + 1))
                pool.tensor_scalar(pw[:, 1, :], mv[:, :, 1], EPS_LN, None, ALU.add)
                pool.tensor_scalar(pw[:, 3, :], mv[:, :, 0], -1.0, None, ALU.mult).then_inc(pool_link, 1)
                pool.wait_ge(pool_link, n + 1)
                if c >= 2:
                    pool.wait_ge(h_done, CT * (c - 1))
                pool.tensor_tensor(hs[c % 2][:, 0, :], pw[:, 1, :], mhalf[:, :], ALU.pow).then_inc(pool_link, 1)
                pool.wait_ge(pool_link, n + 2)
                pool.tensor_tensor(hs[c % 2][:, 1, :], hs[c % 2][:, 0, :], pw[:, 3, :], ALU.mult)\
                    .then_inc(hscale_done, 1)
                pool.wait_ge(hscale_done, c + 1)
                pool.memset(pw[:, 0, 0:1], 0.0).then_inc(pool_link, 1)
                pool.wait_ge(pool_link, n + 3)

        @block.scalar
        def _(act):
            def rowsum(r, slot):
                if isinstance(r, int) and r < 4:
                    act.wait_ge(row_first[slot], 16)
                else:
                    act.wait_ge(row_loaded[slot], r * 4 - slot * 4)
                act.activation(row[slot][:, :], row[slot][:, :], ACT.Copy, accum_out=deg[:, bass.ds(r, 1)])\
                   .then_inc(rowsum_done, 1)

            def exp_row(r, slot, width):
                act.activation(row[slot][:, 0:width], row[slot][:, 0:width], ACT.Exp,
                               bias=nboff[:, bass.ds(r, 1)], scale=-OFF,
                               accum_out=zz[:, 1, bass.ds(r, 1)]).then_inc(exp_done, 1)

            def split(s, c):
                act.wait_ge(raw_loaded[c % 4], s * 4 - (c % 4) * 4 + 16)
                act.wait_ge(units, s * 2 + 2)
                act.activation(ahi[c % 2][:, :, :], raw[c % 4][:, :, :], ACT.Copy).then_inc(split_hi, 1)

            def features(gs, par):
                act.wait_ge(gscale_done, gs + 1)
                if not isinstance(gs, int) or gs:
                    act.wait_ge(g_lo, gs)
                for b in range(GRP):
                    act.activation(gf[:, b, :], xg[par][:, b, :], ACT.Relu, bias=hs[par][:, 1, b:b + 1],
                                   scale=hs[par][:, 0, b:b + 1]).then_inc(gf_done, 1)
                act.wait_ge(gf_done, gs * GRP + GRP)
                act.activation(Ghi[par][:, :, :], gf[:, :, :], ACT.Copy).then_inc(g_hi, 1)

            for r in range(4):
                rowsum(r, r)
                act.wait_ge(nb_done, r + 1)
                exp_row(r, r, N)
            act.wait_ge(gid_copied, BANKS + 1)
            split(0, 0)
            features(0, 0)
            rowsum(4, 0)
            act.wait_ge(nb_done, 5)
            exp_row(4, 0, N)
            act.wait_ge(flag_ready, 1)
            fast_reg = act.value_load(flag[0:1, 0:1], min_val=0, max_val=1)

            def group(g, par):
                static = isinstance(g, int)
                for c in range(CHUNKS):
                    s = CHUNKS * g + c
                    if not static or s + 1 < STEPS:
                        split(s + 1, (c + 1) % CHUNKS)
                    r = GRP * g + 5 + c // 2
                    slot = (1 + c // 2) % 4
                    if not static or r < TILES:
                        if c % 2 == 0:
                            rowsum(r, slot)
                        else:
                            act.wait_ge(nb_done, r + 1)
                            if not static or r >= HT:
                                cond = fast_reg == 1 if static else (fast_reg * HT + r) >= 2 * HT
                                with act.If(cond):
                                    exp_row(r, slot, HALF)
                                with act.Else():
                                    exp_row(r, slot, N)
                            else:
                                exp_row(r, slot, N)
                    if c == 6 and (not static or g + 1 < GROUPS):
                        features(g + 1, 1 - par)

            with act.Fori(0, 3) as u:
                group(u * 2, 0)
                group(u * 2 + 1, 1)
            group(6, 0)
            group(7, 1)

            for i in range(4):
                act.wait_ge(w_loaded, 64)
                act.activation(Whi[:, i, :, :], Wraw[:, i, :, :], ACT.Copy, scale=1.0 / 32 if i == 1 else 1.0)\
                   .then_inc(w_hi, 1)

            def split_agg(c):
                act.wait_ge(acc_done, BANKS + 2 * (STEPS - CHUNKS + c) + 2)
                if c:
                    act.wait_ge(z_full, CT * c)
                act.activation(Ahi[:, :, :], aggT[:, :, CW * c:CW * c + CW], ACT.Copy).then_inc(a_hi, 1)

            def hidden(c):
                act.wait_ge(hscale_done, c + 1)
                if c:
                    act.wait_ge(tr_full, KD * c)
                for b in range(CT):
                    act.activation(hn[:, b, :], x1[c % 3][:, b, :], ACT.Relu, bias=hs[c % 2][:, 1, b:b + 1],
                                   scale=hs[c % 2][:, 0, b:b + 1]).then_inc(h_done, 1)

            def split_hT(c, ring):
                if c:
                    act.wait_ge(ring_full, ring[("v", c - 1, 1)] + 1)
                for k in range(KD):
                    act.wait_ge(tr_full, KD * c + k + 1)
                    act.activation(hTh[:, k, :], ps[2 + k][:, :], ACT.Copy).then_inc(ht_hi, 1)

            def chunks(fast):
                ring = RING[fast]
                split_agg(0)
                hidden(0)
                split_agg(1)
                split_hT(0, ring)
                for c in range(CHUNKS + 1):
                    diag = fast and 1 <= c <= HCH
                    k = c % HCH
                    if diag:
                        n = ring[("PT", c - 1)]
                        act.wait_ge(ring_full, n + 1)
                        if c > 1:
                            act.wait_ge(ring_full, ring[("O", c - 2, 1)] + 1)
                        act.activation(PTdh[:, :], ps[4 + n % 4][:, :], ACT.Copy).then_inc(ptd_hi, 1)
                    if c < CHUNKS:
                        if c >= HCH:
                            if fast:
                                act.wait_ge(ring_full, ring[("O", c - HCH, 1)] + 1)
                            else:
                                act.wait_ge(spilled, 16 * 6 * (c - HCH + 1))
                        for j, (dst, key) in enumerate(((QTh, "q"), (KTh, "k"))):
                            for o in range(KD):
                                n = ring[(key, c, o)]
                                act.wait_ge(ring_full, n + 1)
                                act.activation(dst[:, o, CW * k:CW * k + CW], ps[4 + n % 4][:, :], ACT.Identity,
                                               bias=bcols[:, j, o:o + 1]).then_inc(proj_hi, 1)
                        if c + 1 < CHUNKS:
                            hidden(c + 1)
                        for i in range(2):
                            act.wait_ge(ring_free, ring[("v", c, i)] + 1)
                            act.activation(Vh[:, CT * k + 2 * i:CT * k + 2 * i + 2, :].rearrange("p a d -> p (a d)"),
                                           vf[i][:, :], ACT.Copy).then_inc(proj_hi, 1)
                        if c + 2 < CHUNKS:
                            split_agg(c + 2)
                    if fast and c < HCH:
                        if c:
                            act.wait_ge(ring_full, ring[("PT", c - 1)] + 1)
                        act.wait_ge(nmx_done, c + 1)
                        for b in range(CT):
                            t = CT * c + b
                            act.activation(Ed[:, b, :], Sd[:, b, :], ACT.Exp, bias=nmx[:, t:t + 1],
                                           accum_out=zz[:, 0, t:t + 1]).then_inc(dexp_done, 1)
                        act.wait_ge(dd_done, c + 1)
                        act.activation(ee[:, :, CT * c:CT * c + CT], dd[:, :, CT * c:CT * c + CT], ACT.Exp)\
                           .then_inc(ee_done, 1)
                    if c + 1 < CHUNKS:
                        split_hT(c + 1, ring)

            def attend(i, par):
                act.wait_ge(m_done, i + 1)
                act.activation(SE[par][:, :], SE[par][:, :], ACT.Exp, bias=nmx[:, bass.ds(i + HT, 1)],
                               accum_out=zz[:, 0, bass.ds(i + HT, 1)]).then_inc(e_done, 1)
                act.wait_ge(ddt_done, i + 1)
                act.activation(ee[:, :, bass.ds(i + HT, 1)], dd[:, :, bass.ds(i + HT, 1)], ACT.Exp)\
                   .then_inc(eet_done, 1)

            def turned(i, q):
                act.wait_ge(pt_full, i * 4 + q + 1)
                act.activation(PTh[q % 2][:, :], ps[4 + q % 2][:, :], ACT.Copy).then_inc(pt_hi, 1)

            with act.If(fast_reg == 1):
                chunks(True)
                attend(0, 0)

                def tile(i, par):
                    for q in range(4):
                        turned(i, q)
                    if not isinstance(i, int) or i + 1 < HT:
                        attend(i + 1, 1 - par)

                with act.Fori(0, HT // 2 - 1) as v:
                    tile(v * 2, 0)
                    tile(v * 2 + 1, 1)
                tile(HT - 2, 0)
                tile(HT - 1, 1)
                act.nop()
            with act.Else():
                chunks(False)
                with act.Fori(0, TILES) as t:
                    with act.Fori(0, CHUNKS) as c:
                        n = t * CHUNKS + c
                        act.wait_ge(g_sd, n + 1)
                        act.activation(SE[1][:, 0:CW], SE[0][:, 0:CW], ACT.Exp, bias=nm[:, 0:1],
                                       accum_out=zz[:, 0, 0:1]).then_inc(g_exp, 1)
                        act.activation(ee[:, 0, 0:1], dd[:, 0, 0:1], ACT.Exp).then_inc(g_exp, 1)
                        act.wait_ge(g_tr, n + 1)
                        act.activation(PTh[0][:, :], ps[4][:, :], ACT.Copy).then_inc(g_phi, 1)
                act.nop()

        @block.vector
        def _(dve):
            dve.wait_ge(ptr_loaded, 16)
            dve.tensor_copy(ptrf[:, :], ptri[:, :]).then_inc(setup_link, 1)
            dve.wait_ge(setup_link, 1)
            dve.wait_ge(iota_done, 1)
            dve.tensor_scalar(cmp[:, :], iota[:, :], ptrf[:, 0:1], None, ALU.is_ge).then_inc(cmp_done, 1)
            for k in range(BANKS):
                dve.wait_ge(gid_full, k + 1)
                dve.tensor_copy(gidrow[:, CW * k:CW * k + CW], ps[k][:, :]).then_inc(gid_copied, 1)
            dve.wait_ge(gid_full, BANKS + 1)
            dve.tensor_copy(gidcol[:, :], ps[0][:, 0:TILES]).then_inc(gid_copied, 1)
            dve.wait_ge(gid_copied, BANKS + 1)
            for t in range(HT):
                dve.tensor_scalar(penn[:, t, :], gidrow[:, P * t:P * t + P], gidcol[:, t:t + 1], -BIG,
                                  ALU.not_equal, ALU.mult).then_inc(setup_link, 1)
            edges = gidrow[0:1, 0:HALF + P].rearrange("p (t q) -> p t q", q=P)
            dve.tensor_tensor(flagw[0:1, 0:HT], edges[:, 1:HT + 1, 0], edges[:, 0:HT, P - 1], ALU.is_gt)\
               .then_inc(setup_link, 1)
            dve.tensor_tensor(flagw[0:1, HT:HT + 1], gidrow[0:1, HALF:HALF + 1], gidrow[0:1, N - 1:N], ALU.is_equal)\
               .then_inc(setup_link, 1)
            dve.wait_ge(setup_link, HT + 3)
            dve.tensor_reduce(flag[0:1, 0:1], flagw[0:1, 0:HT + 1], AX_X, ALU.min).then_inc(flag_ready, 1)
            dve.wait_ge(flag_ready, 1)
            fast_reg = dve.value_load(flag[0:1, 0:1], min_val=0, max_val=1)

            def mask_rows(r, slot):
                for k in range(4):
                    m = r * 8 + 2 * k
                    cols = slice(1024 * k, 1024 * k + 1024)
                    dve.tensor_scalar(masktmp[:, :], gidrow[:, cols], gidcol[:, bass.ds(r, 1)], BIG,
                                      ALU.is_equal, ALU.mult).then_inc(mask_link, 1)
                    dve.wait_ge(mask_link, m + 1)
                    dve.tensor_tensor(row[slot][:, cols], row[slot][:, cols], masktmp[:, :], ALU.add)\
                       .then_inc(mask_link, 1)
                    dve.wait_ge(mask_link, m + 2)
                dve.tensor_reduce(mn[:, bass.ds(r, 1)], row[slot][:, :], AX_X, ALU.min).then_inc(mn_done, 1)

            def mask_tile(r, slot):
                own = row[slot][:, bass.ds(r * P, P)]
                dve.scalar_tensor_tensor(out=own, in0=penn[:, bass.ds(r, 1), :].rearrange("p a j -> p (a j)"),
                                         scalar=BIG, in1=own, op0=ALU.add, op1=ALU.add).then_inc(masked, 1)
                dve.wait_ge(masked, r + 1)
                dve.tensor_reduce(mn[:, bass.ds(r, 1)], row[slot][:, :], AX_X, ALU.min).then_inc(mn_done, 1)

            def least(r, slot):
                wait_alone(dve, rowsum_done, r + 1)
                if isinstance(r, int):
                    with dve.If(fast_reg == 1):
                        if r < HT:
                            mask_tile(r, slot)
                        else:
                            dve.tensor_reduce(mn[:, r:r + 1], row[slot][:, 0:HALF], AX_X, ALU.min).then_inc(mn_done, 1)
                    with dve.Else():
                        mask_rows(r, slot)
                else:
                    with dve.If(fast_reg == 1):
                        with dve.If(r < HT):
                            mask_tile(nc.s_assert_within(
                                r, 0, HT - 1, skip_runtime_bounds_check_because="the branch is taken for r < HT"), slot)
                        with dve.Else():
                            dve.tensor_reduce(mn[:, bass.ds(r, 1)], row[slot][:, 0:HALF], AX_X, ALU.min)\
                               .then_inc(mn_done, 1)
                        dve.nop()
                    with dve.Else():
                        mask_rows(r, slot)
                dve.wait_ge(mn_done, r + 1)
                dve.tensor_scalar(nboff[:, bass.ds(r, 1)], mn[:, bass.ds(r, 1)], OFF, None, ALU.mult)\
                   .then_inc(nb_done, 1)

            def moments(gs, par, bs):
                xl = (gs // 2) * 16 + 16 if isinstance(gs, int) else (gs - par) * 8 + 16
                dve.wait_ge(xg_loaded[par], xl)
                if bs[0] == 0 and not (isinstance(gs, int) and gs == 0):
                    dve.wait_ge(gscale_done, gs)
                for b in bs:
                    dve.bn_stats(bnst[:, b, :], xg[par][:, b, :]).then_inc(bns_done, 1)
                for b in bs:
                    wait_alone(dve, bns_done, gs * GRP + b + 1)
                    dve.bn_aggr(mv[:, b, :], bnst[:, b, :]).then_inc(bn_done, 1)

            def split(s, c):
                dve.wait_ge(split_hi, s + 1)
                dve.tensor_tensor(alo[c % 2][:, :, :], raw[c % 4][:, :, :], ahi[c % 2][:, :, :].bitcast(F32),
                                  ALU.subtract).then_inc(split_lo, 1)

            def features(gs, par):
                dve.wait_ge(g_hi, gs + 1)
                dve.tensor_tensor(Glo[par][:, :, :], gf[:, :, :], Ghi[par][:, :, :].bitcast(F32), ALU.subtract)\
                   .then_inc(g_lo, 1)

            moments(0, 0, (0, 1))
            moments(0, 0, (2, 3))
            least(0, 0)
            dve.memset(aggT[:, :, :], 0.0).then_inc(acc_done, BANKS)
            for r in range(1, 4):
                least(r, r)
            split(0, 0)
            features(0, 0)
            least(4, 0)

            def group(g, par):
                static = isinstance(g, int)
                for c in range(CHUNKS):
                    s = CHUNKS * g + c
                    if not static or s + 1 < STEPS:
                        split(s + 1, (c + 1) % CHUNKS)
                    r = GRP * g + 5 + c // 2
                    if c % 2 == 0 and (not static or r < TILES):
                        least(r, (1 + c // 2) % 4)
                    if c in (1, 3) and (not static or g + 1 < GROUPS):
                        moments(g + 1, 1 - par, (c - 1, c))
                    if c == 7 and (not static or g + 1 < GROUPS):
                        features(g + 1, 1 - par)
                    for k in range(KD):
                        dve.wait_ge(units, s * 2 + 5 + k)
                        dst = aggT[:, k, CW * c:CW * c + CW]
                        dve.tensor_tensor(dst, dst, ps[(2 * c + k) % BANKS][:, :], ALU.add).then_inc(acc_done, 1)

            with dve.Fori(0, 3) as u:
                group(u * 2, 0)
                group(u * 2 + 1, 1)
            group(6, 0)
            group(7, 1)

            for i in range(4):
                dve.wait_ge(w_hi, i + 1)
                dve.scalar_tensor_tensor(out=Wlo[:, i, :, :], in0=Wraw[:, i, :, :], scalar=1.0 / 32 if i == 1 else 1.0,
                                         in1=Whi[:, i, :, :].bitcast(F32), op0=ALU.mult, op1=ALU.subtract)\
                   .then_inc(w_done, 1)
            dve.wait_ge(bias_loaded, 16 * 4)
            dve.tensor_scalar(bcols[:, 0, :], bcols[:, 0, :], 1.0 / 32, None, ALU.mult).then_inc(w_done, 1)
            dve.wait_ge(w_done, 5)

            def split_agg(c):
                dve.wait_ge(a_hi, c + 1)
                dve.tensor_tensor(Alo[:, :, :], aggT[:, :, CW * c:CW * c + CW], Ahi[:, :, :].bitcast(F32),
                                  ALU.subtract).then_inc(a_lo, 1)

            def residual(c):
                dve.wait_ge(xb_done, c + 1)
                if c >= 3:
                    dve.wait_ge(x1_stored[c % 3], 16 * (c // 3))
                for b in range(CT):
                    t = CT * c + b
                    dve.wait_ge(z_full, t + 2 - b % 2)
                    dve.scalar_tensor_tensor(out=x1[c % 3][:, b, :], in0=ps[b // 2][:, D * (b % 2):D * (b % 2) + D],
                                             scalar=dis[:, t:t + 1], in1=xc[:, b, :], op0=ALU.mult, op1=ALU.add)\
                       .then_inc(x1_done, 1)
                if c:
                    dve.wait_ge(hscale_done, c)
                for b in range(CT):
                    dve.wait_ge(x1_done, CT * c + b + 1)
                    dve.bn_stats(bnst[:, b, :], x1[c % 3][:, b, :]).then_inc(bns2_done, 1)
                for b in range(CT):
                    dve.wait_ge(bns2_done, CT * c + b + 1)
                    dve.bn_aggr(mv[:, b, :], bnst[:, b, :]).then_inc(bn2_done, 1)

            def split_hT(c):
                for k in range(KD):
                    dve.wait_ge(ht_hi, KD * c + k + 1)
                    dve.tensor_tensor(hTl[:, k, :], ps[2 + k][:, :], hTh[:, k, :].bitcast(F32), ALU.subtract)\
                       .then_inc(ht_lo, 1)

            def row_coefs(cols, link, n, width):
                dve.tensor_tensor(zz[:, :, cols], zz[:, :, cols], ee[:, :, cols], ALU.mult).then_inc(link, 1)
                dve.wait_ge(link, n + 1)
                dve.tensor_tensor(coef[:, cols], zz[:, 0, cols], zz[:, 1, cols], ALU.add).then_inc(link, 1)
                wait_alone(dve, link, n + 2)
                dve.reciprocal(coef[:, cols], coef[:, cols]).then_inc(link, 1)
                dve.wait_ge(link, n + 3)
                dve.tensor_tensor(coef[:, cols], coef[:, cols], ee[:, 0, cols], ALU.mult).then_inc(link, 1)
                dve.wait_ge(link, n + 4)

            def chunks(fast):
                ring = RING[fast]
                split_agg(0)
                residual(0)
                split_agg(1)
                split_hT(0)
                for c in range(CHUNKS + 1):
                    diag = fast and 1 <= c <= HCH
                    k = c % HCH
                    if c + 1 < CHUNKS:
                        residual(c + 1)
                    if diag:
                        n = ring[("PT", c - 1)]
                        dve.wait_ge(ptd_hi, c)
                        dve.tensor_tensor(PTdl[:, :], ps[4 + n % 4][:, :], PTdh[:, :].bitcast(F32), ALU.subtract)\
                           .then_inc(ring_free, 1)
                    if c < CHUNKS:
                        for j, (dst, hi, key) in enumerate(((QTl, QTh, "q"), (KTl, KTh, "k"))):
                            for o in range(KD):
                                n = ring[(key, c, o)]
                                dve.wait_ge(proj_hi, 6 * c + 2 * j + o + 1)
                                dve.scalar_tensor_tensor(
                                    out=dst[:, o, CW * k:CW * k + CW], in0=ps[4 + n % 4][:, :],
                                    scalar=bcols[:, j, o:o + 1], in1=hi[:, o, CW * k:CW * k + CW].bitcast(F32),
                                    op0=ALU.add, op1=ALU.subtract).then_inc(ring_free, 1)
                                dve.wait_ge(ring_free, n + 1)
                                dve.sem_inc(proj_lo, 1)
                    if diag:
                        cols = slice(CT * (c - 1), CT * c)
                        dve.wait_ge(ee_done, c)
                        row_coefs(cols, f_link, 4 * (c - 1), CT)
                        for b in range(CT):
                            t = CT * (c - 1) + b
                            n = ring[("O", c - 1, b // 2)]
                            dve.wait_ge(ring_full, n + 1)
                            xo = x1[(c - 1) % 3][:, b, :]
                            dve.scalar_tensor_tensor(out=xo, in0=ps[4 + n % 4][:, D * (b % 2):D * (b % 2) + D],
                                                     scalar=coef[:, t:t + 1], in1=xo, op0=ALU.mult, op1=ALU.add)\
                               .then_inc(dout_done, 1)
                            if b % 2:
                                dve.wait_ge(dout_done, t + 1)
                                dve.sem_inc(ring_free, 1)
                    if c < CHUNKS:
                        for i in range(2):
                            n = ring[("v", c, i)]
                            dve.wait_ge(ring_full, n + 1)
                            dve.tensor_tensor(vf[i][:, :].rearrange("p (a d) -> p a d", a=2),
                                              ps[4 + n % 4][:, :].rearrange("p (a d) -> p a d", a=2),
                                              bvrow[:, :].rearrange("p (a d) -> p a d", a=1).to_broadcast([P, 2, D]),
                                              ALU.add)\
                               .then_inc(ring_free, 1)
                        for i in range(2):
                            dve.wait_ge(proj_hi, 6 * c + 5 + i)
                            v = slice(CT * k + 2 * i, CT * k + 2 * i + 2)
                            dve.tensor_tensor(Vl[:, v, :].rearrange("p a d -> p (a d)"), vf[i][:, :],
                                              Vh[:, v, :].rearrange("p a d -> p (a d)").bitcast(F32), ALU.subtract)\
                               .then_inc(proj_lo, 1)
                        if c + 2 < CHUNKS:
                            split_agg(c + 2)
                    if fast and c < HCH:
                        n = ring[("S", c)]
                        cols = slice(CT * c, CT * c + CT)
                        dve.wait_ge(ring_full, n + 1)
                        dve.wait_ge(adjd_loaded, 16 * CT * (c + 1))
                        if c:
                            dve.wait_ge(dexp_done, CT * c)
                        flat = Sd[:, :, :].rearrange("p b j -> p (b j)")
                        dve.tensor_tensor(flat, ps[4 + n % 4][:, :], adjd[:, :, :].rearrange("p b j -> p (b j)"),
                                          ALU.add).then_inc(d_link, 1)
                        dve.wait_ge(d_link, 2 * c + 1)
                        dve.scalar_tensor_tensor(out=flat, in0=flat, scalar=2.0,
                                                 in1=penn[:, cols, :].rearrange("p b j -> p (b j)"),
                                                 op0=ALU.mult, op1=ALU.add).then_inc(d_link, 1)
                        dve.sem_inc(ring_free, 1)
                        dve.wait_ge(d_link, 2 * c + 2)
                        dve.tensor_reduce(nmx[:, cols], Sd[:, :, :], AX_X, ALU.max, negate=True).then_inc(nmx_done, 1)
                        dve.wait_ge(nmx_done, c + 1)
                        dve.tensor_tensor(nm[:, cols], nmx[:, cols], nboff[:, cols], ALU.min).then_inc(nmm, 1)
                        dve.wait_ge(nmm, c + 1)
                        dve.tensor_tensor(dd[:, 0, cols], nm[:, cols], nmx[:, cols], ALU.subtract)
                        dve.tensor_tensor(dd[:, 1, cols], nm[:, cols], nboff[:, cols], ALU.subtract)\
                           .then_inc(dd_done, 1)
                    if c + 1 < CHUNKS:
                        split_hT(c + 1)

            def score_bank(i, par, jc):
                if jc == 0:
                    dve.wait_ge(adjr_loaded[par], i * 8 - 8 * par + 16)
                wait_alone(dve, s_full, i * 4 + jc + 1)
                dve.tensor_tensor_reduce(
                    out=SE[par][:, CW * jc:CW * jc + CW], in0=ps[jc][:, :], in1=adjr[par][:, CW * jc:CW * jc + CW],
                    scale=2.0, scalar=-3e38, op0=ALU.add, op1=ALU.max, accum_out=mx4[:, jc:jc + 1])\
                   .then_inc(s_read, 1)

            def greatest(i):
                t = bass.ds(i + HT, 1)
                dve.wait_ge(s_read, i * 4 + 4)
                dve.tensor_reduce(nmx[:, t], mx4[:, :], AX_X, ALU.max, negate=True).then_inc(m_done, 1)
                dve.wait_ge(m_done, i + 1)
                dve.tensor_tensor(nm[:, t], nmx[:, t], nboff[:, t], ALU.min).then_inc(nmt, 1)
                dve.wait_ge(nmt, i + 1)
                dve.tensor_tensor(dd[:, 0, t], nm[:, t], nmx[:, t], ALU.subtract)
                dve.tensor_tensor(dd[:, 1, t], nm[:, t], nboff[:, t], ALU.subtract).then_inc(ddt_done, 1)

            def turned(i, q):
                dve.wait_ge(pt_hi, i * 4 + q + 1)
                dve.tensor_tensor(PTl[q % 2][:, :], ps[4 + q % 2][:, :], PTh[q % 2][:, :].bitcast(F32), ALU.subtract)\
                   .then_inc(pt_lo, 1)

            def finish(i, par):
                t = bass.ds(i + HT, 1)
                dve.wait_ge(eet_done, i + 1)
                row_coefs(t, f_link, i * 4 + 4 * HCH, 1)
                dve.wait_ge(x1t_loaded[par], i * 8 - 8 * par + 16)
                dve.wait_ge(o_full, i + 1)
                if not isinstance(i, int) or i >= 2:
                    dve.wait_ge(outt_stored[par], i * 8 - 8 * par)
                dve.scalar_tensor_tensor(out=outb[par][:, :], in0=ps[6 + par][:, 0:D], scalar=coef[:, t],
                                         in1=x1t[par][:, :], op0=ALU.mult, op1=ALU.add).then_inc(o_read, 1)

            with dve.If(fast_reg == 1):
                chunks(True)

                def tile(i, par):
                    for q in range(4):
                        if not isinstance(i, int) or i + 1 < HT:
                            score_bank(i + 1, 1 - par, q)
                        turned(i, q)
                    if not isinstance(i, int) or i + 1 < HT:
                        greatest(i + 1)
                    finish(i, par)

                for q in range(4):
                    score_bank(0, 0, q)
                greatest(0)
                tile(0, 0)
                tile(1, 1)
                with dve.Fori(1, HT // 2 - 1) as v:
                    tile(v * 2, 0)
                    tile(v * 2 + 1, 1)
                tile(HT - 2, 0)
                tile(HT - 1, 1)
                dve.nop()
            with dve.Else():
                chunks(False)
                dve.sem_inc(g_end, 1)
                with dve.Fori(0, TILES) as t:
                    col = bass.ds(t, 1)
                    dve.tensor_copy(nm[:, 0:1], nboff[:, col]).then_inc(g_link, 1)
                    dve.tensor_copy(zz[:, 1, 0:1], zz[:, 1, col]).then_inc(g_link, 1)
                    dve.memset(Og[:, :], 0.0).then_inc(g_link, 1)
                    with dve.Fori(0, CHUNKS) as c:
                        n = t * CHUNKS + c
                        L = t * (3 + 8 * CHUNKS) + c * 8 + 3
                        dve.wait_ge(g_link, L)
                        dve.wait_ge(g_load, n * 128 + 128)
                        dve.wait_ge(g_score, n + 1)
                        dve.tensor_tensor(SE[0][:, 0:CW], ps[0][:, :], adjr[0][:, 0:CW], ALU.add)
                        dve.tensor_scalar(SE[1][:, CW:2 * CW], gidrow[:, bass.ds(c * CW, CW)], gidcol[:, col], -BIG,
                                          ALU.not_equal, ALU.mult).then_inc(g_link, 1)
                        dve.wait_ge(g_link, L + 1)
                        dve.scalar_tensor_tensor(out=SE[0][:, 0:CW], in0=SE[0][:, 0:CW], scalar=2.0,
                                                 in1=SE[1][:, CW:2 * CW], op0=ALU.mult, op1=ALU.add).then_inc(g_link, 1)
                        dve.wait_ge(g_link, L + 2)
                        dve.tensor_reduce(nmx[:, 0:1], SE[0][:, 0:CW], AX_X, ALU.max, negate=True).then_inc(g_link, 1)
                        dve.wait_ge(g_link, L + 3)
                        dve.tensor_tensor(nmx[:, 1:2], nmx[:, 0:1], nm[:, 0:1], ALU.min).then_inc(g_link, 1)
                        dve.wait_ge(g_link, L + 4)
                        dve.tensor_tensor(dd[:, 0, 0:1], nmx[:, 1:2], nm[:, 0:1], ALU.subtract).then_inc(g_link, 1)
                        dve.wait_ge(g_link, L + 5)
                        dve.tensor_copy(nm[:, 0:1], nmx[:, 1:2]).then_inc(g_sd, 1)
                        dve.wait_ge(g_exp, n * 2 + 2)
                        dve.scalar_tensor_tensor(out=zz[:, 1, 0:1], in0=zz[:, 1, 0:1], scalar=ee[:, 0, 0:1],
                                                 in1=zz[:, 0, 0:1], op0=ALU.mult, op1=ALU.add).then_inc(g_link, 1)
                        dve.wait_ge(g_phi, n + 1)
                        dve.tensor_tensor(PTl[0][:, :], ps[4][:, :], PTh[0][:, :].bitcast(F32), ALU.subtract)\
                           .then_inc(g_plo, 1)
                        dve.wait_ge(g_pv, n + 1)
                        dve.scalar_tensor_tensor(out=Og[:, :], in0=Og[:, :], scalar=ee[:, 0, 0:1],
                                                 in1=ps[6][:, 0:D], op0=ALU.mult, op1=ALU.add).then_inc(g_link, 1)
                        dve.wait_ge(g_link, L + 7)
                        dve.tensor_copy(coef[:, 0:1], zz[:, 1, 0:1]).then_inc(g_link, 1)
                        wait_alone(dve, g_link, L + 8)
                        with dve.If(c < CHUNKS - 1):
                            dve.sem_inc(g_end, 1)
                        with dve.Else():
                            dve.nop()
                        dve.nop()
                    dve.reciprocal(coef[:, 0:1], coef[:, 0:1]).then_inc(g_fin, 1)
                    dve.wait_ge(g_fin, t + 1)
                    dve.scalar_tensor_tensor(out=outb[0][:, :], in0=Og[:, :], scalar=coef[:, 0:1],
                                             in1=x1t[0][:, :], op0=ALU.mult, op1=ALU.add).then_inc(g_out, 1)
                    dve.wait_ge(g_out, t + 1)
                    dve.sem_inc(g_end, 1)
                dve.nop()

        @block.tensor
        def _(pe):
            pe.wait_ge(const_done, 4)
            pe.wait_ge(cmp_done, 1)
            for k in range(BANKS):
                pe.matmul(ps[k][:, :], ones33[:, :], cmp[:, CW * k:CW * k + CW], start=True, stop=True)\
                  .then_inc(gid_full, 1)
            pe.wait_ge(gid_copied, 1)
            for t in range(TILES):
                last = pe.matmul(ps[0][:, t:t + 1], cmp[:, P * t:P * t + P], ones33[:, 0:1], start=True, stop=True)
            last.then_inc(gid_full, 1)
            pe.wait_ge(gid_copied, BANKS + 1)
            pe.sem_inc(units, 4)
            pe.wait_ge(flag_ready, 1)
            fast_reg = pe.value_load(flag[0:1, 0:1], min_val=0, max_val=1)

            def group(g, par):
                pe.wait_ge(g_lo, g + 1)
                for c in range(CHUNKS):
                    s = CHUNKS * g + c
                    pe.wait_ge(split_lo, s + 1)
                    for k in range(KD):
                        pe.wait_ge(acc_done, s * 2 + k + 1)
                        for t in range(GRP):
                            last = mm3(pe, ps[(2 * c + k) % BANKS][:, :],
                                       Ghi[par][:, t, P * k:P * k + P], Glo[par][:, t, P * k:P * k + P],
                                       ahi[c % 2][:, t, :], alo[c % 2][:, t, :], t == 0, t == GRP - 1)
                        last.then_inc(units, 1)

            with pe.Fori(0, 4) as u:
                group(u * 2, 0)
                group(u * 2 + 1, 1)

            pe.wait_ge(acc_done, BANKS + 2 * STEPS)
            pe.wait_ge(w_done, 5)

            def residual(c):
                pe.wait_ge(a_lo, c + 1)
                for b in range(CT):
                    if c:
                        pe.wait_ge(x1_done, CT * (c - 1) + b + 2 - b % 2)
                    for k in range(KD):
                        last = mm3(pe, ps[b // 2][:, D * (b % 2):D * (b % 2) + D],
                                   Ahi[:, k, P * b:P * b + P], Alo[:, k, P * b:P * b + P],
                                   Whi[:, 0, k, :], Wlo[:, 0, k, :], k == 0, k == KD - 1)
                    last.then_inc(z_full, 1)

            def turn(c):
                pe.wait_ge(h_done, CT * (c + 1))
                if c:
                    pe.wait_ge(ht_lo, KD * c)
                for k in range(KD):
                    for b in range(CT):
                        last = pe.transpose(ps[2 + k][:, P * b:P * b + P], hn[:, b, P * k:P * k + P], ident[:, :])
                    last.then_inc(tr_full, 1)

            def chunks(fast):
                ring = RING[fast]

                def bank(key):
                    n = ring[key]
                    if n >= 4:
                        pe.wait_ge(ring_free, n - 3)
                    return ps[4 + n % 4]

                residual(0)
                turn(0)
                for c in range(CHUNKS + 1):
                    diag = fast and 1 <= c <= HCH
                    k = c % HCH
                    if c + 1 < CHUNKS:
                        residual(c + 1)
                    if diag:
                        pe.wait_ge(dexp_done, CT * c)
                        o = bank(("PT", c - 1))
                        for b in range(CT):
                            last = pe.transpose(o[:, P * b:P * b + P], Ed[:, b, :], ident[:, :])
                        last.then_inc(ring_full, 1)
                    if c < CHUNKS:
                        pe.wait_ge(ht_lo, KD * (c + 1))
                        for j, key in ((1, "q"), (2, "k")):
                            for oh in range(KD):
                                o = bank((key, c, oh))
                                for kk in range(KD):
                                    w = slice(P * oh, P * oh + P)
                                    last = mm3(pe, o[:, :], Whi[:, j, kk, w], Wlo[:, j, kk, w],
                                               hTh[:, kk, :], hTl[:, kk, :], kk == 0, kk == KD - 1)
                                last.then_inc(ring_full, 1)
                    if diag:
                        pe.wait_ge(ring_free, ring[("PT", c - 1)] + 1)
                        kd = (c - 1) % HCH
                        pe.wait_ge(proj_lo, 6 * c)
                        for b in range(CT):
                            if b % 2 == 0:
                                o = bank(("O", c - 1, b // 2))
                            last = mm3(pe, o[:, D * (b % 2):D * (b % 2) + D],
                                       PTdh[:, P * b:P * b + P], PTdl[:, P * b:P * b + P],
                                       Vh[:, CT * kd + b, :], Vl[:, CT * kd + b, :], True, True)
                            if b % 2:
                                last.then_inc(ring_full, 1)
                    if c < CHUNKS:
                        for i in range(2):
                            o = bank(("v", c, i))
                            for b in (2 * i, 2 * i + 1):
                                for kk in range(KD):
                                    last = mm3(pe, o[:, D * (b % 2):D * (b % 2) + D],
                                               hTh[:, kk, P * b:P * b + P], hTl[:, kk, P * b:P * b + P],
                                               Whi[:, 3, kk, :], Wlo[:, 3, kk, :], kk == 0, kk == KD - 1)
                            last.then_inc(ring_full, 1)
                    if fast and c < HCH:
                        pe.wait_ge(proj_lo, 6 * c + 4)
                        o = bank(("S", c))
                        for b in range(CT):
                            w = slice(CW * k + P * b, CW * k + P * b + P)
                            for oh in range(KD):
                                last = mm3(pe, o[:, P * b:P * b + P], QTh[:, oh, w], QTl[:, oh, w],
                                           KTh[:, oh, w], KTl[:, oh, w], oh == 0, oh == KD - 1)
                        last.then_inc(ring_full, 1)
                    if c + 1 < CHUNKS:
                        turn(c + 1)
                pe.wait_ge(ring_free, len(ring))
                pe.wait_ge(proj_lo, 6 * CHUNKS)

            def score_bank(i, jc):
                if i:
                    pe.wait_ge(s_read, 4 * (i - 1) + jc + 1)
                for oh in range(KD):
                    w, j = slice(P * i, P * i + P), slice(CW * jc, CW * jc + CW)
                    last = mm3(pe, ps[jc][:, :], QTh[:, oh, w], QTl[:, oh, w], KTh[:, oh, j], KTl[:, oh, j],
                               oh == 0, oh == KD - 1)
                last.then_inc(s_full, 1)

            def turn_quarter(i, q):
                if q == 0:
                    pe.wait_ge(e_done, i + 1)
                if 4 * i + q >= 2:
                    pe.wait_ge(pt_lo, 4 * i + q - 1)
                for b in range(4):
                    j = CW * q + P * b
                    last = pe.transpose(ps[4 + q % 2][:, P * b:P * b + P], SE[i % 2][:, j:j + P], ident[:, :])
                last.then_inc(pt_full, 1)

            def weigh_quarter(i, q):
                pe.wait_ge(pt_lo, 4 * i + q + 1)
                if q == 0 and i >= 2:
                    pe.wait_ge(o_read, i - 1)
                for b in range(4):
                    last = mm3(pe, ps[6 + i % 2][:, 0:D], PTh[q % 2][:, P * b:P * b + P], PTl[q % 2][:, P * b:P * b + P],
                               Vh[:, 4 * q + b, :], Vl[:, 4 * q + b, :], q == 0 and b == 0, q == 3 and b == 3)
                if q == 3:
                    last.then_inc(o_full, 1)

            with pe.If(fast_reg == 1):
                chunks(True)
                for jc in range(4):
                    score_bank(0, jc)
                for i in range(HT):
                    for q in range(4):
                        if i + 1 < HT:
                            score_bank(i + 1, q)
                        turn_quarter(i, q)
                        if q:
                            weigh_quarter(i, q - 1)
                    weigh_quarter(i, 3)
            with pe.Else():
                chunks(False)
                with pe.Fori(0, TILES) as t:
                    with pe.Fori(0, CHUNKS) as c:
                        n = t * CHUNKS + c
                        pe.wait_ge(g_load, n * 128 + 128)
                        for oh in range(KD):
                            last = mm3(pe, ps[0][:, :], QTh[:, oh, 0:P], QTl[:, oh, 0:P], KTh[:, oh, 0:CW],
                                       KTl[:, oh, 0:CW], oh == 0, oh == KD - 1)
                        last.then_inc(g_score, 1)
                        pe.wait_ge(g_exp, n * 2 + 2)
                        for b in range(4):
                            last = pe.transpose(ps[4][:, P * b:P * b + P], SE[1][:, P * b:P * b + P], ident[:, :])
                        last.then_inc(g_tr, 1)
                        pe.wait_ge(g_plo, n + 1)
                        for b in range(4):
                            last = mm3(pe, ps[6][:, 0:D], PTh[0][:, P * b:P * b + P], PTl[0][:, P * b:P * b + P],
                                       Vh[:, b, :], Vl[:, b, :], b == 0, b == 3)
                        last.then_inc(g_pv, 1)
                pe.nop()


def kernel(x, adj, L0_gnn_W, L0_gnn_b, L1_gnn_ptr, L1_gnn_Wq, L1_gnn_bq, L1_gnn_Wk, L1_gnn_bk, L1_gnn_Wv, L1_gnn_bv):
    import numpy as _np
    import concourse.bacc as _bacc
    from concourse import mybir as _mybir
    from concourse.bass_utils import run_bass_kernel_spmd as _run

    a = _np.asarray(adj)
    blocks = a.reshape(CHUNKS, CW, GROUPS, GRP, P).transpose(2, 0, 4, 3, 1).reshape(STEPS * P, GRP * CW)
    ins = {
        "x": x, "adj": a, "adjT": blocks, "W0T": _np.asarray(L0_gnn_W).T, "b0": L0_gnn_b,
        "ptr": _np.asarray(L1_gnn_ptr).reshape(NPTR, 1), "WqT": _np.asarray(L1_gnn_Wq).T, "bq": _np.asarray(L1_gnn_bq).reshape(KD, P).T,
        "WkT": _np.asarray(L1_gnn_Wk).T, "bk": _np.asarray(L1_gnn_bk).reshape(KD, P).T, "WvT": _np.asarray(L1_gnn_Wv).T, "bv": L1_gnn_bv,
    }
    nc = _bacc.Bacc("TRN2", target_bir_lowering=False, num_devices=1)
    arrays, args = {}, {}
    for name, value in ins.items():
        value = _np.ascontiguousarray(value)
        arrays[f"in_{name}_dram"] = value
        args[name] = nc.dram_tensor(f"in_{name}_dram", value.shape, _mybir.dt.from_np(value.dtype),
                                    kind="ExternalInput").ap()
    out = nc.dram_tensor("out_0_dram", (N, D), _mybir.dt.float32, kind="ExternalOutput").ap()
    gnn_kernel(nc, out=out, **args)
    r = _run(nc, [arrays], core_ids=[0])
    return r.results[0]["out_0_dram"]
```

```python
from contextlib import ExitStack

import concourse.bass as bass
from concourse import mybir

F32 = mybir.dt.float32
F32R = mybir.dt.float32r
BF16 = mybir.dt.bfloat16
I32 = mybir.dt.int32
U8 = mybir.dt.uint8
ALU = mybir.AluOpType
ACT = mybir.ActivationFunctionType
AX_X = mybir.AxisListType.X

P = 128
N = 4096
D = 256
KD = D // P
TILES = N // P
GRP = 4
GROUPS = TILES // GRP
CW = 512
CHUNKS = N // CW
STEPS = GROUPS * CHUNKS
CT = CW // P
HALF = N // 2
HCH = CHUNKS // 2
HT = TILES // 2
BANKS = 8
UB = 4
NPTR = 33
BIG = 2.0 ** 100
OFF = 2e6
EPS_DEG = 1e-8
EPS_LN = 1e-5


def gnn_kernel(nc, x, adj, adjT, W0T, b0, ptr, Wq, bq, Wk, bk, WvT, bv, out):
    with ExitStack() as ctx:
        cursor = [nc.sbuf_base + (-nc.sbuf_base) % 32]

        def at(name, shape, dt, offset=None):
            size = {F32: 4, F32R: 4, I32: 4, BF16: 2, U8: 1}[dt]
            for n in shape[1:]:
                size *= n
            size += -size % 32
            if offset is None:
                offset = cursor[0]
                cursor[0] += size
            assert offset + size <= nc.sbuf_usable_end, (name, offset + size, nc.sbuf_usable_end)
            return nc.alloc_sbuf_tensor_at(name, shape, dt, offset=offset), offset

        def sb(name, shape, dt, offset=None):
            return at(name, shape, dt, offset)[0]

        def sem(name):
            return ctx.enter_context(nc.semaphore(name))

        penn = sb("penn", [P, HT, P], BF16)
        gidrow = sb("gidrow", [P, N], U8)
        gidcol = sb("gidcol", [P, TILES], F32)
        deg = sb("deg", [P, TILES], F32)
        dis = sb("dis", [P, TILES], F32)
        mn = sb("mn", [P, TILES], F32)
        nboff = sb("nboff", [P, TILES], F32)
        zz = sb("zz", [P, 2, TILES], F32)
        nmx = sb("nmx", [P, TILES], F32)
        rr = sb("rr", [P, TILES], F32)
        nmr = sb("nmr", [P, TILES], F32)
        nm = sb("nm", [P, TILES], F32)
        dd = sb("dd", [P, 2, TILES], F32)
        ee = sb("ee", [P, 2, TILES], F32)
        coef = sb("coef", [P, TILES], F32)
        ident = sb("ident", [P, P], F32)
        bcols = sb("bcols", [P, 2, KD], F32)
        bqwide = sb("bqwide", [P, KD, P], F32)
        bqk = sb("bqk", [P, KD], F32)
        uf = sb("uf", [P, KD], F32)
        ur = sb("ur", [P, KD, 2], F32R)
        c0 = sb("c0", [P, 1], F32)
        ones1 = sb("ones1", [1, P], F32R)
        b0row = sb("b0row", [P, D], F32)
        bvr = sb("bvr", [1, 2, D], F32R)
        ptri = sb("ptri", [NPTR, 1], I32)
        ptrf = sb("ptrf", [NPTR, 1], F32)
        flagw = sb("flagw", [1, 32], F32)
        flag = sb("flag", [1, 1], I32)
        mhalf = sb("mhalf", [P, GRP], F32)
        epsdeg = sb("epsdeg", [P, GRP], F32)
        bnst = sb("bnst", [P, GRP, 6], F32)
        mv = sb("mv", [P, GRP, 2], F32)
        pw = sb("pw", [P, 4, GRP], F32)
        hs = [sb(f"hs{i}", [P, 2, GRP], F32) for i in range(2)]
        mx4 = sb("mx4", [P, CT], F32)
        mx4t = sb("mx4t", [P, CT], F32)

        regK = cursor[0]
        QTh = sb("QTh", [P, KD, HALF], F32R)
        QTl = sb("QTl", [P, KD, HALF], F32R)
        KTh = sb("KTh", [P, KD, HALF], F32R)
        KTl = sb("KTl", [P, KD, HALF], F32R)
        Vh = sb("Vh", [P, HT, D], F32R)
        Vl = sb("Vl", [P, HT, D], F32R)
        endK = cursor[0]
        cursor[0] = regK
        raw = [sb(f"raw{i}", [P, GRP, CW], F32) for i in range(4)]
        regS = cursor[0]
        ahi = [sb(f"ahi{i}", [P, GRP, CW], F32R) for i in range(2)]
        alo = [sb(f"alo{i}", [P, GRP, CW], F32R) for i in range(2)]
        Ghi = [sb(f"Ghi{i}", [P, GRP, D], F32R) for i in range(2)]
        Glo = [sb(f"Glo{i}", [P, GRP, D], F32R) for i in range(2)]
        gf = sb("gf", [P, GRP, D], F32)
        xg = [sb(f"xg{i}", [P, GRP, D], F32) for i in range(2)]
        masktmp = sb("masktmp", [P, 1024], BF16)
        bvrow = sb("bvrow", [1, D], F32)
        ones33 = sb("ones33", [NPTR, P], BF16)
        assert cursor[0] <= endK
        iota = sb("iota", [NPTR, N], I32, regS)
        cmp = sb("cmp", [NPTR, N], BF16, regS + 4 * N)
        cursor[0] = endK

        regA = cursor[0]
        aggT = sb("aggT", [P, KD, N], F32)
        adjr = [sb(f"adjr{i}", [P, HALF], F32, regA + 4 * HALF * i) for i in range(2)]
        SE = [sb(f"SE{i}", [P, HALF], F32, regA + 4 * HALF * (2 + i)) for i in range(2)]

        regR = cursor[0]
        row = [sb(f"row{i}", [P, N], F32) for i in range(4)]
        endR = cursor[0]
        cursor[0] = regR
        Whi = sb("Whi", [P, 4, KD, D], F32R)
        Wlo = sb("Wlo", [P, 4, KD, D], F32R)
        Mhi = sb("Mhi", [P, KD, D], F32R)
        Mlo = sb("Mlo", [P, KD, D], F32R)
        regPT = cursor[0]
        Ahi = sb("Ahi", [P, KD, CW], F32R)
        Alo = sb("Alo", [P, KD, CW], F32R)
        regH = cursor[0]
        hn = sb("hn", [P, CT, D], F32)
        xc = sb("xc", [P, CT, D], F32)
        regX = cursor[0]
        x1 = [sb(f"x1_{i}", [P, CT, D], F32) for i in range(3)]
        Wraw = sb("Wraw", [P, 4, KD, D], F32, regX)
        adjd = sb("adjd", [P, CT, P], F32)
        Sd = sb("Sd", [P, CT, P], F32)
        Ed = sb("Ed", [P, CT, P], F32)
        PTdh = sb("PTdh", [P, CW], F32R)
        PTdl = sb("PTdl", [P, CW], F32R)
        cursor[0] = max(cursor[0], endR)
        PTh = [sb(f"PTh{i}", [P, CW], F32R, regPT + 4 * CW * i) for i in range(2)]
        PTl = [sb(f"PTl{i}", [P, CW], F32R, regPT + 4 * CW * (2 + i)) for i in range(2)]
        x1t = [sb(f"x1t{i}", [P, D], F32, regH + 4 * D * i) for i in range(2)]
        outb = [sb(f"outb{i}", [P, D], F32, regH + 4 * D * (2 + i)) for i in range(2)]
        Og = sb("Og", [P, D], F32, regX)

        ps = [ctx.enter_context(nc.psum_tensor(f"ps{i}", [P, CW], F32)) for i in range(BANKS)]

        x1_d = nc.dram_tensor("x1_scratch", (N, D), F32, kind="Internal").ap()
        qh_d = nc.dram_tensor("qh_scratch", (P, KD, N), F32, kind="Internal").ap()
        ql_d = nc.dram_tensor("ql_scratch", (P, KD, N), F32, kind="Internal").ap()
        kh_d = nc.dram_tensor("kh_scratch", (P, KD, N), F32, kind="Internal").ap()
        kl_d = nc.dram_tensor("kl_scratch", (P, KD, N), F32, kind="Internal").ap()
        vh_d = nc.dram_tensor("vh_scratch", (P, TILES, D), F32, kind="Internal").ap()
        vl_d = nc.dram_tensor("vl_scratch", (P, TILES, D), F32, kind="Internal").ap()

        ptr_loaded = sem("ptr_loaded")
        bias_loaded = sem("bias_loaded")
        row_first = [sem(f"row_first{i}") for i in range(4)]
        row_loaded = [sem(f"row_loaded{i}") for i in range(4)]
        raw_loaded = [sem(f"raw_loaded{i}") for i in range(4)]
        xg_loaded = [sem(f"xg_loaded{i}") for i in range(2)]
        iota_done = sem("iota_done")
        const_done = sem("const_done")
        agg_zero = sem("agg_zero")
        cmp_done = sem("cmp_done")
        gid_full = sem("gid_full")
        gid_copied = sem("gid_copied")
        setup_link = sem("setup_link")
        flag_ready = sem("flag_ready")
        rowsum_done = sem("rowsum_done")
        mask_link = sem("mask_link")
        masked = sem("masked")
        mn_done = sem("mn_done")
        nb_done = sem("nb_done")
        exp_done = sem("exp_done")
        bns_done = sem("bns_done")
        bn_done = sem("bn_done")
        pool_link = sem("pool_link")
        gscale_done = sem("gscale_done")
        gf_done = sem("gf_done")
        g_hi = sem("g_hi")
        g_lo = sem("g_lo")
        split_hi = sem("split_hi")
        split_lo = sem("split_lo")
        units = sem("units")
        acc_done = sem("acc_done")

        w_loaded = sem("w_loaded")
        w_hi = sem("w_hi")
        w_done = sem("w_done")
        m_full = sem("m_full")
        m_hi = sem("m_hi")
        m_lo = sem("m_lo")
        v_link = sem("v_link")
        vec_done = sem("vec_done")
        x_loaded = sem("x_loaded")
        xb_done = sem("xb_done")
        a_hi = sem("a_hi")
        a_lo = sem("a_lo")
        z_full = sem("z_full")
        x1_done = sem("x1_done")
        x1_stored = [sem(f"x1_stored{i}") for i in range(3)]
        bns2_done = sem("bns2_done")
        bn2_done = sem("bn2_done")
        hscale_done = sem("hscale_done")
        h_done = sem("h_done")
        tr_full = sem("tr_full")
        ht_hi = sem("ht_hi")
        ht_lo = sem("ht_lo")
        ring_full = sem("ring_full")
        ring_free = sem("ring_free")
        r_link = sem("r_link")
        proj_hi = sem("proj_hi")
        adjd_loaded = sem("adjd_loaded")
        adjp_done = sem("adjp_done")
        nmx_done = sem("nmx_done")
        nm_link = sem("nm_link")
        nm_done = sem("nm_done")
        dd_done = sem("dd_done")
        dexp_done = sem("dexp_done")
        ee_done = sem("ee_done")
        ptd_hi = sem("ptd_hi")
        ptd_lo = sem("ptd_lo")
        z_done = sem("z_done")
        coef_link = sem("coef_link")
        coef_done = sem("coef_done")
        out_stored = sem("out_stored")
        spilled = sem("spilled")

        adjr_loaded = [sem(f"adjr_loaded{i}") for i in range(2)]
        x1t_loaded = [sem(f"x1t_loaded{i}") for i in range(2)]
        s_full = sem("s_full")
        s_read = sem("s_read")
        m_done = sem("m_done")
        nmt_link = sem("nmt_link")
        nmt_done = sem("nmt_done")
        ddt_done = sem("ddt_done")
        e_done = sem("e_done")
        eet_done = sem("eet_done")
        pt_full = sem("pt_full")
        pt_hi = sem("pt_hi")
        pt_lo = sem("pt_lo")
        o_full = sem("o_full")
        z_link = sem("z_link")
        zt_link = sem("zt_link")
        zt_done = sem("zt_done")
        coeft_link = sem("coeft_link")
        coeft_done = sem("coeft_done")
        o_read = sem("o_read")
        outt_stored = [sem(f"outt_stored{i}") for i in range(2)]

        g_load = sem("g_load")
        g_score = sem("g_score")
        g_link = sem("g_link")
        g_rlink = sem("g_rlink")
        g_sd = sem("g_sd")
        g_exp = sem("g_exp")
        g_tr = sem("g_tr")
        g_phi = sem("g_phi")
        g_plo = sem("g_plo")
        g_pv = sem("g_pv")
        g_end = sem("g_end")
        g_out = sem("g_out")
        g_fin = sem("g_fin")

        def rows_of(t, n=1):
            return bass.ds(t * P, n * P)

        def tiles_of(a, t):
            return a[bass.ds(t * P, GRP * P), :].rearrange("(b p) d -> p b d", p=P)

        def ring_plan(fast):
            order = []
            for c in range(CHUNKS + 1):
                diag = fast and 1 <= c <= HCH
                if diag:
                    order.append(("PT", c - 1))
                if c < CHUNKS:
                    order += [("q", c, 0), ("q", c, 1), ("r", c)]
                if diag:
                    order += [("O", c - 1, 0), ("O", c - 1, 1)]
                if c < CHUNKS:
                    order += [("v", c, 0), ("v", c, 1)]
                if fast and c < HCH:
                    order.append(("S", c))
            return {k: i for i, k in enumerate(order)}

        RING = {True: ring_plan(True), False: ring_plan(False)}

        def mm3(e, o, lh, ll, rh, rl, first, last):
            e.matmul(o, lh, rh, start=first, stop=False)
            e.matmul(o, lh, rl, start=False, stop=False)
            return e.matmul(o, ll, rh, start=False, stop=last)

        unread = {e.engine: sem(f"unread_{k}") for k, e in enumerate((nc.sync, nc.vector, nc.gpsimd))}

        def wait_alone(e, semaphore, value):
            e.wait_ge(semaphore, value)
            e.sem_inc(unread[e.engine], 1)

        block = ctx.enter_context(nc.Block())

        @block.sync
        def _(sp):
            sp.dma_start(ptri[:, :], ptr).then_inc(ptr_loaded, 16)
            for t in range(4):
                sp.dma_start(row[t][:, :], adj[rows_of(t), :]).then_inc(row_first[t], 16)
                if t == 0:
                    sp.dma_start(xg[0][:, :, :], tiles_of(x, 0)).then_inc(xg_loaded[0], 16)
            for s in range(4):
                sp.dma_start(raw[s][:, :, :], adjT[rows_of(s), :].rearrange("p (t i) -> p t i", t=GRP))\
                  .then_inc(raw_loaded[s], 16)
            sp.dma_start(xg[1][:, :, :], tiles_of(x, GRP)).then_inc(xg_loaded[1], 16)
            sp.dma_start(bcols[:, 0, :], bq).then_inc(bias_loaded, 16)
            sp.dma_start(bcols[:, 1, :], bk).then_inc(bias_loaded, 16)
            sp.dma_start(b0row[:, :], b0.rearrange("(a d) -> a d", a=1).partition_broadcast(P))\
              .then_inc(bias_loaded, 16)
            sp.dma_start(bvrow[:, :], bv.rearrange("(a d) -> a d", a=1))\
              .then_inc(bias_loaded, 16)

            def group(g, par):
                if not isinstance(g, int) or g + 2 < GROUPS:
                    wait_alone(sp, gf_done, GRP * g + GRP)
                    sp.dma_start(xg[par][:, :, :], tiles_of(x, GRP * g + 2 * GRP)).then_inc(xg_loaded[par], 16)
                for c in range(CHUNKS):
                    s = CHUNKS * g + c
                    if not isinstance(g, int) or s + 4 < STEPS:
                        wait_alone(sp, split_lo, s + 1)
                        sp.dma_start(raw[c % 4][:, :, :],
                                     adjT[bass.ds(s * P + 4 * P, P), :].rearrange("p (t i) -> p t i", t=GRP))\
                          .then_inc(raw_loaded[c % 4], 16)
                    if isinstance(g, int) and g == GROUPS - 1 and c == 0:
                        sp.wait_ge(exp_done, TILES)
                        for i, w in enumerate((W0T, Wq, Wk, WvT)):
                            sp.dma_start(Wraw[:, i, :, :], w.rearrange("(k p) o -> p k o", p=P)).then_inc(w_loaded, 16)
                        sp.dma_start(xc[:, :, :], tiles_of(x, 0)).then_inc(x_loaded, 16)

            with sp.Fori(0, 3) as u:
                group(u * 2, 0)
                group(u * 2 + 1, 1)
            group(6, 0)
            group(7, 1)

            sp.wait_ge(flag_ready, 1)
            fast_reg = sp.value_load(flag[0:1, 0:1], min_val=0, max_val=1)

            def load_adjd(c):
                for b in range(CT):
                    t = CT * c + b
                    sp.dma_start(adjd[:, b, :], adj[t * P:t * P + P, t * P:t * P + P]).then_inc(adjd_loaded, 16)

            def chunks(fast):
                ring = RING[fast]
                if fast:
                    load_adjd(0)
                for c in range(-1, CHUNKS + 1):
                    if c + 1 < CHUNKS:
                        sp.wait_ge(x1_done, CT * (c + 2))
                        if c + 2 < CHUNKS:
                            sp.dma_start(xc[:, :, :], tiles_of(x, CT * (c + 2))).then_inc(x_loaded, 16)
                        if not fast or c + 1 >= HCH:
                            sp.dma_start(tiles_of(x1_d, CT * (c + 1)), x1[(c + 1) % 3][:, :, :])\
                              .then_inc(x1_stored[(c + 1) % 3], 16)
                    if fast and 1 <= c <= HCH:
                        sp.wait_ge(ring_free, ring[("O", c - 1, 1)] + 1)
                        sp.dma_start(tiles_of(out, CT * (c - 1)), x1[(c - 1) % 3][:, :, :])\
                          .then_inc(x1_stored[(c - 1) % 3], 16)
                    if fast and 0 <= c < HCH - 1:
                        sp.wait_ge(ring_free, ring[("S", c)] + 1)
                        load_adjd(c + 1)
                    if not fast and 0 <= c < CHUNKS:
                        sp.wait_ge(ring_free, ring[("v", c, 1)] + 1)
                        k = c % HCH
                        for d_, s_ in ((qh_d, QTh), (ql_d, QTl), (kh_d, KTh), (kl_d, KTl)):
                            sp.dma_start(d_[:, :, CW * c:CW * c + CW], s_[:, :, CW * k:CW * k + CW].bitcast(F32))\
                              .then_inc(spilled, 16)
                        for d_, s_ in ((vh_d, Vh), (vl_d, Vl)):
                            sp.dma_start(d_[:, CT * c:CT * c + CT, :], s_[:, CT * k:CT * k + CT, :].bitcast(F32))\
                              .then_inc(spilled, 16)
                for i in range(3):
                    sp.wait_ge(x1_stored[i], 16 * len(range(i, CHUNKS, 3)))

            def rows_for(i, par):
                sp.dma_start(adjr[par][:, :], adj[bass.ds(i * P + HALF, P), HALF:N]).then_inc(adjr_loaded[par], 16)
                sp.dma_start(x1t[par][:, :], x1_d[bass.ds(i * P + HALF, P), :]).then_inc(x1t_loaded[par], 16)

            def store_rows(i, par):
                wait_alone(sp, o_read, i + 1)
                sp.dma_start(out[bass.ds(i * P + HALF, P), :], outb[par][:, :]).then_inc(outt_stored[par], 16)

            with sp.If(fast_reg == 1):
                chunks(True)
                sp.wait_ge(a_lo, CHUNKS)
                sp.wait_ge(ring_full, RING[True][("v", CHUNKS - 1, 1)] + 1)
                rows_for(0, 0)
                rows_for(1, 1)
                with sp.Fori(0, HT // 2 - 1) as v:
                    for par in range(2):
                        i = v * 2 + par
                        wait_alone(sp, s_read, i * CT + CT)
                        sp.dma_start(adjr[par][:, :], adj[bass.ds(i * P + 2 * P + HALF, P), HALF:N])\
                          .then_inc(adjr_loaded[par], 16)
                        store_rows(i, par)
                        sp.dma_start(x1t[par][:, :], x1_d[bass.ds(i * P + 2 * P + HALF, P), :])\
                          .then_inc(x1t_loaded[par], 16)
                store_rows(HT - 2, 0)
                store_rows(HT - 1, 1)
                sp.wait_ge(outt_stored[0], 16 * HT // 2)
                sp.wait_ge(outt_stored[1], 16 * HT // 2)
            with sp.Else():
                chunks(False)
                sp.wait_ge(spilled, 16 * 6 * CHUNKS)
                with sp.Fori(0, TILES) as t:
                    with sp.Fori(0, CHUNKS) as c:
                        wait_alone(sp, g_end, t * CHUNKS + c + 1)
                        for d_, s_ in ((qh_d, QTh), (ql_d, QTl)):
                            sp.dma_start(s_[:, :, 0:P].bitcast(F32), d_[:, :, rows_of(t)]).then_inc(g_load, 16)
                        for d_, s_ in ((kh_d, KTh), (kl_d, KTl)):
                            sp.dma_start(s_[:, :, 0:CW].bitcast(F32), d_[:, :, bass.ds(c * CW, CW)]).then_inc(g_load, 16)
                        for d_, s_ in ((vh_d, Vh), (vl_d, Vl)):
                            sp.dma_start(s_[:, 0:CT, :].bitcast(F32), d_[:, bass.ds(c * CT, CT), :]).then_inc(g_load, 16)
                        sp.dma_start(adjr[0][:, 0:CW], adj[rows_of(t), bass.ds(c * CW, CW)]).then_inc(g_load, 16)
                        sp.dma_start(x1t[0][:, :], x1_d[rows_of(t), :]).then_inc(g_load, 16)
                    wait_alone(sp, g_out, t + 1)
                    sp.dma_start(out[rows_of(t), :], outb[0][:, :]).then_inc(outt_stored[0], 16)
                    wait_alone(sp, outt_stored[0], t * 16 + 16)
                sp.nop()

        @block.gpsimd
        def _(pool):
            pool.iota(iota[:, :], pattern=[[1, N]], base=0, channel_multiplier=0).then_inc(iota_done, 1)
            pool.memset(ident[:, :], 0.0).then_inc(pool_link, 1)
            pool.memset(mhalf[:, :], -0.5).then_inc(const_done, 1)
            pool.memset(epsdeg[:, :], EPS_DEG).then_inc(const_done, 1)
            pool.memset(ones33[:, :], 1.0).then_inc(const_done, 1)
            pool.wait_ge(pool_link, 1)
            pool.affine_select(out=ident[:, :], in_=ident[:, :], compare_op=ALU.not_equal, fill=1.0, base=0,
                               pattern=[[-1, P]], channel_multiplier=1).then_inc(const_done, 1)
            pool.memset(aggT[:, :, :], 0.0).then_inc(agg_zero, 1)
            LINKS = 3

            def scales(gs, par):
                n = gs * LINKS + 1
                r = gs * GRP
                pool.wait_ge(rowsum_done, r + GRP)
                pool.wait_ge(bn_done, r + GRP)
                pool.wait_ge(const_done, 4)
                pool.tensor_tensor(pw[:, 0, :], deg[:, bass.ds(r, GRP)], epsdeg[:, :], ALU.add)
                pool.tensor_scalar(pw[:, 1, :], mv[:, :, 1], EPS_LN, None, ALU.add).then_inc(pool_link, 1)
                wait_alone(pool, pool_link, n + 1)
                pool.tensor_tensor(dis[:, bass.ds(r, GRP)], pw[:, 0, :], mhalf[:, :], ALU.pow)
                pool.tensor_tensor(pw[:, 2, :], pw[:, 1, :], mhalf[:, :], ALU.pow)
                pool.tensor_scalar(pw[:, 3, :], mv[:, :, 0], -1.0, None, ALU.mult).then_inc(pool_link, 1)
                wait_alone(pool, pool_link, n + 2)
                pool.tensor_tensor(hs[par][:, 0, :], pw[:, 2, :], dis[:, bass.ds(r, GRP)], ALU.mult)\
                    .then_inc(pool_link, 1)
                pool.wait_ge(pool_link, n + 3)
                pool.tensor_tensor(hs[par][:, 1, :], hs[par][:, 0, :], pw[:, 3, :], ALU.mult)\
                    .then_inc(gscale_done, 1)

            def next_row(r, slot):
                pool.wait_ge(exp_done, r + 1)
                pool.dma_start(row[slot][:, :], adj[bass.ds(r * P + 4 * P, P), :]).then_inc(row_loaded[slot], 16)

            next_row(0, 0)
            scales(0, 0)
            for r in range(1, 4):
                next_row(r, r)

            def group(g, par):
                for c in range(1, CHUNKS, 2):
                    r = GRP * g + 4 + c // 2
                    if not isinstance(g, int) or r + 4 < TILES:
                        next_row(r, c // 2)
                    if c == 3 and (not isinstance(g, int) or g + 1 < GROUPS):
                        scales(g + 1, 1 - par)

            with pool.Fori(0, 3) as u:
                group(u * 2, 0)
                group(u * 2 + 1, 1)
            group(6, 0)
            pool.wait_ge(flag_ready, 1)
            fast_reg = pool.value_load(flag[0:1, 0:1], min_val=0, max_val=1)

            def shares(cols, greatest, g_n, link, l_n, done, exps, e_n, zdone):
                wait_alone(pool, greatest, g_n)
                pool.tensor_tensor(dd[:, 0, cols], nm[:, cols], nmr[:, cols], ALU.subtract)
                pool.tensor_tensor(dd[:, 1, cols], nm[:, cols], nboff[:, cols], ALU.subtract).then_inc(done, 1)
                wait_alone(pool, exps, e_n)
                pool.tensor_tensor(zz[:, 0, cols], zz[:, 0, cols], ee[:, 0, cols], ALU.mult)
                pool.tensor_tensor(zz[:, 1, cols], zz[:, 1, cols], ee[:, 1, cols], ALU.mult).then_inc(link, 1)
                wait_alone(pool, link, l_n + 1)
                pool.tensor_tensor(coef[:, cols], zz[:, 0, cols], zz[:, 1, cols], ALU.add).then_inc(zdone, 1)

            def hidden_scales(c):
                n = GROUPS * LINKS + 1 + 2 * c
                pool.wait_ge(bn2_done, CT * (c + 1))
                pool.tensor_scalar(pw[:, 1, :], mv[:, :, 1], EPS_LN, None, ALU.add)
                pool.tensor_scalar(pw[:, 3, :], mv[:, :, 0], -1.0, None, ALU.mult).then_inc(pool_link, 1)
                pool.wait_ge(pool_link, n + 1)
                if c >= 2:
                    pool.wait_ge(h_done, CT * (c - 1))
                pool.tensor_tensor(hs[c % 2][:, 0, :], pw[:, 1, :], mhalf[:, :], ALU.pow).then_inc(pool_link, 1)
                pool.wait_ge(pool_link, n + 2)
                pool.tensor_tensor(hs[c % 2][:, 1, :], hs[c % 2][:, 0, :], pw[:, 3, :], ALU.mult)\
                    .then_inc(hscale_done, 1)
                pool.wait_ge(hscale_done, c + 1)

            def with_b0(c):
                pool.wait_ge(x_loaded, 16 * (c + 1))
                b0wide = b0row[:, :].rearrange("p (a d) -> p a d", a=1).to_broadcast([P, CT, D])
                pool.tensor_tensor(xc[:, :, :], xc[:, :, :], b0wide, ALU.add).then_inc(xb_done, 1)

            def chunks(fast):
                with_b0(0)
                hidden_scales(0)
                for c in range(-1, CHUNKS):
                    if c >= 0 and c + 1 < CHUNKS:
                        hidden_scales(c + 1)
                    if c + 2 < CHUNKS:
                        with_b0(c + 2) if c >= 0 else with_b0(1)
                    if fast and 0 <= c < HCH:
                        pool.wait_ge(adjd_loaded, 16 * CT * (c + 1))
                        pool.tensor_tensor(adjd[:, :, :], adjd[:, :, :], penn[:, CT * c:CT * c + CT, :], ALU.add)\
                            .then_inc(adjp_done, 1)
                        shares(slice(CT * c, CT * c + CT), nm_done, c + 1, z_link, c, dd_done,
                               ee_done, c + 1, z_done)

            pool.wait_ge(bias_loaded, 16 * 4)
            with pool.If(fast_reg == 1):
                chunks(True)
                with pool.Fori(0, HT) as i:
                    shares(bass.ds(i + HT, 1), nmt_done, i + 1, zt_link, i, ddt_done, eet_done, i + 1, zt_done)
                pool.nop()
            with pool.Else():
                chunks(False)
                pool.nop()

        @block.scalar
        def _(act):
            def rowsum(r, slot):
                if isinstance(r, int) and r < 4:
                    act.wait_ge(row_first[slot], 16)
                else:
                    act.wait_ge(row_loaded[slot], r * 4 - slot * 4)
                act.activation(row[slot][:, :], row[slot][:, :], ACT.Copy, accum_out=deg[:, bass.ds(r, 1)])\
                   .then_inc(rowsum_done, 1)

            def exp_row(r, slot, width):
                act.activation(row[slot][:, 0:width], row[slot][:, 0:width], ACT.Exp,
                               bias=nboff[:, bass.ds(r, 1)], scale=-OFF,
                               accum_out=zz[:, 1, bass.ds(r, 1)]).then_inc(exp_done, 1)

            def split(s, c):
                act.wait_ge(raw_loaded[c % 4], s * 4 - (c % 4) * 4 + 16)
                act.wait_ge(units, s * 2 + 2)
                act.activation(ahi[c % 2][:, :, :], raw[c % 4][:, :, :], ACT.Copy).then_inc(split_hi, 1)

            def features(gs, par):
                act.wait_ge(gscale_done, gs + 1)
                if not isinstance(gs, int) or gs:
                    act.wait_ge(g_lo, gs)
                for b in range(GRP):
                    act.activation(gf[:, b, :], xg[par][:, b, :], ACT.Relu, bias=hs[par][:, 1, b:b + 1],
                                   scale=hs[par][:, 0, b:b + 1]).then_inc(gf_done, 1)
                act.wait_ge(gf_done, gs * GRP + GRP)
                act.activation(Ghi[par][:, :, :], gf[:, :, :], ACT.Copy).then_inc(g_hi, 1)

            def exp_first(r):
                act.wait_ge(nb_done, r + 1)
                exp_row(r, r % 4, N)

            rowsum(0, 0)
            rowsum(1, 1)
            exp_first(0)
            rowsum(2, 2)
            rowsum(3, 3)
            act.wait_ge(gid_copied, BANKS + 1)
            split(0, 0)
            features(0, 0)
            exp_first(1)
            exp_first(2)
            exp_first(3)
            rowsum(4, 0)
            act.wait_ge(flag_ready, 1)
            fast_reg = act.value_load(flag[0:1, 0:1], min_val=0, max_val=1)

            def split_agg(c):
                act.wait_ge(acc_done, UB + 2 * (STEPS - CHUNKS + c) + 2)
                if c:
                    act.wait_ge(z_full, CT * c)
                act.activation(Ahi[:, :, :], aggT[:, :, CW * c:CW * c + CW], ACT.Copy).then_inc(a_hi, 1)

            def hidden(c):
                act.wait_ge(hscale_done, c + 1)
                if c:
                    act.wait_ge(tr_full, KD * c)
                for b in range(CT):
                    act.activation(hn[:, b, :], x1[c % 3][:, b, :], ACT.Relu, bias=hs[c % 2][:, 1, b:b + 1],
                                   scale=hs[c % 2][:, 0, b:b + 1]).then_inc(h_done, 1)

            def group(g, par):
                static = isinstance(g, int)
                for c in range(CHUNKS):
                    s = CHUNKS * g + c
                    if not static or s + 1 < STEPS:
                        split(s + 1, (c + 1) % CHUNKS)
                    if c == 6 and (not static or g + 1 < GROUPS):
                        features(g + 1, 1 - par)
                    r = GRP * g + 4 + c // 2
                    slot = c // 2
                    if c % 2 == 0:
                        if not static or r + 1 < TILES:
                            rowsum(r + 1, (slot + 1) % 4)
                    elif not static or r < TILES:
                        act.wait_ge(nb_done, r + 1)
                        cond = fast_reg == 1 if static else (fast_reg * HT + r) >= 2 * HT
                        with act.If(cond):
                            exp_row(r, slot, HALF)
                        with act.Else():
                            exp_row(r, slot, N)
                    if static and g == GROUPS - 1:
                        if c == 1:
                            for i in range(4):
                                act.wait_ge(w_loaded, 64)
                                act.activation(Whi[:, i, :, :], Wraw[:, i, :, :], ACT.Copy,
                                               scale=1.0 / 32 if i == 1 else 1.0).then_inc(w_hi, 1)
                            act.wait_ge(bias_loaded, 16 * 4)
                            act.activation(bvr[:, 0, :], bvrow[:, :], ACT.Copy).then_inc(w_hi, 1)
                            act.activation(ones1[:, :], bvrow[:, 0:P], ACT.Copy, bias=1.0, scale=0.0).then_inc(w_hi, 1)
                        if c == 3:
                            split_agg(0)
                        if c == 4:
                            act.wait_ge(m_full, 1)
                            act.activation(Mhi[:, :, :].rearrange("p k d -> p (k d)"), ps[2][:, :], ACT.Copy)\
                               .then_inc(m_hi, 1)
                        if c == 7:
                            hidden(0)

            with act.Fori(0, 3) as u:
                group(u * 2, 0)
                group(u * 2 + 1, 1)
            group(6, 0)
            group(7, 1)

            def split_hT(c, ring, fast):
                k = c % HCH
                if c >= HCH:
                    if fast:
                        act.wait_ge(ring_full, ring[("S", c - HCH)] + 1)
                    else:
                        act.wait_ge(spilled, 16 * 6 * (c - HCH + 1))
                for kk in range(KD):
                    act.wait_ge(tr_full, KD * c + kk + 1)
                    act.activation(KTh[:, kk, CW * k:CW * k + CW], ps[2 + kk][:, :], ACT.Copy).then_inc(ht_hi, 1)

            def chunks(fast):
                ring = RING[fast]
                split_agg(1)
                split_hT(0, ring, fast)
                for c in range(CHUNKS + 1):
                    diag = fast and 1 <= c <= HCH
                    k = c % HCH
                    if diag:
                        n = ring[("PT", c - 1)]
                        act.wait_ge(ring_full, n + 1)
                        if c > 1:
                            act.wait_ge(ring_full, ring[("O", c - 2, 1)] + 1)
                        act.activation(PTdh[:, :], ps[4 + n % 4][:, :], ACT.Copy).then_inc(ptd_hi, 1)
                    if c < CHUNKS:
                        if not fast and c >= HCH:
                            act.wait_ge(spilled, 16 * 6 * (c - HCH + 1))
                        for o in range(KD):
                            n = ring[("q", c, o)]
                            act.wait_ge(ring_full, n + 1)
                            act.activation(QTh[:, o, CW * k:CW * k + CW], ps[4 + n % 4][:, :], ACT.Identity,
                                           bias=bqk[:, o:o + 1]).then_inc(proj_hi, 1)
                        if c + 1 < CHUNKS:
                            hidden(c + 1)
                        if fast and c >= HCH:
                            act.wait_ge(ring_full, ring[("O", c - HCH, 1)] + 1)
                        for i in range(2):
                            n = ring[("v", c, i)]
                            act.wait_ge(ring_full, n + 1)
                            act.activation(Vh[:, CT * k + 2 * i:CT * k + 2 * i + 2, :].rearrange("p a d -> p (a d)"),
                                           ps[4 + n % 4][:, :], ACT.Copy).then_inc(proj_hi, 1)
                        if c + 2 < CHUNKS:
                            split_agg(c + 2)
                    if fast and c < HCH:
                        if c:
                            act.wait_ge(ring_full, ring[("PT", c - 1)] + 1)
                        act.wait_ge(nmx_done, c + 1)
                        for b in range(CT):
                            t = CT * c + b
                            act.activation(Ed[:, b, :], Sd[:, b, :], ACT.Exp, bias=nmx[:, t:t + 1],
                                           accum_out=zz[:, 0, t:t + 1]).then_inc(dexp_done, 1)
                        act.wait_ge(dd_done, c + 1)
                        act.activation(ee[:, :, CT * c:CT * c + CT], dd[:, :, CT * c:CT * c + CT], ACT.Exp)\
                           .then_inc(ee_done, 1)
                    if c + 1 < CHUNKS:
                        split_hT(c + 1, ring, fast)

            def attend(i, par):
                act.wait_ge(m_done, i + 1)
                act.activation(SE[par][:, :], SE[par][:, :], ACT.Exp, bias=nmx[:, bass.ds(i + HT, 1)],
                               accum_out=zz[:, 0, bass.ds(i + HT, 1)]).then_inc(e_done, 1)
                act.wait_ge(ddt_done, i + 1)
                act.activation(ee[:, :, bass.ds(i + HT, 1)], dd[:, :, bass.ds(i + HT, 1)], ACT.Exp)\
                   .then_inc(eet_done, 1)

            def turned(i, q):
                act.wait_ge(pt_full, i * 4 + q + 1)
                act.activation(PTh[q % 2][:, :], ps[4 + q % 2][:, :], ACT.Copy).then_inc(pt_hi, 1)

            with act.If(fast_reg == 1):
                chunks(True)
                attend(0, 0)

                def tile(i, par):
                    for q in range(4):
                        turned(i, q)
                    if not isinstance(i, int) or i + 1 < HT:
                        attend(i + 1, 1 - par)

                with act.Fori(0, HT // 2 - 1) as v:
                    tile(v * 2, 0)
                    tile(v * 2 + 1, 1)
                tile(HT - 2, 0)
                tile(HT - 1, 1)
                act.nop()
            with act.Else():
                chunks(False)
                with act.Fori(0, TILES) as t:
                    with act.Fori(0, CHUNKS) as c:
                        n = t * CHUNKS + c
                        act.wait_ge(g_sd, n + 1)
                        act.activation(SE[1][:, 0:CW], SE[0][:, 0:CW], ACT.Exp, bias=nm[:, 0:1],
                                       accum_out=zz[:, 0, 0:1]).then_inc(g_exp, 1)
                        act.activation(ee[:, 0, 0:1], dd[:, 0, 0:1], ACT.Exp).then_inc(g_exp, 1)
                        act.wait_ge(g_tr, n + 1)
                        act.activation(PTh[0][:, :], ps[4][:, :], ACT.Copy).then_inc(g_phi, 1)
                act.nop()

        @block.vector
        def _(dve):
            dve.wait_ge(ptr_loaded, 16)
            dve.tensor_copy(ptrf[:, :], ptri[:, :]).then_inc(setup_link, 1)
            dve.wait_ge(setup_link, 1)
            dve.wait_ge(iota_done, 1)
            dve.tensor_scalar(cmp[:, :], iota[:, :], ptrf[:, 0:1], None, ALU.is_ge).then_inc(cmp_done, 1)
            for k in range(BANKS):
                dve.wait_ge(gid_full, k + 1)
                dve.tensor_copy(gidrow[:, CW * k:CW * k + CW], ps[k][:, :]).then_inc(gid_copied, 1)
            dve.wait_ge(gid_full, BANKS + 1)
            dve.tensor_copy(gidcol[:, :], ps[0][:, 0:TILES]).then_inc(gid_copied, 1)
            dve.wait_ge(gid_copied, BANKS + 1)
            for t in range(HT):
                dve.tensor_scalar(penn[:, t, :], gidrow[:, P * t:P * t + P], gidcol[:, t:t + 1], -BIG / 2,
                                  ALU.not_equal, ALU.mult).then_inc(setup_link, 1)
            edges = gidrow[0:1, 0:HALF + P].rearrange("p (t q) -> p t q", q=P)
            dve.tensor_tensor(flagw[0:1, 0:HT], edges[:, 1:HT + 1, 0], edges[:, 0:HT, P - 1], ALU.is_gt)\
               .then_inc(setup_link, 1)
            dve.tensor_tensor(flagw[0:1, HT:HT + 1], gidrow[0:1, HALF:HALF + 1], gidrow[0:1, N - 1:N], ALU.is_equal)\
               .then_inc(setup_link, 1)
            dve.wait_ge(setup_link, HT + 3)
            dve.tensor_reduce(flag[0:1, 0:1], flagw[0:1, 0:HT + 1], AX_X, ALU.min).then_inc(flag_ready, 1)
            dve.wait_ge(flag_ready, 1)
            fast_reg = dve.value_load(flag[0:1, 0:1], min_val=0, max_val=1)

            def mask_rows(r, slot):
                for k in range(4):
                    m = r * 8 + 2 * k
                    cols = slice(1024 * k, 1024 * k + 1024)
                    dve.tensor_scalar(masktmp[:, :], gidrow[:, cols], gidcol[:, bass.ds(r, 1)], BIG,
                                      ALU.is_equal, ALU.mult).then_inc(mask_link, 1)
                    dve.wait_ge(mask_link, m + 1)
                    dve.tensor_tensor(row[slot][:, cols], row[slot][:, cols], masktmp[:, :], ALU.add)\
                       .then_inc(mask_link, 1)
                    dve.wait_ge(mask_link, m + 2)
                dve.tensor_reduce(mn[:, bass.ds(r, 1)], row[slot][:, :], AX_X, ALU.min).then_inc(mn_done, 1)

            def mask_tile(r, slot):
                own = row[slot][:, bass.ds(r * P, P)]
                dve.scalar_tensor_tensor(out=own, in0=penn[:, bass.ds(r, 1), :].rearrange("p a j -> p (a j)"),
                                         scalar=BIG / 2, in1=own, op0=ALU.add, op1=ALU.add).then_inc(masked, 1)
                dve.wait_ge(masked, r + 1)
                dve.tensor_reduce(mn[:, bass.ds(r, 1)], row[slot][:, :], AX_X, ALU.min).then_inc(mn_done, 1)

            def least(r, slot):
                wait_alone(dve, rowsum_done, r + 1)
                if isinstance(r, int):
                    with dve.If(fast_reg == 1):
                        if r < HT:
                            mask_tile(r, slot)
                        else:
                            dve.tensor_reduce(mn[:, r:r + 1], row[slot][:, 0:HALF], AX_X, ALU.min).then_inc(mn_done, 1)
                    with dve.Else():
                        mask_rows(r, slot)
                else:
                    with dve.If(fast_reg == 1):
                        with dve.If(r < HT):
                            mask_tile(nc.s_assert_within(
                                r, 0, HT - 1, skip_runtime_bounds_check_because="the branch is taken for r < HT"), slot)
                        with dve.Else():
                            dve.tensor_reduce(mn[:, bass.ds(r, 1)], row[slot][:, 0:HALF], AX_X, ALU.min)\
                               .then_inc(mn_done, 1)
                        dve.nop()
                    with dve.Else():
                        mask_rows(r, slot)
                dve.wait_ge(mn_done, r + 1)
                dve.tensor_scalar(nboff[:, bass.ds(r, 1)], mn[:, bass.ds(r, 1)], OFF, None, ALU.mult)\
                   .then_inc(nb_done, 1)

            def moments(gs, par, bs):
                xl = (gs // 2) * 16 + 16 if isinstance(gs, int) else (gs - par) * 8 + 16
                dve.wait_ge(xg_loaded[par], xl)
                if bs[0] == 0 and not (isinstance(gs, int) and gs == 0):
                    dve.wait_ge(gscale_done, gs)
                for b in bs:
                    dve.bn_stats(bnst[:, b, :], xg[par][:, b, :]).then_inc(bns_done, 1)
                for b in bs:
                    wait_alone(dve, bns_done, gs * GRP + b + 1)
                    dve.bn_aggr(mv[:, b, :], bnst[:, b, :]).then_inc(bn_done, 1)

            def split(s, c):
                dve.wait_ge(split_hi, s + 1)
                dve.tensor_tensor(alo[c % 2][:, :, :], raw[c % 4][:, :, :], ahi[c % 2][:, :, :].bitcast(F32),
                                  ALU.subtract).then_inc(split_lo, 1)

            def features(gs, par):
                dve.wait_ge(g_hi, gs + 1)
                dve.tensor_tensor(Glo[par][:, :, :], gf[:, :, :], Ghi[par][:, :, :].bitcast(F32), ALU.subtract)\
                   .then_inc(g_lo, 1)

            moments(0, 0, (0, 1))
            moments(0, 0, (2, 3))
            least(0, 0)
            least(1, 1)
            least(2, 2)
            split(0, 0)
            features(0, 0)
            least(3, 3)
            dve.wait_ge(agg_zero, 1)
            dve.sem_inc(acc_done, UB)

            def split_weights():
                for i in range(4):
                    dve.wait_ge(w_hi, i + 1)
                    dve.scalar_tensor_tensor(out=Wlo[:, i, :, :], in0=Wraw[:, i, :, :],
                                             scalar=1.0 / 32 if i == 1 else 1.0, in1=Whi[:, i, :, :].bitcast(F32),
                                             op0=ALU.mult, op1=ALU.subtract).then_inc(w_done, 1)
                dve.wait_ge(w_hi, 6)
                dve.tensor_tensor(bvr[:, 1, :], bvrow[:, :], bvr[:, 0, :].bitcast(F32), ALU.subtract).then_inc(w_done, 1)
                for k in range(KD):
                    dve.tensor_scalar(bqwide[:, k, :], ident[:, :], 0.0, bcols[:, 0, k:k + 1], ALU.mult, ALU.add)\
                       .then_inc(w_done, 1)

            def split_M():
                dve.wait_ge(m_hi, 1)
                dve.tensor_tensor(Mlo[:, :, :].rearrange("p k d -> p (k d)"), ps[2][:, :],
                                  Mhi[:, :, :].rearrange("p k d -> p (k d)").bitcast(F32), ALU.subtract)\
                   .then_inc(m_lo, 1)
                dve.wait_ge(m_full, 2)
                dve.tensor_scalar(bqk[:, :], ps[3][:, 0:KD], 1.0 / 32, None, ALU.mult)
                dve.tensor_scalar(c0[:, :], ps[3][:, 2 * KD:2 * KD + 1], 1.0 / 16, None, ALU.mult)
                dve.tensor_scalar(uf[:, :], ps[3][:, KD:2 * KD], 1.0 / 16, None, ALU.mult).then_inc(v_link, 1)
                dve.wait_ge(v_link, 1)
                dve.tensor_copy(ur[:, :, 0], uf[:, :]).then_inc(v_link, 1)
                dve.wait_ge(v_link, 2)
                dve.tensor_tensor(ur[:, :, 1], uf[:, :], ur[:, :, 0].bitcast(F32), ALU.subtract).then_inc(vec_done, 1)

            def split_agg(c):
                dve.wait_ge(a_hi, c + 1)
                dve.tensor_tensor(Alo[:, :, :], aggT[:, :, CW * c:CW * c + CW], Ahi[:, :, :].bitcast(F32),
                                  ALU.subtract).then_inc(a_lo, 1)

            def residual(c):
                dve.wait_ge(xb_done, c + 1)
                if c >= 3:
                    dve.wait_ge(x1_stored[c % 3], 16 * (c // 3))
                for b in range(CT):
                    t = CT * c + b
                    dve.wait_ge(z_full, t + 2 - b % 2)
                    dve.scalar_tensor_tensor(out=x1[c % 3][:, b, :], in0=ps[b // 2][:, D * (b % 2):D * (b % 2) + D],
                                             scalar=dis[:, t:t + 1], in1=xc[:, b, :], op0=ALU.mult, op1=ALU.add)\
                       .then_inc(x1_done, 1)
                if c:
                    dve.wait_ge(hscale_done, c)
                for b in range(CT):
                    dve.wait_ge(x1_done, CT * c + b + 1)
                    dve.bn_stats(bnst[:, b, :], x1[c % 3][:, b, :]).then_inc(bns2_done, 1)
                for b in range(CT):
                    dve.wait_ge(bns2_done, CT * c + b + 1)
                    dve.bn_aggr(mv[:, b, :], bnst[:, b, :]).then_inc(bn2_done, 1)

            def group(g, par):
                static = isinstance(g, int)
                for c in range(CHUNKS):
                    s = CHUNKS * g + c
                    if not static or s + 1 < STEPS:
                        split(s + 1, (c + 1) % CHUNKS)
                    r = GRP * g + 4 + c // 2
                    if c % 2 == 0 and (not static or r < TILES):
                        least(r, c // 2)
                    if c in (1, 3) and (not static or g + 1 < GROUPS):
                        moments(g + 1, 1 - par, (c - 1, c))
                    if c == 7 and (not static or g + 1 < GROUPS):
                        features(g + 1, 1 - par)
                    for k in range(KD):
                        dve.wait_ge(units, s * 2 + 5 + k)
                        dst = aggT[:, k, CW * c:CW * c + CW]
                        dve.tensor_tensor(dst, dst, ps[UB + (2 * c + k) % UB][:, :], ALU.add).then_inc(acc_done, 1)
                    if static and g == GROUPS - 1:
                        if c == 1:
                            split_weights()
                        if c == 3:
                            split_agg(0)
                        if c == 4:
                            split_M()
                        if c == 5:
                            residual(0)

            with dve.Fori(0, 3) as u:
                group(u * 2, 0)
                group(u * 2 + 1, 1)
            group(6, 0)
            group(7, 1)

            def split_hT(c):
                k = c % HCH
                for kk in range(KD):
                    dve.wait_ge(ht_hi, KD * c + kk + 1)
                    dve.tensor_tensor(KTl[:, kk, CW * k:CW * k + CW], ps[2 + kk][:, :],
                                      KTh[:, kk, CW * k:CW * k + CW].bitcast(F32), ALU.subtract).then_inc(ht_lo, 1)

            def row_greatest(cols, nmx_ready, n, link, done):
                dve.wait_ge(nmx_ready, n)
                dve.tensor_tensor(nmr[:, cols], nmx[:, cols], rr[:, cols], ALU.subtract).then_inc(link, 1)
                dve.wait_ge(link, n)
                dve.tensor_tensor(nm[:, cols], nmr[:, cols], nboff[:, cols], ALU.min).then_inc(done, 1)

            def row_coefs(cols, zd, z_n, link, l_n, done):
                wait_alone(dve, zd, z_n)
                dve.reciprocal(coef[:, cols], coef[:, cols]).then_inc(link, 1)
                dve.wait_ge(link, l_n)
                dve.tensor_tensor(coef[:, cols], coef[:, cols], ee[:, 0, cols], ALU.mult).then_inc(done, 1)
                dve.wait_ge(done, l_n)

            def chunks(fast):
                ring = RING[fast]
                split_agg(1)
                split_hT(0)
                for c in range(CHUNKS + 1):
                    diag = fast and 1 <= c <= HCH
                    k = c % HCH
                    if c + 1 < CHUNKS:
                        residual(c + 1)
                    if diag:
                        n = ring[("PT", c - 1)]
                        dve.wait_ge(ptd_hi, c)
                        dve.tensor_tensor(PTdl[:, :], ps[4 + n % 4][:, :], PTdh[:, :].bitcast(F32), ALU.subtract)\
                           .then_inc(ring_free, 1)
                    if c < CHUNKS:
                        for o in range(KD):
                            n = ring[("q", c, o)]
                            dve.wait_ge(proj_hi, 4 * c + o + 1)
                            dve.scalar_tensor_tensor(
                                out=QTl[:, o, CW * k:CW * k + CW], in0=ps[4 + n % 4][:, :],
                                scalar=bqk[:, o:o + 1], in1=QTh[:, o, CW * k:CW * k + CW].bitcast(F32),
                                op0=ALU.add, op1=ALU.subtract).then_inc(ring_free, 1)
                        n = ring[("r", c)]
                        pairs = ps[4 + n % 4][:, 0:2 * CT].rearrange("p (b a) -> p b a", a=2)
                        dve.wait_ge(ring_full, n + 1)
                        dve.tensor_scalar(rr[:, CT * c:CT * c + CT], pairs[:, :, 0], c0[:, 0:1], None, ALU.add)\
                           .then_inc(r_link, 1)
                        dve.wait_ge(r_link, c + 1)
                        dve.tensor_tensor(rr[:, CT * c:CT * c + CT], rr[:, CT * c:CT * c + CT], pairs[:, :, 1],
                                          ALU.add).then_inc(ring_free, 1)
                    if diag:
                        row_coefs(slice(CT * (c - 1), CT * c), z_done, c, coef_link, c, coef_done)
                        for b in range(CT):
                            t = CT * (c - 1) + b
                            n = ring[("O", c - 1, b // 2)]
                            dve.wait_ge(ring_full, n + 1)
                            xo = x1[(c - 1) % 3][:, b, :]
                            last = dve.scalar_tensor_tensor(
                                out=xo, in0=ps[4 + n % 4][:, D * (b % 2):D * (b % 2) + D], scalar=coef[:, t:t + 1],
                                in1=xo, op0=ALU.mult, op1=ALU.add)
                            if b % 2:
                                last.then_inc(ring_free, 1)
                    if c < CHUNKS:
                        for i in range(2):
                            n = ring[("v", c, i)]
                            dve.wait_ge(proj_hi, 4 * c + 3 + i)
                            v = slice(CT * k + 2 * i, CT * k + 2 * i + 2)
                            dve.tensor_tensor(Vl[:, v, :].rearrange("p a d -> p (a d)"), ps[4 + n % 4][:, :],
                                              Vh[:, v, :].rearrange("p a d -> p (a d)").bitcast(F32), ALU.subtract)\
                               .then_inc(ring_free, 1)
                        if c + 2 < CHUNKS:
                            split_agg(c + 2)
                    if fast and c < HCH:
                        n = ring[("S", c)]
                        dve.wait_ge(ring_full, n + 1)
                        dve.wait_ge(adjp_done, c + 1)
                        if c:
                            dve.wait_ge(dexp_done, CT * c)
                        for b in range(CT):
                            last = dve.tensor_tensor_reduce(
                                out=Sd[:, b, :], in0=ps[4 + n % 4][:, P * b:P * b + P], in1=adjd[:, b, :],
                                scale=2.0, scalar=-3e38, op0=ALU.add, op1=ALU.max, accum_out=mx4[:, b:b + 1])
                        last.then_inc(ring_free, 1)
                        dve.wait_ge(ring_free, n + 1)
                        dve.tensor_scalar(nmx[:, CT * c:CT * c + CT], mx4[:, :], -1.0, None, ALU.mult)\
                           .then_inc(nmx_done, 1)
                        row_greatest(slice(CT * c, CT * c + CT), nmx_done, c + 1, nm_link, nm_done)
                    if c + 1 < CHUNKS:
                        split_hT(c + 1)

            def score_bank(i, par, jc):
                if jc == 0:
                    dve.wait_ge(adjr_loaded[par], i * 8 - 8 * par + 16)
                wait_alone(dve, s_full, i * 4 + jc + 1)
                dve.tensor_tensor_reduce(
                    out=SE[par][:, CW * jc:CW * jc + CW], in0=ps[jc][:, :], in1=adjr[par][:, CW * jc:CW * jc + CW],
                    scale=2.0, scalar=-3e38, op0=ALU.add, op1=ALU.max, accum_out=mx4t[:, jc:jc + 1])\
                   .then_inc(s_read, 1)

            def greatest(i):
                t = bass.ds(i + HT, 1)
                dve.wait_ge(s_read, i * 4 + 4)
                dve.tensor_reduce(nmx[:, t], mx4t[:, :], AX_X, ALU.max, negate=True).then_inc(m_done, 1)
                row_greatest(t, m_done, i + 1, nmt_link, nmt_done)

            def turned(i, q):
                dve.wait_ge(pt_hi, i * 4 + q + 1)
                dve.tensor_tensor(PTl[q % 2][:, :], ps[4 + q % 2][:, :], PTh[q % 2][:, :].bitcast(F32), ALU.subtract)\
                   .then_inc(pt_lo, 1)

            def finish(i, par):
                t = bass.ds(i + HT, 1)
                row_coefs(t, zt_done, i + 1, coeft_link, i + 1, coeft_done)
                dve.wait_ge(x1t_loaded[par], i * 8 - 8 * par + 16)
                dve.wait_ge(o_full, i + 1)
                if not isinstance(i, int) or i >= 2:
                    dve.wait_ge(outt_stored[par], i * 8 - 8 * par)
                dve.scalar_tensor_tensor(out=outb[par][:, :], in0=ps[6 + par][:, 0:D], scalar=coef[:, t],
                                         in1=x1t[par][:, :], op0=ALU.mult, op1=ALU.add).then_inc(o_read, 1)

            with dve.If(fast_reg == 1):
                chunks(True)

                def tile(i, par):
                    for q in range(4):
                        if not isinstance(i, int) or i + 1 < HT:
                            score_bank(i + 1, 1 - par, q)
                        turned(i, q)
                    if not isinstance(i, int) or i + 1 < HT:
                        greatest(i + 1)
                    finish(i, par)

                for q in range(4):
                    score_bank(0, 0, q)
                greatest(0)
                tile(0, 0)
                tile(1, 1)
                with dve.Fori(1, HT // 2 - 1) as v:
                    tile(v * 2, 0)
                    tile(v * 2 + 1, 1)
                tile(HT - 2, 0)
                tile(HT - 1, 1)
                dve.nop()
            with dve.Else():
                chunks(False)
                dve.wait_ge(x1_stored[0], 16 * len(range(0, CHUNKS, 3)))
                dve.sem_inc(g_end, 1)
                with dve.Fori(0, TILES) as t:
                    col = bass.ds(t, 1)
                    dve.tensor_copy(nm[:, 0:1], nboff[:, col]).then_inc(g_link, 1)
                    dve.tensor_copy(zz[:, 1, 0:1], zz[:, 1, col]).then_inc(g_link, 1)
                    dve.memset(Og[:, :], 0.0).then_inc(g_link, 1)
                    with dve.Fori(0, CHUNKS) as c:
                        n = t * CHUNKS + c
                        L = t * (3 + 8 * CHUNKS) + c * 8 + 3
                        dve.wait_ge(g_link, L)
                        dve.wait_ge(g_load, n * 128 + 128)
                        dve.wait_ge(g_score, n + 1)
                        dve.tensor_tensor(SE[0][:, 0:CW], ps[0][:, :], adjr[0][:, 0:CW], ALU.add)
                        dve.tensor_scalar(SE[1][:, CW:2 * CW], gidrow[:, bass.ds(c * CW, CW)], gidcol[:, col], -BIG,
                                          ALU.not_equal, ALU.mult).then_inc(g_link, 1)
                        dve.wait_ge(g_link, L + 1)
                        dve.scalar_tensor_tensor(out=SE[0][:, 0:CW], in0=SE[0][:, 0:CW], scalar=2.0,
                                                 in1=SE[1][:, CW:2 * CW], op0=ALU.mult, op1=ALU.add).then_inc(g_link, 1)
                        dve.wait_ge(g_link, L + 2)
                        dve.tensor_scalar(SE[0][:, 0:CW], SE[0][:, 0:CW], rr[:, col], None, ALU.add)\
                           .then_inc(g_rlink, 1)
                        dve.wait_ge(g_rlink, n + 1)
                        dve.tensor_reduce(nmx[:, 0:1], SE[0][:, 0:CW], AX_X, ALU.max, negate=True).then_inc(g_link, 1)
                        dve.wait_ge(g_link, L + 3)
                        dve.tensor_tensor(nmx[:, 1:2], nmx[:, 0:1], nm[:, 0:1], ALU.min).then_inc(g_link, 1)
                        dve.wait_ge(g_link, L + 4)
                        dve.tensor_tensor(dd[:, 0, 0:1], nmx[:, 1:2], nm[:, 0:1], ALU.subtract).then_inc(g_link, 1)
                        dve.wait_ge(g_link, L + 5)
                        dve.tensor_copy(nm[:, 0:1], nmx[:, 1:2]).then_inc(g_sd, 1)
                        dve.wait_ge(g_exp, n * 2 + 2)
                        dve.scalar_tensor_tensor(out=zz[:, 1, 0:1], in0=zz[:, 1, 0:1], scalar=ee[:, 0, 0:1],
                                                 in1=zz[:, 0, 0:1], op0=ALU.mult, op1=ALU.add).then_inc(g_link, 1)
                        dve.wait_ge(g_phi, n + 1)
                        dve.tensor_tensor(PTl[0][:, :], ps[4][:, :], PTh[0][:, :].bitcast(F32), ALU.subtract)\
                           .then_inc(g_plo, 1)
                        dve.wait_ge(g_pv, n + 1)
                        dve.scalar_tensor_tensor(out=Og[:, :], in0=Og[:, :], scalar=ee[:, 0, 0:1],
                                                 in1=ps[6][:, 0:D], op0=ALU.mult, op1=ALU.add).then_inc(g_link, 1)
                        dve.wait_ge(g_link, L + 7)
                        dve.tensor_copy(coef[:, 0:1], zz[:, 1, 0:1]).then_inc(g_link, 1)
                        wait_alone(dve, g_link, L + 8)
                        with dve.If(c < CHUNKS - 1):
                            dve.sem_inc(g_end, 1)
                        with dve.Else():
                            dve.nop()
                        dve.nop()
                    dve.reciprocal(coef[:, 0:1], coef[:, 0:1]).then_inc(g_fin, 1)
                    dve.wait_ge(g_fin, t + 1)
                    dve.scalar_tensor_tensor(out=outb[0][:, :], in0=Og[:, :], scalar=coef[:, 0:1],
                                             in1=x1t[0][:, :], op0=ALU.mult, op1=ALU.add).then_inc(g_out, 1)
                    dve.wait_ge(g_out, t + 1)
                    dve.sem_inc(g_end, 1)
                dve.nop()

        @block.tensor
        def _(pe):
            pe.wait_ge(const_done, 4)
            pe.wait_ge(cmp_done, 1)
            for k in range(BANKS):
                pe.matmul(ps[k][:, :], ones33[:, :], cmp[:, CW * k:CW * k + CW], start=True, stop=True)\
                  .then_inc(gid_full, 1)
            pe.wait_ge(gid_copied, 1)
            for t in range(TILES):
                last = pe.matmul(ps[0][:, t:t + 1], cmp[:, P * t:P * t + P], ones33[:, 0:1], start=True, stop=True)
            last.then_inc(gid_full, 1)
            pe.wait_ge(gid_copied, BANKS + 1)
            pe.sem_inc(units, 4)
            pe.wait_ge(flag_ready, 1)
            fast_reg = pe.value_load(flag[0:1, 0:1], min_val=0, max_val=1)

            def group(g, par):
                pe.wait_ge(g_lo, g + 1)
                for c in range(CHUNKS):
                    s = CHUNKS * g + c
                    pe.wait_ge(split_lo, s + 1)
                    for k in range(KD):
                        pe.wait_ge(acc_done, s * 2 + k + 1)
                        for t in range(GRP):
                            last = mm3(pe, ps[UB + (2 * c + k) % UB][:, :],
                                       Ghi[par][:, t, P * k:P * k + P], Glo[par][:, t, P * k:P * k + P],
                                       ahi[c % 2][:, t, :], alo[c % 2][:, t, :], t == 0, t == GRP - 1)
                        last.then_inc(units, 1)
                    if isinstance(g, int) and g == GROUPS - 1:
                        if c == 3:
                            fold()
                        if c == 5:
                            residual(0)

            def fold():
                pe.wait_ge(w_done, 7)
                for k in range(KD):
                    for o in range(KD):
                        last = mm3(pe, ps[2][:, D * k:D * k + D], Whi[:, 1, o, P * k:P * k + P],
                                   Wlo[:, 1, o, P * k:P * k + P], Whi[:, 2, o, :], Wlo[:, 2, o, :], o == 0, o == KD - 1)
                last.then_inc(m_full, 1)
                for j, i, k in ((0, 2, 0), (0, 2, 1), (1, 1, 0), (1, 1, 1)):
                    for o in range(KD):
                        pe.matmul(ps[3][:, KD * j + k:KD * j + k + 1], Wraw[:, i, o, P * k:P * k + P],
                                  bcols[:, j, o:o + 1], start=o == 0, stop=o == KD - 1)
                for o in range(KD):
                    last = pe.matmul(ps[3][:, 2 * KD:2 * KD + 1], bqwide[:, o, :], bcols[:, 1, o:o + 1],
                                     start=o == 0, stop=o == KD - 1)
                last.then_inc(m_full, 1)

            def residual(c):
                pe.wait_ge(a_lo, c + 1)
                for b in range(CT):
                    if c:
                        pe.wait_ge(x1_done, CT * (c - 1) + b + 2 - b % 2)
                    for k in range(KD):
                        last = mm3(pe, ps[b // 2][:, D * (b % 2):D * (b % 2) + D],
                                   Ahi[:, k, P * b:P * b + P], Alo[:, k, P * b:P * b + P],
                                   Whi[:, 0, k, :], Wlo[:, 0, k, :], k == 0, k == KD - 1)
                    last.then_inc(z_full, 1)

            def turn(c):
                pe.wait_ge(h_done, CT * (c + 1))
                if c:
                    pe.wait_ge(ht_lo, KD * c)
                for k in range(KD):
                    for b in range(CT):
                        last = pe.transpose(ps[2 + k][:, P * b:P * b + P], hn[:, b, P * k:P * k + P], ident[:, :])
                    last.then_inc(tr_full, 1)

            with pe.Fori(0, 3) as u:
                group(u * 2, 0)
                group(u * 2 + 1, 1)
            group(6, 0)
            group(7, 1)

            def chunks(fast):
                ring = RING[fast]

                def bank(key):
                    n = ring[key]
                    if n >= 4:
                        pe.wait_ge(ring_free, n - 3)
                    return ps[4 + n % 4]

                pe.wait_ge(acc_done, UB + 2 * STEPS)
                pe.wait_ge(m_lo, 1)
                pe.wait_ge(vec_done, 1)
                turn(0)
                for c in range(CHUNKS + 1):
                    diag = fast and 1 <= c <= HCH
                    k = c % HCH
                    ch = slice(CW * k, CW * k + CW)
                    if c + 1 < CHUNKS:
                        residual(c + 1)
                    if diag:
                        pe.wait_ge(dexp_done, CT * c)
                        o = bank(("PT", c - 1))
                        for b in range(CT):
                            last = pe.transpose(o[:, P * b:P * b + P], Ed[:, b, :], ident[:, :])
                        last.then_inc(ring_full, 1)
                    if c < CHUNKS:
                        pe.wait_ge(ht_lo, KD * (c + 1))
                        for oh in range(KD):
                            o = bank(("q", c, oh))
                            for kk in range(KD):
                                w = slice(P * oh, P * oh + P)
                                last = mm3(pe, o[:, :], Mhi[:, kk, w], Mlo[:, kk, w], KTh[:, kk, ch], KTl[:, kk, ch],
                                           kk == 0, kk == KD - 1)
                            last.then_inc(ring_full, 1)
                        o = bank(("r", c))
                        for b in range(CT):
                            w = slice(CW * k + P * b, CW * k + P * b + P)
                            for kk in range(KD):
                                pe.matmul(o[:, 2 * b:2 * b + 2], KTh[:, kk, w], ur[:, kk, :], start=kk == 0, stop=False)
                                last = pe.matmul(o[:, 2 * b:2 * b + 2], KTl[:, kk, w], ur[:, kk, :], start=False,
                                                 stop=kk == KD - 1)
                        last.then_inc(ring_full, 1)
                    if diag:
                        pe.wait_ge(ring_free, ring[("PT", c - 1)] + 1)
                        kd = (c - 1) % HCH
                        for b in range(CT):
                            if b % 2 == 0:
                                o = bank(("O", c - 1, b // 2))
                            last = mm3(pe, o[:, D * (b % 2):D * (b % 2) + D],
                                       PTdh[:, P * b:P * b + P], PTdl[:, P * b:P * b + P],
                                       Vh[:, CT * kd + b, :], Vl[:, CT * kd + b, :], True, True)
                            if b % 2:
                                last.then_inc(ring_full, 1)
                    if c < CHUNKS:
                        for i in range(2):
                            o = bank(("v", c, i))
                            for b in (2 * i, 2 * i + 1):
                                ob = o[:, D * (b % 2):D * (b % 2) + D]
                                w = slice(CW * k + P * b, CW * k + P * b + P)
                                pe.matmul(ob, ones1[:, :], bvr[:, 0, :], start=True, stop=False)
                                pe.matmul(ob, ones1[:, :], bvr[:, 1, :], start=False, stop=False)
                                for kk in range(KD):
                                    last = mm3(pe, ob, KTh[:, kk, w], KTl[:, kk, w],
                                               Whi[:, 3, kk, :], Wlo[:, 3, kk, :], False, kk == KD - 1)
                            last.then_inc(ring_full, 1)
                    if fast and c < HCH:
                        pe.wait_ge(ring_free, ring[("q", c, 1)] + 1)
                        o = bank(("S", c))
                        for b in range(CT):
                            w = slice(CW * k + P * b, CW * k + P * b + P)
                            for oh in range(KD):
                                last = mm3(pe, o[:, P * b:P * b + P], QTh[:, oh, w], QTl[:, oh, w],
                                           KTh[:, oh, w], KTl[:, oh, w], oh == 0, oh == KD - 1)
                        last.then_inc(ring_full, 1)
                    if c + 1 < CHUNKS:
                        turn(c + 1)
                pe.wait_ge(ring_free, len(ring))

            def score_bank(i, jc):
                if i:
                    pe.wait_ge(s_read, 4 * (i - 1) + jc + 1)
                for oh in range(KD):
                    w, j = slice(P * i, P * i + P), slice(CW * jc, CW * jc + CW)
                    last = mm3(pe, ps[jc][:, :], QTh[:, oh, w], QTl[:, oh, w], KTh[:, oh, j], KTl[:, oh, j],
                               oh == 0, oh == KD - 1)
                last.then_inc(s_full, 1)

            def turn_quarter(i, q):
                if q == 0:
                    pe.wait_ge(e_done, i + 1)
                if 4 * i + q >= 2:
                    pe.wait_ge(pt_lo, 4 * i + q - 1)
                for b in range(4):
                    j = CW * q + P * b
                    last = pe.transpose(ps[4 + q % 2][:, P * b:P * b + P], SE[i % 2][:, j:j + P], ident[:, :])
                last.then_inc(pt_full, 1)

            def weigh_quarter(i, q):
                pe.wait_ge(pt_lo, 4 * i + q + 1)
                if q == 0 and i >= 2:
                    pe.wait_ge(o_read, i - 1)
                for b in range(4):
                    last = mm3(pe, ps[6 + i % 2][:, 0:D], PTh[q % 2][:, P * b:P * b + P], PTl[q % 2][:, P * b:P * b + P],
                               Vh[:, 4 * q + b, :], Vl[:, 4 * q + b, :], q == 0 and b == 0, q == 3 and b == 3)
                if q == 3:
                    last.then_inc(o_full, 1)

            with pe.If(fast_reg == 1):
                chunks(True)
                for jc in range(4):
                    score_bank(0, jc)
                for i in range(HT):
                    for q in range(4):
                        if i + 1 < HT:
                            score_bank(i + 1, q)
                        turn_quarter(i, q)
                        if q:
                            weigh_quarter(i, q - 1)
                    weigh_quarter(i, 3)
            with pe.Else():
                chunks(False)
                with pe.Fori(0, TILES) as t:
                    with pe.Fori(0, CHUNKS) as c:
                        n = t * CHUNKS + c
                        pe.wait_ge(g_load, n * 128 + 128)
                        for oh in range(KD):
                            last = mm3(pe, ps[0][:, :], QTh[:, oh, 0:P], QTl[:, oh, 0:P], KTh[:, oh, 0:CW],
                                       KTl[:, oh, 0:CW], oh == 0, oh == KD - 1)
                        last.then_inc(g_score, 1)
                        pe.wait_ge(g_exp, n * 2 + 2)
                        for b in range(4):
                            last = pe.transpose(ps[4][:, P * b:P * b + P], SE[1][:, P * b:P * b + P], ident[:, :])
                        last.then_inc(g_tr, 1)
                        pe.wait_ge(g_plo, n + 1)
                        for b in range(4):
                            last = mm3(pe, ps[6][:, 0:D], PTh[0][:, P * b:P * b + P], PTl[0][:, P * b:P * b + P],
                                       Vh[:, b, :], Vl[:, b, :], b == 0, b == 3)
                        last.then_inc(g_pv, 1)
                pe.nop()


def kernel(x, adj, L0_gnn_W, L0_gnn_b, L1_gnn_ptr, L1_gnn_Wq, L1_gnn_bq, L1_gnn_Wk, L1_gnn_bk, L1_gnn_Wv, L1_gnn_bv):
    import numpy as _np
    import concourse.bacc as _bacc
    from concourse import mybir as _mybir
    from concourse.bass_utils import run_bass_kernel_spmd as _run

    a = _np.asarray(adj)
    blocks = a.reshape(CHUNKS, CW, GROUPS, GRP, P).transpose(2, 0, 4, 3, 1).reshape(STEPS * P, GRP * CW)
    ins = {
        "x": x, "adj": a, "adjT": blocks, "W0T": _np.asarray(L0_gnn_W).T, "b0": L0_gnn_b,
        "ptr": _np.asarray(L1_gnn_ptr).reshape(NPTR, 1), "Wq": L1_gnn_Wq, "bq": _np.asarray(L1_gnn_bq).reshape(KD, P).T,
        "Wk": L1_gnn_Wk, "bk": _np.asarray(L1_gnn_bk).reshape(KD, P).T, "WvT": _np.asarray(L1_gnn_Wv).T, "bv": L1_gnn_bv,
    }
    nc = _bacc.Bacc("TRN2", target_bir_lowering=False, num_devices=1)
    arrays, args = {}, {}
    for name, value in ins.items():
        value = _np.ascontiguousarray(value)
        arrays[f"in_{name}_dram"] = value
        args[name] = nc.dram_tensor(f"in_{name}_dram", value.shape, _mybir.dt.from_np(value.dtype),
                                    kind="ExternalInput").ap()
    out = nc.dram_tensor("out_0_dram", (N, D), _mybir.dt.float32, kind="ExternalOutput").ap()
    gnn_kernel(nc, out=out, **args)
    r = _run(nc, [arrays], core_ids=[0])
    return r.results[0]["out_0_dram"]
```

```python
from contextlib import ExitStack

import concourse.bass as bass
from concourse import mybir

F32 = mybir.dt.float32
F32R = mybir.dt.float32r
BF16 = mybir.dt.bfloat16
I32 = mybir.dt.int32
U8 = mybir.dt.uint8
ALU = mybir.AluOpType
ACT = mybir.ActivationFunctionType
AX_X = mybir.AxisListType.X

P = 128
N = 4096
D = 256
KD = D // P
TILES = N // P
GRP = 4
GROUPS = TILES // GRP
CW = 512
CHUNKS = N // CW
STEPS = GROUPS * CHUNKS
CT = CW // P
HALF = N // 2
HCH = CHUNKS // 2
HT = TILES // 2
BANKS = 8
UB = 4
NPTR = 33
BK = 33
DV = D + 2
BIG = 2.0 ** 100
OFF = 2e6
EPS_DEG = 1e-8
EPS_LN = 1e-5


def gnn_kernel(nc, x, adj, adjT, W0T, b0, ptr, Wq, bq, Wk, bk, WvT, bv, out):
    with ExitStack() as ctx:
        cursor = [nc.sbuf_base + (-nc.sbuf_base) % 32]

        def at(name, shape, dt, offset=None):
            size = {F32: 4, F32R: 4, I32: 4, BF16: 2, U8: 1}[dt]
            for n in shape[1:]:
                size *= n
            size += -size % 32
            if offset is None:
                offset = cursor[0]
                cursor[0] += size
            assert offset + size <= nc.sbuf_usable_end, (name, offset + size, nc.sbuf_usable_end)
            return nc.alloc_sbuf_tensor_at(name, shape, dt, offset=offset), offset

        def sb(name, shape, dt, offset=None):
            return at(name, shape, dt, offset)[0]

        def sem(name):
            return ctx.enter_context(nc.semaphore(name))

        penn = sb("penn", [P, HT, P], BF16)
        gidrow = sb("gidrow", [P, N], U8)
        gidcol = sb("gidcol", [P, TILES], F32)
        deg = sb("deg", [P, TILES], F32)
        dis = sb("dis", [P, TILES], F32)
        mn = sb("mn", [P, TILES], F32)
        nboff = sb("nboff", [P, TILES], F32)
        zz = sb("zz", [P, 2, TILES], F32)
        nmx = sb("nmx", [P, TILES], F32)
        rr = sb("rr", [P, TILES], F32)
        nmr = sb("nmr", [P, TILES], F32)
        nm = sb("nm", [P, TILES], F32)
        dd = sb("dd", [P, 2, TILES], F32)
        ee = sb("ee", [P, 2, TILES], F32)
        coef = sb("coef", [P, TILES], F32)
        ident = sb("ident", [P, P], F32)
        bcols = sb("bcols", [P, 2, KD], F32)
        bqwide = sb("bqwide", [P, KD, P], F32)
        bqk = sb("bqk", [P, KD], F32)
        uf = sb("uf", [P, KD], F32)
        c0 = sb("c0", [P, 1], F32)
        pick = sb("pick", [BK, P], F32R)
        pickc = sb("pickc", [BK, 1], F32)
        b0row = sb("b0row", [P, D], F32)
        bvr = sb("bvr", [BK, DV], F32R)
        ptri = sb("ptri", [NPTR, 1], I32)
        ptrf = sb("ptrf", [NPTR, 1], F32)
        flagw = sb("flagw", [1, 32], F32)
        flag = sb("flag", [1, 1], I32)
        mhalf = sb("mhalf", [P, GRP], F32)
        epsdeg = sb("epsdeg", [P, GRP], F32)
        off1 = sb("off1", [P, 1], F32)
        bnst = sb("bnst", [P, GRP, 6], F32)
        mv = sb("mv", [P, GRP, 2], F32)
        pw = sb("pw", [P, 4, GRP], F32)
        hs = [sb(f"hs{i}", [P, 2, GRP], F32) for i in range(2)]
        mx4 = sb("mx4", [P, CT], F32)
        mx4t = sb("mx4t", [P, CT], F32)

        regK = cursor[0]
        QTh = sb("QTh", [P, KD, HALF], F32R)
        QTl = sb("QTl", [P, KD, HALF], F32R)
        KTh = sb("KTh", [P, KD, HALF], F32R)
        KTl = sb("KTl", [P, KD, HALF], F32R)
        Vh = sb("Vh", [P, HT, D], F32R)
        Vl = sb("Vl", [P, HT, D], F32R)
        endK = cursor[0]
        cursor[0] = regK
        raw = [sb(f"raw{i}", [P, GRP, CW], F32) for i in range(4)]
        regS = cursor[0]
        ahi = [sb(f"ahi{i}", [P, GRP, CW], F32R) for i in range(2)]
        alo = [sb(f"alo{i}", [P, GRP, CW], F32R) for i in range(2)]
        Ghi = [sb(f"Ghi{i}", [P, GRP, D], F32R) for i in range(2)]
        Glo = [sb(f"Glo{i}", [P, GRP, D], F32R) for i in range(2)]
        gf = sb("gf", [P, GRP, D], F32)
        xg = [sb(f"xg{i}", [P, GRP, D], F32) for i in range(2)]
        masktmp = sb("masktmp", [P, 1024], BF16)
        bvrow = sb("bvrow", [BK, DV], F32)
        ones33 = sb("ones33", [NPTR, P], BF16)
        assert cursor[0] <= endK
        iota = sb("iota", [NPTR, N], I32, regS)
        cmp = sb("cmp", [NPTR, N], BF16, regS + 4 * N)
        cursor[0] = endK

        regA = cursor[0]
        aggT = sb("aggT", [P, KD, N], F32)
        adjr = [sb(f"adjr{i}", [P, HALF], F32, regA + 4 * HALF * i) for i in range(2)]
        SE = [sb(f"SE{i}", [P, HALF], F32, regA + 4 * HALF * (2 + i)) for i in range(2)]

        regR = cursor[0]
        row = [sb(f"row{i}", [P, N], F32) for i in range(4)]
        endR = cursor[0]
        cursor[0] = regR
        Whi = sb("Whi", [P, 3, KD, D], F32R)
        Wlo = sb("Wlo", [P, 3, KD, D], F32R)
        Vwh = sb("Vwh", [P, KD, DV], F32R)
        Vwl = sb("Vwl", [P, KD, DV], F32R)
        Mhi = sb("Mhi", [P, KD, D], F32R)
        Mlo = sb("Mlo", [P, KD, D], F32R)
        regPT = cursor[0]
        Ahi = sb("Ahi", [P, KD, CW], F32R)
        Alo = sb("Alo", [P, KD, CW], F32R)
        regH = cursor[0]
        hn = sb("hn", [P, CT, D], F32)
        xc = sb("xc", [P, CT, D], F32)
        regX = cursor[0]
        x1 = [sb(f"x1_{i}", [P, CT, D], F32) for i in range(3)]
        Wraw = sb("Wraw", [P, 4, KD, D], F32, regX)
        adjd = sb("adjd", [P, CT, P], F32)
        Sd = sb("Sd", [P, CT, P], F32)
        Ed = sb("Ed", [P, CT, P], F32)
        PTdh = sb("PTdh", [P, CW], F32R)
        PTdl = sb("PTdl", [P, CW], F32R)
        cursor[0] = max(cursor[0], endR)
        PTh = [sb(f"PTh{i}", [P, CW], F32R, regPT + 4 * CW * i) for i in range(2)]
        PTl = [sb(f"PTl{i}", [P, CW], F32R, regPT + 4 * CW * (2 + i)) for i in range(2)]
        x1t = [sb(f"x1t{i}", [P, D], F32, regH + 4 * D * i) for i in range(2)]
        outb = [sb(f"outb{i}", [P, D], F32, regH + 4 * D * (2 + i)) for i in range(2)]
        Og = sb("Og", [P, D], F32, regX)

        ps = [ctx.enter_context(nc.psum_tensor(f"ps{i}", [P, CW], F32)) for i in range(BANKS)]

        x1_d = nc.dram_tensor("x1_scratch", (N, D), F32, kind="Internal").ap()
        qh_d = nc.dram_tensor("qh_scratch", (P, KD, N), F32, kind="Internal").ap()
        ql_d = nc.dram_tensor("ql_scratch", (P, KD, N), F32, kind="Internal").ap()
        kh_d = nc.dram_tensor("kh_scratch", (P, KD, N), F32, kind="Internal").ap()
        kl_d = nc.dram_tensor("kl_scratch", (P, KD, N), F32, kind="Internal").ap()
        vh_d = nc.dram_tensor("vh_scratch", (P, TILES, D), F32, kind="Internal").ap()
        vl_d = nc.dram_tensor("vl_scratch", (P, TILES, D), F32, kind="Internal").ap()

        ptr_loaded = sem("ptr_loaded")
        bias_loaded = sem("bias_loaded")
        row_first = [sem(f"row_first{i}") for i in range(4)]
        row_loaded = [sem(f"row_loaded{i}") for i in range(4)]
        raw_loaded = [sem(f"raw_loaded{i}") for i in range(4)]
        xg_loaded = [sem(f"xg_loaded{i}") for i in range(2)]
        iota_done = sem("iota_done")
        const_done = sem("const_done")
        agg_zero = sem("agg_zero")
        cmp_done = sem("cmp_done")
        gid_full = sem("gid_full")
        gid_copied = sem("gid_copied")
        gid_copied_act = sem("gid_copied_act")
        bv_zero = sem("bv_zero")
        setup_link = sem("setup_link")
        flag_ready = sem("flag_ready")
        rowsum_done = sem("rowsum_done")
        mask_link = sem("mask_link")
        masked = sem("masked")
        mn_done = sem("mn_done")
        nb_done = sem("nb_done")
        exp_done = sem("exp_done")
        bns_done = sem("bns_done")
        bn_done = sem("bn_done")
        pool_link = sem("pool_link")
        gscale_done = sem("gscale_done")
        gf_done = sem("gf_done")
        g_hi = sem("g_hi")
        g_lo = sem("g_lo")
        split_hi = sem("split_hi")
        split_lo = sem("split_lo")
        units = sem("units")
        acc_done = sem("acc_done")

        w_loaded = sem("w_loaded")
        w_hi = sem("w_hi")
        w_done = sem("w_done")
        m_full = sem("m_full")
        m_hi = sem("m_hi")
        m_lo = sem("m_lo")
        v_link = sem("v_link")
        vec_done = sem("vec_done")
        x_loaded = sem("x_loaded")
        xb_done = sem("xb_done")
        a_hi = sem("a_hi")
        a_lo = sem("a_lo")
        z_full = sem("z_full")
        x1_done = sem("x1_done")
        x1_stored = [sem(f"x1_stored{i}") for i in range(3)]
        bns2_done = sem("bns2_done")
        bn2_done = sem("bn2_done")
        hscale_done = sem("hscale_done")
        h_done = sem("h_done")
        tr_full = sem("tr_full")
        ht_hi = sem("ht_hi")
        ht_lo = sem("ht_lo")
        ring_full = sem("ring_full")
        ring_free = sem("ring_free")
        proj_hi = sem("proj_hi")
        adjd_loaded = sem("adjd_loaded")
        adjp_done = sem("adjp_done")
        nmx_done = sem("nmx_done")
        nm_link = sem("nm_link")
        nm_done = sem("nm_done")
        dd_done = sem("dd_done")
        dexp_done = sem("dexp_done")
        ee_done = sem("ee_done")
        ptd_hi = sem("ptd_hi")
        z_done = sem("z_done")
        coef_link = sem("coef_link")
        coef_done = sem("coef_done")
        spilled = sem("spilled")

        adjr_loaded = [sem(f"adjr_loaded{i}") for i in range(2)]
        x1t_loaded = [sem(f"x1t_loaded{i}") for i in range(2)]
        s_full = sem("s_full")
        s_read = sem("s_read")
        m_done = sem("m_done")
        nmt_link = sem("nmt_link")
        nmt_done = sem("nmt_done")
        ddt_done = sem("ddt_done")
        e_done = sem("e_done")
        eet_done = sem("eet_done")
        pt_full = sem("pt_full")
        pt_hi = sem("pt_hi")
        pt_lo = sem("pt_lo")
        o_full = sem("o_full")
        z_link = sem("z_link")
        zt_link = sem("zt_link")
        zt_done = sem("zt_done")
        coeft_link = sem("coeft_link")
        coeft_done = sem("coeft_done")
        o_read = sem("o_read")
        outt_stored = [sem(f"outt_stored{i}") for i in range(2)]

        g_load = sem("g_load")
        g_score = sem("g_score")
        g_link = sem("g_link")
        g_rlink = sem("g_rlink")
        g_sd = sem("g_sd")
        g_exp = sem("g_exp")
        g_tr = sem("g_tr")
        g_phi = sem("g_phi")
        g_plo = sem("g_plo")
        g_pv = sem("g_pv")
        g_end = sem("g_end")
        g_out = sem("g_out")
        g_fin = sem("g_fin")

        def rows_of(t, n=1):
            return bass.ds(t * P, n * P)

        def tiles_of(a, t):
            return a[bass.ds(t * P, GRP * P), :].rearrange("(b p) d -> p b d", p=P)

        def tile_at(u, q, b):
            return u * 4 + q * 2 + b // 2 + HT * (b % 2)

        def of_group(a, u, q):
            return a[:, :].rearrange("p (h t) -> p t h", h=2)[:, bass.ds(u * 4 + q * 2, GRP // 2), :]

        def quad(a):
            return a.rearrange("p (t h) -> p t h", h=2)

        def ring_plan(fast):
            order = []
            for c in range(CHUNKS + 1):
                diag = fast and 1 <= c <= HCH
                if diag:
                    order.append(("PT", c - 1))
                if c < CHUNKS:
                    order += [("q", c, 0), ("q", c, 1)]
                if diag:
                    order += [("O", c - 1, 0), ("O", c - 1, 1)]
                if c < CHUNKS:
                    order += [("v", c, b) for b in range(CT)]
                if fast and c < HCH:
                    order.append(("S", c))
            return {k: i for i, k in enumerate(order)}

        RING = {True: ring_plan(True), False: ring_plan(False)}

        def mm3(e, o, lh, ll, rh, rl, first, last):
            e.matmul(o, lh, rh, start=first, stop=False)
            e.matmul(o, lh, rl, start=False, stop=False)
            return e.matmul(o, ll, rh, start=False, stop=last)

        unread = {e.engine: sem(f"unread_{k}") for k, e in enumerate((nc.sync, nc.vector, nc.gpsimd))}

        def wait_alone(e, semaphore, value):
            e.wait_ge(semaphore, value)
            e.sem_inc(unread[e.engine], 1)

        block = ctx.enter_context(nc.Block())

        @block.sync
        def _(sp):
            sp.dma_start(ptri[:, :], ptr).then_inc(ptr_loaded, 16)
            def load_x(u, q):
                for h in range(2):
                    rows = x[bass.ds((u * 4 + q * 2) * P + HALF * h, 2 * P), :]
                    sp.dma_start(xg[q % 2][:, h::2, :], rows.rearrange("(b p) d -> p b d", p=P))\
                      .then_inc(xg_loaded[q % 2], 16)

            load_x(0, 0)
            for t in range(4):
                sp.dma_start(row[t][:, :], adj[rows_of(tile_at(0, 0, t)), :]).then_inc(row_first[t], 16)
            for s in range(4):
                sp.dma_start(raw[s][:, :, :], adjT[rows_of(s), :].rearrange("p (t i) -> p t i", t=GRP))\
                  .then_inc(raw_loaded[s], 16)
            load_x(0, 1)
            sp.dma_start(bcols[:, 0, :], bq).then_inc(bias_loaded, 16)
            sp.dma_start(bcols[:, 1, :], bk).then_inc(bias_loaded, 16)
            sp.dma_start(b0row[:, :], b0.rearrange("(a d) -> a d", a=1).partition_broadcast(P))\
              .then_inc(bias_loaded, 16)
            sp.wait_ge(bv_zero, 1)
            sp.dma_start(bvrow[:, 0:D], bv.rearrange("(a d) -> a d", a=1).partition_broadcast(BK))\
              .then_inc(bias_loaded, 16)

            def group(u, par):
                g = u * 2 + par
                if not isinstance(g, int) or g + 2 < GROUPS:
                    wait_alone(sp, gf_done, GRP * g + GRP)
                    load_x(u, par + 2)
                for c in range(CHUNKS):
                    s = CHUNKS * g + c
                    if not isinstance(g, int) or s + 4 < STEPS:
                        wait_alone(sp, split_lo, s * 2 + 2)
                        sp.dma_start(raw[c % 4][:, :, :],
                                     adjT[bass.ds(s * P + 4 * P, P), :].rearrange("p (t i) -> p t i", t=GRP))\
                          .then_inc(raw_loaded[c % 4], 16)
                    if isinstance(g, int) and g == GROUPS - 1 and c == 0:
                        sp.wait_ge(exp_done, TILES)
                        for i, w in enumerate((W0T, Wq, Wk, WvT)):
                            sp.dma_start(Wraw[:, i, :, :], w.rearrange("(k p) o -> p k o", p=P)).then_inc(w_loaded, 16)
                        sp.dma_start(xc[:, :, :], tiles_of(x, 0)).then_inc(x_loaded, 16)

            with sp.Fori(0, 3) as u:
                group(u, 0)
                group(u, 1)
            group(3, 0)
            group(3, 1)

            sp.wait_ge(flag_ready, 1)
            fast_reg = sp.value_load(flag[0:1, 0:1], min_val=0, max_val=1)

            def load_adjd(c):
                for b in range(CT):
                    t = CT * c + b
                    sp.dma_start(adjd[:, b, :], adj[t * P:t * P + P, t * P:t * P + P]).then_inc(adjd_loaded, 16)

            def chunks(fast):
                ring = RING[fast]

                def residual_rows(c):
                    sp.wait_ge(x1_done, CT * (c + 1))
                    if c + 1 < CHUNKS:
                        sp.dma_start(xc[:, :, :], tiles_of(x, CT * (c + 1))).then_inc(x_loaded, 16)
                    if not fast or c >= HCH:
                        sp.dma_start(tiles_of(x1_d, CT * c), x1[c % 3][:, :, :]).then_inc(x1_stored[c % 3], 16)

                residual_rows(0)
                if fast:
                    load_adjd(0)
                residual_rows(1)
                for c in range(CHUNKS):
                    if fast and c in (HCH, CHUNKS - 2):
                        sp.wait_ge(a_lo, c + 2)
                        par = c // (CHUNKS - 2)
                        sp.dma_start(adjr[par][:, :], adj[HALF + P * par:HALF + P * par + P, HALF:N])\
                          .then_inc(adjr_loaded[par], 16)
                    if fast and 1 <= c <= HCH:
                        sp.wait_ge(ring_free, ring[("O", c - 1, 1)] + 1)
                        sp.dma_start(tiles_of(out, CT * (c - 1)), x1[(c - 1) % 3][:, :, :])\
                          .then_inc(x1_stored[(c - 1) % 3], 16)
                    if fast and c < HCH - 1:
                        sp.wait_ge(ring_free, ring[("S", c)] + 1)
                        load_adjd(c + 1)
                    if not fast:
                        sp.wait_ge(ring_free, ring[("v", c, CT - 1)] + 1)
                        k = c % HCH
                        for d_, s_ in ((qh_d, QTh), (ql_d, QTl), (kh_d, KTh), (kl_d, KTl)):
                            sp.dma_start(d_[:, :, CW * c:CW * c + CW], s_[:, :, CW * k:CW * k + CW].bitcast(F32))\
                              .then_inc(spilled, 16)
                        for d_, s_ in ((vh_d, Vh), (vl_d, Vl)):
                            sp.dma_start(d_[:, CT * c:CT * c + CT, :], s_[:, CT * k:CT * k + CT, :].bitcast(F32))\
                              .then_inc(spilled, 16)
                    if c + 2 < CHUNKS:
                        residual_rows(c + 2)
                for i in range(3):
                    sp.wait_ge(x1_stored[i], 16 * len(range(i, CHUNKS, 3)))

            def store_rows(i, par):
                wait_alone(sp, o_read, i + 1)
                sp.dma_start(out[bass.ds(i * P + HALF, P), :], outb[par][:, :]).then_inc(outt_stored[par], 16)

            with sp.If(fast_reg == 1):
                chunks(True)
                sp.wait_ge(tr_full, KD * CHUNKS)
                for par in range(2):
                    sp.dma_start(x1t[par][:, :], x1_d[HALF + P * par:HALF + P * par + P, :])\
                      .then_inc(x1t_loaded[par], 16)
                with sp.Fori(0, HT // 2 - 1) as v:
                    for par in range(2):
                        i = v * 2 + par
                        wait_alone(sp, s_read, i * CT + CT)
                        sp.dma_start(adjr[par][:, :], adj[bass.ds(i * P + 2 * P + HALF, P), HALF:N])\
                          .then_inc(adjr_loaded[par], 16)
                        store_rows(i, par)
                        sp.dma_start(x1t[par][:, :], x1_d[bass.ds(i * P + 2 * P + HALF, P), :])\
                          .then_inc(x1t_loaded[par], 16)
                store_rows(HT - 2, 0)
                store_rows(HT - 1, 1)
                sp.wait_ge(outt_stored[0], 16 * HT // 2)
                sp.wait_ge(outt_stored[1], 16 * HT // 2)
            with sp.Else():
                chunks(False)
                sp.wait_ge(spilled, 16 * 6 * CHUNKS)
                with sp.Fori(0, TILES) as t:
                    with sp.Fori(0, CHUNKS) as c:
                        wait_alone(sp, g_end, t * CHUNKS + c + 1)
                        for d_, s_ in ((qh_d, QTh), (ql_d, QTl)):
                            sp.dma_start(s_[:, :, 0:P].bitcast(F32), d_[:, :, rows_of(t)]).then_inc(g_load, 16)
                        for d_, s_ in ((kh_d, KTh), (kl_d, KTl)):
                            sp.dma_start(s_[:, :, 0:CW].bitcast(F32), d_[:, :, bass.ds(c * CW, CW)])\
                              .then_inc(g_load, 16)
                        for d_, s_ in ((vh_d, Vh), (vl_d, Vl)):
                            sp.dma_start(s_[:, 0:CT, :].bitcast(F32), d_[:, bass.ds(c * CT, CT), :])\
                              .then_inc(g_load, 16)
                        sp.dma_start(adjr[0][:, 0:CW], adj[rows_of(t), bass.ds(c * CW, CW)]).then_inc(g_load, 16)
                        sp.dma_start(x1t[0][:, :], x1_d[rows_of(t), :]).then_inc(g_load, 16)
                    wait_alone(sp, g_out, t + 1)
                    sp.dma_start(out[rows_of(t), :], outb[0][:, :]).then_inc(outt_stored[0], 16)
                    wait_alone(sp, outt_stored[0], t * 16 + 16)
                sp.nop()

        @block.gpsimd
        def _(pool):
            pool.iota(iota[:, :], pattern=[[1, N]], base=0, channel_multiplier=0).then_inc(iota_done, 1)
            pool.memset(ident[:, :], 0.0).then_inc(pool_link, 1)
            pool.memset(mhalf[:, :], -0.5).then_inc(const_done, 1)
            pool.memset(epsdeg[:, :], EPS_DEG).then_inc(const_done, 1)
            pool.memset(off1[:, :], OFF).then_inc(const_done, 1)
            pool.memset(ones33[:, :], 1.0).then_inc(const_done, 1)
            pool.wait_ge(pool_link, 1)
            pool.affine_select(out=ident[:, :], in_=ident[:, :], compare_op=ALU.not_equal, fill=1.0, base=0,
                               pattern=[[-1, P]], channel_multiplier=1).then_inc(const_done, 1)
            pool.memset(bvrow[:, :], 0.0).then_inc(bv_zero, 1)
            pool.memset(aggT[:, :, :], 0.0).then_inc(agg_zero, 1)
            LINKS = 3

            def scales(u, q):
                gs, par = u * 2 + q, q % 2
                n = gs * LINKS + 1
                pool.wait_ge(rowsum_done, gs * GRP + GRP)
                pool.wait_ge(bn_done, gs * GRP + GRP)
                pool.wait_ge(const_done, 5)
                pool.tensor_tensor(quad(pw[:, 0, :]), of_group(deg, u, q), quad(epsdeg[:, :]), ALU.add)
                pool.tensor_scalar(pw[:, 1, :], mv[:, :, 1], EPS_LN, None, ALU.add).then_inc(pool_link, 1)
                wait_alone(pool, pool_link, n + 1)
                pool.tensor_tensor(of_group(dis, u, q), quad(pw[:, 0, :]), quad(mhalf[:, :]), ALU.pow)
                pool.tensor_tensor(pw[:, 2, :], pw[:, 1, :], mhalf[:, :], ALU.pow)
                pool.tensor_scalar(pw[:, 3, :], mv[:, :, 0], -1.0, None, ALU.mult).then_inc(pool_link, 1)
                wait_alone(pool, pool_link, n + 2)
                pool.tensor_tensor(quad(hs[par][:, 0, :]), quad(pw[:, 2, :]), of_group(dis, u, q), ALU.mult)\
                    .then_inc(pool_link, 1)
                pool.wait_ge(pool_link, n + 3)
                pool.tensor_tensor(hs[par][:, 1, :], hs[par][:, 0, :], pw[:, 3, :], ALU.mult)\
                    .then_inc(gscale_done, 1)

            def next_row(r, slot, tile):
                pool.wait_ge(exp_done, r + 1)
                pool.dma_start(row[slot][:, :], adj[bass.ds(tile * P, P), :]).then_inc(row_loaded[slot], 16)

            def greatest_off(r, tile):
                wait_alone(pool, mn_done, r + 1)
                pool.tensor_tensor(nboff[:, bass.ds(tile, 1)], mn[:, bass.ds(tile, 1)], off1[:, :], ALU.mult)\
                    .then_inc(nb_done, 1)

            pool.wait_ge(const_done, 5)
            greatest_off(0, 0)
            greatest_off(1, tile_at(0, 0, 1))
            next_row(0, 0, tile_at(0, 1, 0))
            greatest_off(2, tile_at(0, 0, 2))
            scales(0, 0)
            greatest_off(3, tile_at(0, 0, 3))
            for r in (1, 2):
                next_row(r, r, tile_at(0, 1, r))

            def group(u, par):
                g = u * 2 + par
                for c in range(1, CHUNKS, 2):
                    slot = c // 2
                    greatest_off(GRP * g + 4 + slot, tile_at(u, par + 1, slot))
                    if slot == 0:
                        next_row(GRP * g + 3, 3, tile_at(u, par + 1, 3))
                    elif not isinstance(g, int) or g + 2 < GROUPS:
                        next_row(GRP * g + 3 + slot, slot - 1, tile_at(u, par + 2, slot - 1))
                    if c == 3 and (not isinstance(g, int) or g + 1 < GROUPS):
                        scales(u, par + 1)

            with pool.Fori(0, 3) as u:
                group(u, 0)
                group(u, 1)
            group(3, 0)
            pool.wait_ge(flag_ready, 1)
            fast_reg = pool.value_load(flag[0:1, 0:1], min_val=0, max_val=1)

            def shares(cols, greatest, g_n, link, l_n, done, exps, e_n, zdone):
                wait_alone(pool, greatest, g_n)
                pool.tensor_tensor(dd[:, 0, cols], nm[:, cols], nmr[:, cols], ALU.subtract)
                pool.tensor_tensor(dd[:, 1, cols], nm[:, cols], nboff[:, cols], ALU.subtract).then_inc(done, 1)
                wait_alone(pool, exps, e_n)
                pool.tensor_tensor(zz[:, 0, cols], zz[:, 0, cols], ee[:, 0, cols], ALU.mult)
                pool.tensor_tensor(zz[:, 1, cols], zz[:, 1, cols], ee[:, 1, cols], ALU.mult).then_inc(link, 1)
                wait_alone(pool, link, l_n + 1)
                pool.tensor_tensor(coef[:, cols], zz[:, 0, cols], zz[:, 1, cols], ALU.add).then_inc(zdone, 1)

            def hidden_scales(c):
                n = GROUPS * LINKS + 1 + 2 * c
                pool.wait_ge(bn2_done, CT * (c + 1))
                pool.tensor_scalar(pw[:, 1, :], mv[:, :, 1], EPS_LN, None, ALU.add)
                pool.tensor_scalar(pw[:, 3, :], mv[:, :, 0], -1.0, None, ALU.mult).then_inc(pool_link, 1)
                pool.wait_ge(pool_link, n + 1)
                if c >= 2:
                    pool.wait_ge(h_done, CT * (c - 1))
                pool.tensor_tensor(hs[c % 2][:, 0, :], pw[:, 1, :], mhalf[:, :], ALU.pow).then_inc(pool_link, 1)
                pool.wait_ge(pool_link, n + 2)
                pool.tensor_tensor(hs[c % 2][:, 1, :], hs[c % 2][:, 0, :], pw[:, 3, :], ALU.mult)\
                    .then_inc(hscale_done, 1)
                pool.wait_ge(hscale_done, c + 1)

            def with_b0(c):
                pool.wait_ge(x_loaded, 16 * (c + 1))
                b0wide = b0row[:, :].rearrange("p (a d) -> p a d", a=1).to_broadcast([P, CT, D])
                pool.tensor_tensor(xc[:, :, :], xc[:, :, :], b0wide, ALU.add).then_inc(xb_done, 1)

            def split_agg(c):
                pool.wait_ge(a_hi, c + 1)
                pool.tensor_tensor(Alo[:, :, :], aggT[:, :, CW * c:CW * c + CW], Ahi[:, :, :].bitcast(F32),
                                   ALU.subtract).then_inc(a_lo, 1)

            def chunks(fast):
                with_b0(0)
                split_agg(0)
                hidden_scales(0)
                split_agg(1)
                with_b0(1)
                hidden_scales(1)
                for c in range(CHUNKS):
                    if c < HCH:
                        split_agg(c + 2)
                    if c + 2 < CHUNKS:
                        with_b0(c + 2)
                    if fast and c < HCH:
                        pool.wait_ge(adjd_loaded, 16 * CT * (c + 1))
                        pool.tensor_tensor(adjd[:, :, :], adjd[:, :, :], penn[:, CT * c:CT * c + CT, :], ALU.add)\
                            .then_inc(adjp_done, 1)
                        shares(slice(CT * c, CT * c + CT), nm_done, c + 1, z_link, c, dd_done,
                               ee_done, c + 1, z_done)
                    if c + 2 < CHUNKS:
                        hidden_scales(c + 2)

            pool.wait_ge(bias_loaded, 16 * 4)
            with pool.If(fast_reg == 1):
                chunks(True)
                with pool.Fori(0, HT) as i:
                    shares(bass.ds(i + HT, 1), nmt_done, i + 1, zt_link, i, ddt_done, eet_done, i + 1, zt_done)
                pool.nop()
            with pool.Else():
                chunks(False)
                pool.nop()

        @block.scalar
        def _(act):
            def rowsum(r, slot, tile):
                if isinstance(r, int) and r < 4:
                    act.wait_ge(row_first[slot], 16)
                else:
                    act.wait_ge(row_loaded[slot], r * 4 - slot * 4)
                act.activation(row[slot][:, :], row[slot][:, :], ACT.Copy, accum_out=deg[:, bass.ds(tile, 1)])\
                   .then_inc(rowsum_done, 1)

            def exp_row(r, slot, tile, width):
                act.wait_ge(nb_done, r + 1)
                act.activation(row[slot][:, 0:width], row[slot][:, 0:width], ACT.Exp,
                               bias=nboff[:, bass.ds(tile, 1)], scale=-OFF,
                               accum_out=zz[:, 1, bass.ds(tile, 1)]).then_inc(exp_done, 1)

            def split(s, c, h):
                act.wait_ge(raw_loaded[c % 4], s * 4 - (c % 4) * 4 + 16)
                act.wait_ge(units, s * 3 + 2 * h + 1)
                t = slice(2 * h, 2 * h + 2)
                act.activation(ahi[c % 2][:, t, :], raw[c % 4][:, t, :], ACT.Copy).then_inc(split_hi, 1)

            def features(gs, par):
                act.wait_ge(gscale_done, gs + 1)
                if not isinstance(gs, int) or gs:
                    act.wait_ge(g_lo, gs)
                for b in range(GRP):
                    act.activation(gf[:, b, :], xg[par][:, b, :], ACT.Relu, bias=hs[par][:, 1, b:b + 1],
                                   scale=hs[par][:, 0, b:b + 1]).then_inc(gf_done, 1)
                act.wait_ge(gf_done, gs * GRP + GRP)
                act.activation(Ghi[par][:, :, :], gf[:, :, :], ACT.Copy).then_inc(g_hi, 1)

            def exp_masked(r, slot, tile, upper):
                if upper:
                    with act.If(fast_reg == 1):
                        exp_row(r, slot, tile, HALF)
                    with act.Else():
                        exp_row(r, slot, tile, N)
                else:
                    exp_row(r, slot, tile, N)

            rowsum(0, 0, 0)
            for k in range(BANKS // 2, BANKS):
                act.wait_ge(gid_full, k + 1)
                act.activation(gidrow[:, CW * k:CW * k + CW], ps[k][:, :], ACT.Copy).then_inc(gid_copied_act, 1)
            rowsum(1, 1, tile_at(0, 0, 1))
            act.wait_ge(flag_ready, 1)
            fast_reg = act.value_load(flag[0:1, 0:1], min_val=0, max_val=1)
            rowsum(2, 2, tile_at(0, 0, 2))
            exp_masked(0, 0, 0, False)
            rowsum(3, 3, tile_at(0, 0, 3))
            act.wait_ge(gid_copied, BANKS // 2 + 1)
            split(0, 0, 0)
            split(0, 0, 1)
            exp_masked(1, 1, tile_at(0, 0, 1), True)
            features(0, 0)
            split(1, 1, 0)
            split(1, 1, 1)
            exp_masked(2, 2, tile_at(0, 0, 2), False)
            exp_masked(3, 3, tile_at(0, 0, 3), True)
            rowsum(4, 0, tile_at(0, 1, 0))

            def split_agg(c):
                act.wait_ge(acc_done, UB + 2 * (STEPS - CHUNKS + c) + 2)
                if c:
                    act.wait_ge(z_full, CT * c)
                act.activation(Ahi[:, :, :], aggT[:, :, CW * c:CW * c + CW], ACT.Copy).then_inc(a_hi, 1)

            def hidden(c):
                act.wait_ge(hscale_done, c + 1)
                if c:
                    act.wait_ge(tr_full, KD * c)
                for b in range(CT):
                    act.activation(hn[:, b, :], x1[c % 3][:, b, :], ACT.Relu, bias=hs[c % 2][:, 1, b:b + 1],
                                   scale=hs[c % 2][:, 0, b:b + 1]).then_inc(h_done, 1)

            def group(u, par):
                g = u * 2 + par
                static = isinstance(g, int)
                for c in range(CHUNKS):
                    s = CHUNKS * g + c
                    if not static or s + 2 < STEPS:
                        split(s + 2, (c + 2) % CHUNKS, 0)
                    if c == 6 and (not static or g + 1 < GROUPS):
                        features(g + 1, 1 - par)
                    r = GRP * g + 4 + c // 2
                    slot = c // 2
                    if c % 2 and (not static or s + 2 < STEPS):
                        split(s + 2, (c + 2) % CHUNKS, 1)
                    if c % 2 == 0:
                        if not static or r + 1 < TILES:
                            rowsum(r + 1, (slot + 1) % 4,
                                   tile_at(u, par + 2, 0) if c == 6 else tile_at(u, par + 1, slot + 1))
                    elif not static or r < TILES:
                        exp_masked(r, slot, tile_at(u, par + 1, slot), slot % 2 == 1)
                    if c % 2 == 0 and (not static or s + 2 < STEPS):
                        split(s + 2, (c + 2) % CHUNKS, 1)
                    if static and g == GROUPS - 1:
                        if c == 1:
                            for i in range(4):
                                act.wait_ge(w_loaded, 64)
                                act.activation(Whi[:, i, :, :] if i < 3 else Vwh[:, :, 0:D], Wraw[:, i, :, :],
                                               ACT.Copy, scale=1.0 / 32 if i == 1 else 1.0).then_inc(w_hi, 1)
                            act.wait_ge(bias_loaded, 16 * 4)
                            act.activation(bvr[:, :], bvrow[:, :], ACT.Copy).then_inc(w_hi, 1)
                        if c == 3:
                            split_agg(0)
                        if c == 4:
                            act.wait_ge(m_full, 1)
                            act.activation(Mhi[:, :, :].rearrange("p k d -> p (k d)"), ps[2][:, :], ACT.Copy)\
                               .then_inc(m_hi, 1)
                        if c == 7:
                            split_agg(1)
                            hidden(0)

            with act.Fori(0, 3) as u:
                group(u, 0)
                group(u, 1)
            group(3, 0)
            group(3, 1)

            def attend(i, par):
                act.wait_ge(m_done, i + 1)
                act.activation(SE[par][:, :], SE[par][:, :], ACT.Exp, bias=nmx[:, bass.ds(i + HT, 1)],
                               accum_out=zz[:, 0, bass.ds(i + HT, 1)]).then_inc(e_done, 1)

            def attend_shares(i):
                act.wait_ge(ddt_done, i + 1)
                act.activation(ee[:, :, bass.ds(i + HT, 1)], dd[:, :, bass.ds(i + HT, 1)], ACT.Exp)\
                   .then_inc(eet_done, 1)

            def split_hT(c, ring, fast):
                k = c % HCH
                if c >= HCH:
                    if fast:
                        act.wait_ge(ring_full, ring[("S", c - HCH)] + 1)
                    else:
                        act.wait_ge(spilled, 16 * 6 * (c - HCH + 1))
                for kk in range(KD):
                    act.wait_ge(tr_full, KD * c + kk + 1)
                    act.activation(KTh[:, kk, CW * k:CW * k + CW], ps[2 + kk][:, :], ACT.Copy).then_inc(ht_hi, 1)

            def chunks(fast):
                ring = RING[fast]
                split_hT(0, ring, fast)
                for c in range(CHUNKS):
                    diag = fast and 1 <= c <= HCH
                    k = c % HCH
                    if diag:
                        n = ring[("PT", c - 1)]
                        act.wait_ge(ring_full, n + 1)
                        if c > 1:
                            act.wait_ge(ring_full, ring[("O", c - 2, 1)] + 1)
                        act.activation(PTdh[:, :], ps[4 + n % 4][:, :], ACT.Copy).then_inc(ptd_hi, 1)
                    if not fast and c >= HCH:
                        act.wait_ge(spilled, 16 * 6 * (c - HCH + 1))
                    for o in range(KD):
                        n = ring[("q", c, o)]
                        act.wait_ge(ring_full, n + 1)
                        act.activation(QTh[:, o, CW * k:CW * k + CW], ps[4 + n % 4][:, :], ACT.Identity,
                                       bias=bqk[:, o:o + 1]).then_inc(proj_hi, 1)
                    if c + 2 < CHUNKS:
                        split_agg(c + 2)
                    ahead = CT if c == 0 else CT // 2 if c >= HCH else 0
                    if fast and c >= HCH:
                        act.wait_ge(ring_full, ring[("O", c - HCH, 1)] + 1)
                    for b in range(CT):
                        if b == ahead and c + 1 < CHUNKS:
                            hidden(c + 1)
                        if b == ahead and fast and c == CHUNKS - 1:
                            attend(0, 0)
                        n = ring[("v", c, b)]
                        act.wait_ge(ring_full, n + 1)
                        act.activation(Vh[:, CT * k + b, :], ps[4 + n % 4][:, 0:D], ACT.Copy).then_inc(proj_hi, 1)
                    if ahead == CT:
                        hidden(c + 1)
                    if fast and c == CHUNKS - 1:
                        attend_shares(0)
                    if c + 1 < CHUNKS:
                        split_hT(c + 1, ring, fast)
                    if fast and c < HCH:
                        if c:
                            act.wait_ge(ring_full, ring[("PT", c - 1)] + 1)
                        act.wait_ge(nmx_done, c + 1)
                        for b in range(CT):
                            t = CT * c + b
                            act.activation(Ed[:, b, :], Sd[:, b, :], ACT.Exp, bias=nmx[:, t:t + 1],
                                           accum_out=zz[:, 0, t:t + 1]).then_inc(dexp_done, 1)
                        act.wait_ge(dd_done, c + 1)
                        act.activation(ee[:, :, CT * c:CT * c + CT], dd[:, :, CT * c:CT * c + CT], ACT.Exp)\
                           .then_inc(ee_done, 1)

            def turned(i, q):
                act.wait_ge(pt_full, i * 4 + q + 1)
                act.activation(PTh[q % 2][:, :], ps[4 + q % 2][:, :], ACT.Copy).then_inc(pt_hi, 1)

            with act.If(fast_reg == 1):
                chunks(True)

                def tile(i, par):
                    for q in range(4):
                        turned(i, q)
                    if not isinstance(i, int) or i + 1 < HT:
                        attend(i + 1, 1 - par)
                        attend_shares(i + 1)

                with act.Fori(0, HT // 2 - 1) as v:
                    tile(v * 2, 0)
                    tile(v * 2 + 1, 1)
                tile(HT - 2, 0)
                tile(HT - 1, 1)
                act.nop()
            with act.Else():
                chunks(False)
                with act.Fori(0, TILES) as t:
                    with act.Fori(0, CHUNKS) as c:
                        n = t * CHUNKS + c
                        act.wait_ge(g_sd, n + 1)
                        act.activation(SE[1][:, 0:CW], SE[0][:, 0:CW], ACT.Exp, bias=nm[:, 0:1],
                                       accum_out=zz[:, 0, 0:1]).then_inc(g_exp, 1)
                        act.activation(ee[:, 0, 0:1], dd[:, 0, 0:1], ACT.Exp).then_inc(g_exp, 1)
                        act.wait_ge(g_tr, n + 1)
                        act.activation(PTh[0][:, :], ps[4][:, :], ACT.Copy).then_inc(g_phi, 1)
                act.nop()

        @block.vector
        def _(dve):
            dve.wait_ge(ptr_loaded, 16)
            dve.tensor_copy(ptrf[:, :], ptri[:, :]).then_inc(setup_link, 1)
            for b in range(GRP):
                dve.wait_ge(xg_loaded[0], 32)
                dve.bn_stats(bnst[:, b, :], xg[0][:, b, :]).then_inc(bns_done, 1)
            for b in range(GRP):
                dve.wait_ge(bns_done, b + 1)
                dve.bn_aggr(mv[:, b, :], bnst[:, b, :]).then_inc(bn_done, 1)
            dve.wait_ge(setup_link, 1)
            dve.wait_ge(iota_done, 1)
            dve.tensor_scalar(cmp[:, :], iota[:, :], ptrf[:, 0:1], None, ALU.is_ge).then_inc(cmp_done, 1)
            for k in range(BANKS // 2):
                dve.wait_ge(gid_full, k + 1)
                dve.tensor_copy(gidrow[:, CW * k:CW * k + CW], ps[k][:, :]).then_inc(gid_copied, 1)
            dve.wait_ge(gid_full, BANKS + 1)
            dve.tensor_copy(gidcol[:, :], ps[0][:, 0:TILES]).then_inc(gid_copied, 1)
            dve.wait_ge(gid_copied, BANKS // 2 + 1)
            for t in range(HT):
                dve.tensor_scalar(penn[:, t, :], gidrow[:, P * t:P * t + P], gidcol[:, t:t + 1], -BIG / 2,
                                  ALU.not_equal, ALU.mult).then_inc(setup_link, 1)
            dve.wait_ge(gid_copied_act, BANKS // 2)
            edges = gidrow[0:1, 0:HALF + P].rearrange("p (t q) -> p t q", q=P)
            dve.tensor_tensor(flagw[0:1, 0:HT], edges[:, 1:HT + 1, 0], edges[:, 0:HT, P - 1], ALU.is_gt)\
               .then_inc(setup_link, 1)
            dve.tensor_tensor(flagw[0:1, HT:HT + 1], gidrow[0:1, HALF:HALF + 1], gidrow[0:1, N - 1:N], ALU.is_equal)\
               .then_inc(setup_link, 1)
            dve.wait_ge(setup_link, HT + 3)
            dve.tensor_reduce(flag[0:1, 0:1], flagw[0:1, 0:HT + 1], AX_X, ALU.min).then_inc(flag_ready, 1)
            dve.wait_ge(flag_ready, 1)
            fast_reg = dve.value_load(flag[0:1, 0:1], min_val=0, max_val=1)

            def mask_rows(r, slot, tile):
                for k in range(4):
                    m = r * 8 + 2 * k
                    cols = slice(1024 * k, 1024 * k + 1024)
                    dve.tensor_scalar(masktmp[:, :], gidrow[:, cols], gidcol[:, bass.ds(tile, 1)], BIG,
                                      ALU.is_equal, ALU.mult).then_inc(mask_link, 1)
                    dve.wait_ge(mask_link, m + 1)
                    dve.tensor_tensor(row[slot][:, cols], row[slot][:, cols], masktmp[:, :], ALU.add)\
                       .then_inc(mask_link, 1)
                    dve.wait_ge(mask_link, m + 2)
                dve.tensor_reduce(mn[:, bass.ds(tile, 1)], row[slot][:, :], AX_X, ALU.min).then_inc(mn_done, 1)

            def mask_tile(slot, tile):
                own = row[slot][:, bass.ds(tile * P, P)]
                dve.scalar_tensor_tensor(out=own, in0=penn[:, bass.ds(tile, 1), :].rearrange("p a j -> p (a j)"),
                                         scalar=BIG / 2, in1=own, op0=ALU.add, op1=ALU.add).then_inc(masked, 1)
                dve.wait_ge(masked, tile + 1)
                dve.tensor_reduce(mn[:, bass.ds(tile, 1)], row[slot][:, :], AX_X, ALU.min).then_inc(mn_done, 1)

            def least(r, slot, tile, upper):
                wait_alone(dve, rowsum_done, r + 1)
                with dve.If(fast_reg == 1):
                    if upper:
                        dve.tensor_reduce(mn[:, bass.ds(tile, 1)], row[slot][:, 0:HALF], AX_X, ALU.min)\
                           .then_inc(mn_done, 1)
                    else:
                        mask_tile(slot, tile)
                with dve.Else():
                    mask_rows(r, slot, tile)

            def moments(gs, par, bs):
                xl = (gs // 2) * 32 + 32 if isinstance(gs, int) else (gs - par) * 16 + 32
                dve.wait_ge(xg_loaded[par], xl)
                if bs[0] == 0 and not (isinstance(gs, int) and gs == 0):
                    dve.wait_ge(gscale_done, gs)
                for b in bs:
                    dve.bn_stats(bnst[:, b, :], xg[par][:, b, :]).then_inc(bns_done, 1)
                for b in bs:
                    wait_alone(dve, bns_done, gs * GRP + b + 1)
                    dve.bn_aggr(mv[:, b, :], bnst[:, b, :]).then_inc(bn_done, 1)

            def split(s, c, h):
                dve.wait_ge(split_hi, s * 2 + h + 1)
                t = slice(2 * h, 2 * h + 2)
                dve.tensor_tensor(alo[c % 2][:, t, :], raw[c % 4][:, t, :], ahi[c % 2][:, t, :].bitcast(F32),
                                  ALU.subtract).then_inc(split_lo, 1)

            def features(gs, par):
                dve.wait_ge(g_hi, gs + 1)
                dve.tensor_tensor(Glo[par][:, :, :], gf[:, :, :], Ghi[par][:, :, :].bitcast(F32), ALU.subtract)\
                   .then_inc(g_lo, 1)

            for r in range(GRP):
                least(r, r, tile_at(0, 0, r), r % 2 == 1)
            split(0, 0, 0)
            split(0, 0, 1)
            features(0, 0)
            split(1, 1, 0)
            split(1, 1, 1)
            dve.wait_ge(agg_zero, 1)
            dve.sem_inc(acc_done, UB)

            def split_weights():
                for i in range(4):
                    dve.wait_ge(w_hi, i + 1)
                    dve.scalar_tensor_tensor(out=Wlo[:, i, :, :] if i < 3 else Vwl[:, :, 0:D], in0=Wraw[:, i, :, :],
                                             scalar=1.0 / 32 if i == 1 else 1.0,
                                             in1=(Whi[:, i, :, :] if i < 3 else Vwh[:, :, 0:D]).bitcast(F32),
                                             op0=ALU.mult, op1=ALU.subtract).then_inc(w_done, 1)
                dve.tensor_tensor(pickc[:, :], ident[0:BK, 0:1], ident[0:BK, BK - 1:BK], ALU.add).then_inc(w_done, 1)
                dve.wait_ge(w_done, 5)
                dve.tensor_scalar(pick[:, :], ident[0:BK, :], 0.0, pickc[:, 0:1], ALU.mult, ALU.add)\
                   .then_inc(w_done, 1)
                dve.wait_ge(w_hi, 5)
                dve.tensor_tensor(bvr[BK - 1:BK, :], bvrow[BK - 1:BK, :], bvr[BK - 1:BK, :].bitcast(F32),
                                  ALU.subtract).then_inc(w_done, 1)
                for k in range(KD):
                    dve.tensor_scalar(bqwide[:, k, :], ident[:, :], 0.0, bcols[:, 0, k:k + 1], ALU.mult, ALU.add)\
                       .then_inc(w_done, 1)

            def split_M():
                dve.wait_ge(m_hi, 1)
                dve.tensor_tensor(Mlo[:, :, :].rearrange("p k d -> p (k d)"), ps[2][:, :],
                                  Mhi[:, :, :].rearrange("p k d -> p (k d)").bitcast(F32), ALU.subtract)\
                   .then_inc(m_lo, 1)
                dve.wait_ge(m_full, 2)
                dve.tensor_scalar(bqk[:, :], ps[3][:, 0:KD], 1.0 / 32, None, ALU.mult)
                dve.tensor_scalar(c0[:, :], ps[3][:, 2 * KD:2 * KD + 1], 1.0 / 16, None, ALU.mult)
                dve.tensor_scalar(uf[:, :], ps[3][:, KD:2 * KD], 1.0 / 16, None, ALU.mult).then_inc(v_link, 1)
                dve.wait_ge(v_link, 1)
                for i in range(DV - D):
                    dve.tensor_copy(Vwh[:, :, D + i], uf[:, :]).then_inc(v_link, 1)
                for i in range(DV - D):
                    dve.wait_ge(v_link, 1 + DV - D)
                    dve.tensor_tensor(Vwl[:, :, D + i], uf[:, :], Vwh[:, :, D + i].bitcast(F32), ALU.subtract)\
                       .then_inc(vec_done, 1)

            def residual(c):
                dve.wait_ge(xb_done, c + 1)
                if c >= 3:
                    dve.wait_ge(x1_stored[c % 3], 16 * (c // 3))
                for b in range(CT):
                    t = CT * c + b
                    dve.wait_ge(z_full, t + 2 - b % 2)
                    dve.scalar_tensor_tensor(out=x1[c % 3][:, b, :], in0=ps[b // 2][:, D * (b % 2):D * (b % 2) + D],
                                             scalar=dis[:, t:t + 1], in1=xc[:, b, :], op0=ALU.mult, op1=ALU.add)\
                       .then_inc(x1_done, 1)
                if c:
                    dve.wait_ge(hscale_done, c)
                for b in range(CT):
                    dve.wait_ge(x1_done, CT * c + b + 1)
                    dve.bn_stats(bnst[:, b, :], x1[c % 3][:, b, :]).then_inc(bns2_done, 1)
                for b in range(CT):
                    dve.wait_ge(bns2_done, CT * c + b + 1)
                    dve.bn_aggr(mv[:, b, :], bnst[:, b, :]).then_inc(bn2_done, 1)

            def group(u, par):
                g = u * 2 + par
                static = isinstance(g, int)
                for c in range(CHUNKS):
                    s = CHUNKS * g + c
                    if not static or s + 2 < STEPS:
                        split(s + 2, (c + 2) % CHUNKS, 0)
                    if c == 6 and (not static or g + 1 < GROUPS):
                        features(g + 1, 1 - par)
                    if c % 2 == 0 and (not static or g + 1 < GROUPS):
                        least(GRP * g + 4 + c // 2, c // 2, tile_at(u, par + 1, c // 2), c // 2 % 2 == 1)
                    if c in (1, 3) and (not static or g + 1 < GROUPS):
                        moments(g + 1, 1 - par, (c - 1, c))
                    for k in range(KD):
                        dve.wait_ge(units, s * 3 + 8 + k)
                        dst = aggT[:, k, CW * c:CW * c + CW]
                        dve.tensor_tensor(dst, dst, ps[UB + (2 * c + k) % UB][:, :], ALU.add).then_inc(acc_done, 1)
                    if not static or s + 2 < STEPS:
                        split(s + 2, (c + 2) % CHUNKS, 1)
                    if static and g == GROUPS - 1:
                        if c == 1:
                            split_weights()
                        if c == 4:
                            split_M()
                        if c == 5:
                            residual(0)

            with dve.Fori(0, 3) as u:
                group(u, 0)
                group(u, 1)
            group(3, 0)
            group(3, 1)

            def split_hT(c):
                k = c % HCH
                for kk in range(KD):
                    dve.wait_ge(ht_hi, KD * c + kk + 1)
                    dve.tensor_tensor(KTl[:, kk, CW * k:CW * k + CW], ps[2 + kk][:, :],
                                      KTh[:, kk, CW * k:CW * k + CW].bitcast(F32), ALU.subtract).then_inc(ht_lo, 1)

            def row_greatest(cols, nmx_ready, n, link, done):
                dve.wait_ge(nmx_ready, n)
                dve.tensor_tensor(nmr[:, cols], nmx[:, cols], rr[:, cols], ALU.subtract).then_inc(link, 1)
                dve.wait_ge(link, n)
                dve.tensor_tensor(nm[:, cols], nmr[:, cols], nboff[:, cols], ALU.min).then_inc(done, 1)

            def row_coefs(cols, zd, z_n, link, l_n, done):
                wait_alone(dve, zd, z_n)
                dve.reciprocal(coef[:, cols], coef[:, cols]).then_inc(link, 1)
                dve.wait_ge(link, l_n)
                dve.tensor_tensor(coef[:, cols], coef[:, cols], ee[:, 0, cols], ALU.mult).then_inc(done, 1)
                dve.wait_ge(done, l_n)

            def score_bank(i, par, jc):
                if jc == 0:
                    dve.wait_ge(adjr_loaded[par], i * 8 - 8 * par + 16)
                wait_alone(dve, s_full, i * 4 + jc + 1)
                dve.tensor_tensor_reduce(
                    out=SE[par][:, CW * jc:CW * jc + CW], in0=ps[jc][:, :], in1=adjr[par][:, CW * jc:CW * jc + CW],
                    scale=2.0, scalar=-3e38, op0=ALU.add, op1=ALU.max, accum_out=mx4t[:, jc:jc + 1])\
                   .then_inc(s_read, 1)

            def greatest(i):
                t = bass.ds(i + HT, 1)
                dve.wait_ge(s_read, i * 4 + 4)
                dve.tensor_reduce(nmx[:, t], mx4t[:, :], AX_X, ALU.max, negate=True).then_inc(m_done, 1)
                row_greatest(t, m_done, i + 1, nmt_link, nmt_done)

            def chunks(fast):
                ring = RING[fast]
                split_hT(0)
                residual(1)
                for c in range(CHUNKS):
                    diag = fast and 1 <= c <= HCH
                    k = c % HCH
                    if diag:
                        n = ring[("PT", c - 1)]
                        dve.wait_ge(ptd_hi, c)
                        dve.tensor_tensor(PTdl[:, :], ps[4 + n % 4][:, :], PTdh[:, :].bitcast(F32), ALU.subtract)\
                           .then_inc(ring_free, 1)
                    for o in range(KD):
                        n = ring[("q", c, o)]
                        dve.wait_ge(proj_hi, (KD + CT) * c + o + 1)
                        dve.scalar_tensor_tensor(
                            out=QTl[:, o, CW * k:CW * k + CW], in0=ps[4 + n % 4][:, :],
                            scalar=bqk[:, o:o + 1], in1=QTh[:, o, CW * k:CW * k + CW].bitcast(F32),
                            op0=ALU.add, op1=ALU.subtract).then_inc(ring_free, 1)
                    if fast and c == CHUNKS - 1:
                        for jc in range(4):
                            score_bank(0, 0, jc)
                        greatest(0)
                    if diag:
                        row_coefs(slice(CT * (c - 1), CT * c), z_done, c, coef_link, c, coef_done)
                        for b in range(CT):
                            t = CT * (c - 1) + b
                            n = ring[("O", c - 1, b // 2)]
                            dve.wait_ge(ring_full, n + 1)
                            xo = x1[(c - 1) % 3][:, b, :]
                            last = dve.scalar_tensor_tensor(
                                out=xo, in0=ps[4 + n % 4][:, D * (b % 2):D * (b % 2) + D], scalar=coef[:, t:t + 1],
                                in1=xo, op0=ALU.mult, op1=ALU.add)
                            if b % 2:
                                last.then_inc(ring_free, 1)
                    if HCH <= c and c + 2 < CHUNKS:
                        dve.wait_ge(a_hi, c + 3)
                        dve.tensor_tensor(Alo[:, :, :], aggT[:, :, CW * (c + 2):CW * (c + 3)],
                                          Ahi[:, :, :].bitcast(F32), ALU.subtract).then_inc(a_lo, 1)
                    for b in range(CT):
                        n = ring[("v", c, b)]
                        dve.wait_ge(proj_hi, (KD + CT) * c + KD + b + 1)
                        dve.tensor_tensor(Vl[:, CT * k + b, :], ps[4 + n % 4][:, 0:D],
                                          Vh[:, CT * k + b, :].bitcast(F32), ALU.subtract)
                        dve.tensor_scalar(rr[:, CT * c + b:CT * c + b + 1], ps[4 + n % 4][:, D:D + 1], c0[:, 0:1],
                                          None, ALU.add).then_inc(ring_free, 1)
                    if fast and c < HCH:
                        n = ring[("S", c)]
                        dve.wait_ge(ring_full, n + 1)
                        dve.wait_ge(adjp_done, c + 1)
                        if c:
                            dve.wait_ge(dexp_done, CT * c)
                        for b in range(CT):
                            last = dve.tensor_tensor_reduce(
                                out=Sd[:, b, :], in0=ps[4 + n % 4][:, P * b:P * b + P], in1=adjd[:, b, :],
                                scale=2.0, scalar=-3e38, op0=ALU.add, op1=ALU.max, accum_out=mx4[:, b:b + 1])
                        last.then_inc(ring_free, 1)
                        dve.wait_ge(ring_free, n + 1)
                        dve.tensor_scalar(nmx[:, CT * c:CT * c + CT], mx4[:, :], -1.0, None, ALU.mult)\
                           .then_inc(nmx_done, 1)
                        row_greatest(slice(CT * c, CT * c + CT), nmx_done, c + 1, nm_link, nm_done)
                    if c + 1 < CHUNKS:
                        split_hT(c + 1)
                    if c + 2 < CHUNKS:
                        residual(c + 2)

            def turned(i, q):
                dve.wait_ge(pt_hi, i * 4 + q + 1)
                dve.tensor_tensor(PTl[q % 2][:, :], ps[4 + q % 2][:, :], PTh[q % 2][:, :].bitcast(F32), ALU.subtract)\
                   .then_inc(pt_lo, 1)

            def finish(i, par):
                t = bass.ds(i + HT, 1)
                row_coefs(t, zt_done, i + 1, coeft_link, i + 1, coeft_done)
                dve.wait_ge(x1t_loaded[par], i * 8 - 8 * par + 16)
                dve.wait_ge(o_full, i + 1)
                if not isinstance(i, int) or i >= 2:
                    dve.wait_ge(outt_stored[par], i * 8 - 8 * par)
                dve.scalar_tensor_tensor(out=outb[par][:, :], in0=ps[6 + par][:, 0:D], scalar=coef[:, t],
                                         in1=x1t[par][:, :], op0=ALU.mult, op1=ALU.add).then_inc(o_read, 1)

            with dve.If(fast_reg == 1):
                chunks(True)

                def tile(i, par):
                    for q in range(4):
                        if q == 3:
                            turned(i, q)
                        if not isinstance(i, int) or i + 1 < HT:
                            score_bank(i + 1, 1 - par, q)
                        if q < 3:
                            turned(i, q)
                    if not isinstance(i, int) or i + 1 < HT:
                        greatest(i + 1)
                    finish(i, par)

                tile(0, 0)
                tile(1, 1)
                with dve.Fori(1, HT // 2 - 1) as v:
                    tile(v * 2, 0)
                    tile(v * 2 + 1, 1)
                tile(HT - 2, 0)
                tile(HT - 1, 1)
                dve.nop()
            with dve.Else():
                chunks(False)
                dve.wait_ge(x1_stored[0], 16 * len(range(0, CHUNKS, 3)))
                dve.sem_inc(g_end, 1)
                with dve.Fori(0, TILES) as t:
                    col = bass.ds(t, 1)
                    dve.tensor_copy(nm[:, 0:1], nboff[:, col]).then_inc(g_link, 1)
                    dve.tensor_copy(zz[:, 1, 0:1], zz[:, 1, col]).then_inc(g_link, 1)
                    dve.memset(Og[:, :], 0.0).then_inc(g_link, 1)
                    with dve.Fori(0, CHUNKS) as c:
                        n = t * CHUNKS + c
                        L = t * (3 + 8 * CHUNKS) + c * 8 + 3
                        dve.wait_ge(g_link, L)
                        dve.wait_ge(g_load, n * 128 + 128)
                        dve.wait_ge(g_score, n + 1)
                        dve.tensor_tensor(SE[0][:, 0:CW], ps[0][:, :], adjr[0][:, 0:CW], ALU.add)
                        dve.tensor_scalar(SE[1][:, CW:2 * CW], gidrow[:, bass.ds(c * CW, CW)], gidcol[:, col], -BIG,
                                          ALU.not_equal, ALU.mult).then_inc(g_link, 1)
                        dve.wait_ge(g_link, L + 1)
                        dve.scalar_tensor_tensor(out=SE[0][:, 0:CW], in0=SE[0][:, 0:CW], scalar=2.0,
                                                 in1=SE[1][:, CW:2 * CW], op0=ALU.mult, op1=ALU.add).then_inc(g_link, 1)
                        dve.wait_ge(g_link, L + 2)
                        dve.tensor_scalar(SE[0][:, 0:CW], SE[0][:, 0:CW], rr[:, col], None, ALU.add)\
                           .then_inc(g_rlink, 1)
                        dve.wait_ge(g_rlink, n + 1)
                        dve.tensor_reduce(nmx[:, 0:1], SE[0][:, 0:CW], AX_X, ALU.max, negate=True).then_inc(g_link, 1)
                        dve.wait_ge(g_link, L + 3)
                        dve.tensor_tensor(nmx[:, 1:2], nmx[:, 0:1], nm[:, 0:1], ALU.min).then_inc(g_link, 1)
                        dve.wait_ge(g_link, L + 4)
                        dve.tensor_tensor(dd[:, 0, 0:1], nmx[:, 1:2], nm[:, 0:1], ALU.subtract).then_inc(g_link, 1)
                        dve.wait_ge(g_link, L + 5)
                        dve.tensor_copy(nm[:, 0:1], nmx[:, 1:2]).then_inc(g_sd, 1)
                        dve.wait_ge(g_exp, n * 2 + 2)
                        dve.scalar_tensor_tensor(out=zz[:, 1, 0:1], in0=zz[:, 1, 0:1], scalar=ee[:, 0, 0:1],
                                                 in1=zz[:, 0, 0:1], op0=ALU.mult, op1=ALU.add).then_inc(g_link, 1)
                        dve.wait_ge(g_phi, n + 1)
                        dve.tensor_tensor(PTl[0][:, :], ps[4][:, :], PTh[0][:, :].bitcast(F32), ALU.subtract)\
                           .then_inc(g_plo, 1)
                        dve.wait_ge(g_pv, n + 1)
                        dve.scalar_tensor_tensor(out=Og[:, :], in0=Og[:, :], scalar=ee[:, 0, 0:1],
                                                 in1=ps[6][:, 0:D], op0=ALU.mult, op1=ALU.add).then_inc(g_link, 1)
                        dve.wait_ge(g_link, L + 7)
                        dve.tensor_copy(coef[:, 0:1], zz[:, 1, 0:1]).then_inc(g_link, 1)
                        wait_alone(dve, g_link, L + 8)
                        with dve.If(c < CHUNKS - 1):
                            dve.sem_inc(g_end, 1)
                        with dve.Else():
                            dve.nop()
                        dve.nop()
                    dve.reciprocal(coef[:, 0:1], coef[:, 0:1]).then_inc(g_fin, 1)
                    dve.wait_ge(g_fin, t + 1)
                    dve.scalar_tensor_tensor(out=outb[0][:, :], in0=Og[:, :], scalar=coef[:, 0:1],
                                             in1=x1t[0][:, :], op0=ALU.mult, op1=ALU.add).then_inc(g_out, 1)
                    dve.wait_ge(g_out, t + 1)
                    dve.sem_inc(g_end, 1)
                dve.nop()

        @block.tensor
        def _(pe):
            pe.wait_ge(const_done, 5)
            pe.wait_ge(cmp_done, 1)
            for k in range(BANKS):
                pe.matmul(ps[k][:, :], ones33[:, :], cmp[:, CW * k:CW * k + CW], start=True, stop=True)\
                  .then_inc(gid_full, 1)
            pe.wait_ge(gid_copied, 1)
            for t in range(TILES):
                last = pe.matmul(ps[0][:, t:t + 1], cmp[:, P * t:P * t + P], ones33[:, 0:1], start=True, stop=True)
            last.then_inc(gid_full, 1)
            pe.wait_ge(gid_copied, BANKS // 2 + 1)
            pe.wait_ge(gid_copied_act, BANKS // 2)
            pe.sem_inc(units, 6)
            pe.wait_ge(flag_ready, 1)
            fast_reg = pe.value_load(flag[0:1, 0:1], min_val=0, max_val=1)

            def group(u, par):
                g = u * 2 + par
                pe.wait_ge(g_lo, g + 1)
                for c in range(CHUNKS):
                    s = CHUNKS * g + c
                    for h in range(2):
                        pe.wait_ge(split_lo, s * 2 + h + 1)
                        for k in range(KD):
                            if h == 0:
                                pe.wait_ge(acc_done, s * 2 + k + 1)
                            for t in (2 * h, 2 * h + 1):
                                last = mm3(pe, ps[UB + (2 * c + k) % UB][:, :],
                                           Ghi[par][:, t, P * k:P * k + P], Glo[par][:, t, P * k:P * k + P],
                                           ahi[c % 2][:, t, :], alo[c % 2][:, t, :], t == 0, t == GRP - 1)
                            if h or k:
                                last.then_inc(units, 1)
                    if isinstance(g, int) and g == GROUPS - 1:
                        if c == 3:
                            fold()
                        if c == 5:
                            residual(0)

            def fold():
                pe.wait_ge(w_done, 9)
                for k in range(KD):
                    for o in range(KD):
                        last = mm3(pe, ps[2][:, D * k:D * k + D], Whi[:, 1, o, P * k:P * k + P],
                                   Wlo[:, 1, o, P * k:P * k + P], Whi[:, 2, o, :], Wlo[:, 2, o, :], o == 0, o == KD - 1)
                last.then_inc(m_full, 1)
                for j, i, k in ((0, 2, 0), (0, 2, 1), (1, 1, 0), (1, 1, 1)):
                    for o in range(KD):
                        pe.matmul(ps[3][:, KD * j + k:KD * j + k + 1], Wraw[:, i, o, P * k:P * k + P],
                                  bcols[:, j, o:o + 1], start=o == 0, stop=o == KD - 1)
                for o in range(KD):
                    last = pe.matmul(ps[3][:, 2 * KD:2 * KD + 1], bqwide[:, o, :], bcols[:, 1, o:o + 1],
                                     start=o == 0, stop=o == KD - 1)
                last.then_inc(m_full, 1)

            def residual(c, tiles=range(CT)):
                pe.wait_ge(a_lo, c + 1)
                for b in tiles:
                    if c:
                        pe.wait_ge(x1_done, CT * (c - 1) + b + 2 - b % 2)
                    for k in range(KD):
                        last = mm3(pe, ps[b // 2][:, D * (b % 2):D * (b % 2) + D],
                                   Ahi[:, k, P * b:P * b + P], Alo[:, k, P * b:P * b + P],
                                   Whi[:, 0, k, :], Wlo[:, 0, k, :], k == 0, k == KD - 1)
                    last.then_inc(z_full, 1)

            def turn(c):
                pe.wait_ge(h_done, CT * (c + 1))
                if c:
                    pe.wait_ge(ht_lo, KD * c)
                for k in range(KD):
                    for b in range(CT):
                        last = pe.transpose(ps[2 + k][:, P * b:P * b + P], hn[:, b, P * k:P * k + P], ident[:, :])
                    last.then_inc(tr_full, 1)

            with pe.Fori(0, 3) as u:
                group(u, 0)
                group(u, 1)
            group(3, 0)
            group(3, 1)

            def score_bank(i, jc):
                if i:
                    pe.wait_ge(s_read, 4 * (i - 1) + jc + 1)
                for oh in range(KD):
                    w, j = slice(P * i, P * i + P), slice(CW * jc, CW * jc + CW)
                    last = mm3(pe, ps[jc][:, :], QTh[:, oh, w], QTl[:, oh, w], KTh[:, oh, j], KTl[:, oh, j],
                               oh == 0, oh == KD - 1)
                last.then_inc(s_full, 1)

            def chunks(fast):
                ring = RING[fast]

                def bank(key):
                    n = ring[key]
                    if n >= 4:
                        pe.wait_ge(ring_free, n - 3)
                    return ps[4 + n % 4]

                pe.wait_ge(acc_done, UB + 2 * STEPS)
                pe.wait_ge(m_lo, 1)
                pe.wait_ge(vec_done, DV - D)
                turn(0)
                residual(1)
                for c in range(CHUNKS):
                    diag = fast and 1 <= c <= HCH
                    k = c % HCH
                    ch = slice(CW * k, CW * k + CW)
                    if diag:
                        pe.wait_ge(dexp_done, CT * c)
                        o = bank(("PT", c - 1))
                        for b in range(CT):
                            last = pe.transpose(o[:, P * b:P * b + P], Ed[:, b, :], ident[:, :])
                        last.then_inc(ring_full, 1)
                    tail = fast and c == CHUNKS - 1
                    if tail:
                        pe.wait_ge(x1_done, CT * CHUNKS)
                        score_bank(0, 0)
                        score_bank(0, 1)
                    pe.wait_ge(ht_lo, KD * (c + 1))
                    for oh in range(KD):
                        o = bank(("q", c, oh))
                        for kk in range(KD):
                            w = slice(P * oh, P * oh + P)
                            last = mm3(pe, o[:, :], Mhi[:, kk, w], Mlo[:, kk, w], KTh[:, kk, ch], KTl[:, kk, ch],
                                       kk == 0, kk == KD - 1)
                        last.then_inc(ring_full, 1)
                    if diag:
                        pe.wait_ge(ring_free, ring[("PT", c - 1)] + 1)
                        kd = (c - 1) % HCH
                        for b in range(CT):
                            if b % 2 == 0:
                                o = bank(("O", c - 1, b // 2))
                            last = mm3(pe, o[:, D * (b % 2):D * (b % 2) + D],
                                       PTdh[:, P * b:P * b + P], PTdl[:, P * b:P * b + P],
                                       Vh[:, CT * kd + b, :], Vl[:, CT * kd + b, :], True, True)
                            if b % 2:
                                last.then_inc(ring_full, 1)
                    if tail:
                        score_bank(0, 2)
                        score_bank(0, 3)
                    for b in range(CT):
                        o = bank(("v", c, b))[:, 0:DV]
                        w = slice(CW * k + P * b, CW * k + P * b + P)
                        pe.matmul(o, pick[:, :], bvr[:, :], start=True, stop=False)
                        for kk in range(KD):
                            last = mm3(pe, o, KTh[:, kk, w], KTl[:, kk, w], Vwh[:, kk, :], Vwl[:, kk, :],
                                       False, kk == KD - 1)
                        last.then_inc(ring_full, 1)
                    if fast and c < HCH:
                        pe.wait_ge(ring_free, ring[("q", c, 1)] + 1)
                        o = bank(("S", c))
                        for b in range(CT):
                            w = slice(CW * k + P * b, CW * k + P * b + P)
                            for oh in range(KD):
                                last = mm3(pe, o[:, P * b:P * b + P], QTh[:, oh, w], QTl[:, oh, w],
                                           KTh[:, oh, w], KTl[:, oh, w], oh == 0, oh == KD - 1)
                        last.then_inc(ring_full, 1)
                    ahead = 0 if fast and c < HCH else CT // 2
                    if c + 2 < CHUNKS:
                        residual(c + 2, range(ahead))
                    if c + 1 < CHUNKS:
                        turn(c + 1)
                    if c + 2 < CHUNKS:
                        residual(c + 2, range(ahead, CT))
                if not fast:
                    pe.wait_ge(ring_free, len(ring))

            def ring_end(b):
                return len(RING[True]) - (len(RING[True]) - 1 - b) % 4

            def turn_quarter(i, q):
                if i == 0 and q < 2:
                    pe.wait_ge(ring_free, ring_end(q))
                if q == 0:
                    pe.wait_ge(e_done, i + 1)
                if 4 * i + q >= 2:
                    pe.wait_ge(pt_lo, 4 * i + q - 1)
                for b in range(4):
                    j = CW * q + P * b
                    last = pe.transpose(ps[4 + q % 2][:, P * b:P * b + P], SE[i % 2][:, j:j + P], ident[:, :])
                last.then_inc(pt_full, 1)

            def weigh_quarter(i, q):
                pe.wait_ge(pt_lo, 4 * i + q + 1)
                if q == 0:
                    pe.wait_ge(o_read, i - 1) if i >= 2 else pe.wait_ge(ring_free, ring_end(2 + i))
                for b in range(4):
                    w = slice(P * b, P * b + P)
                    last = mm3(pe, ps[6 + i % 2][:, 0:D], PTh[q % 2][:, w], PTl[q % 2][:, w],
                               Vh[:, 4 * q + b, :], Vl[:, 4 * q + b, :], q == 0 and b == 0, q == 3 and b == 3)
                if q == 3:
                    last.then_inc(o_full, 1)

            with pe.If(fast_reg == 1):
                chunks(True)
                for i in range(HT):
                    for q in range(4):
                        if i + 1 < HT and q < 3:
                            score_bank(i + 1, q)
                        turn_quarter(i, q)
                        if i + 1 < HT and q == 3:
                            score_bank(i + 1, q)
                        if q:
                            weigh_quarter(i, q - 1)
                    weigh_quarter(i, 3)
            with pe.Else():
                chunks(False)
                with pe.Fori(0, TILES) as t:
                    with pe.Fori(0, CHUNKS) as c:
                        n = t * CHUNKS + c
                        pe.wait_ge(g_load, n * 128 + 128)
                        for oh in range(KD):
                            last = mm3(pe, ps[0][:, :], QTh[:, oh, 0:P], QTl[:, oh, 0:P], KTh[:, oh, 0:CW],
                                       KTl[:, oh, 0:CW], oh == 0, oh == KD - 1)
                        last.then_inc(g_score, 1)
                        pe.wait_ge(g_exp, n * 2 + 2)
                        for b in range(4):
                            last = pe.transpose(ps[4][:, P * b:P * b + P], SE[1][:, P * b:P * b + P], ident[:, :])
                        last.then_inc(g_tr, 1)
                        pe.wait_ge(g_plo, n + 1)
                        for b in range(4):
                            last = mm3(pe, ps[6][:, 0:D], PTh[0][:, P * b:P * b + P], PTl[0][:, P * b:P * b + P],
                                       Vh[:, b, :], Vl[:, b, :], b == 0, b == 3)
                        last.then_inc(g_pv, 1)
                pe.nop()


def kernel(x, adj, L0_gnn_W, L0_gnn_b, L1_gnn_ptr, L1_gnn_Wq, L1_gnn_bq, L1_gnn_Wk, L1_gnn_bk, L1_gnn_Wv, L1_gnn_bv):
    import numpy as _np
    import concourse.bacc as _bacc
    from concourse import mybir as _mybir
    from concourse.bass_utils import run_bass_kernel_spmd as _run

    a = _np.asarray(adj)
    blocks = a.reshape(CHUNKS, CW, 2, GROUPS, GRP // 2, P).transpose(3, 0, 5, 4, 2, 1).reshape(STEPS * P, GRP * CW)
    ins = {
        "x": x, "adj": a, "adjT": blocks, "W0T": _np.asarray(L0_gnn_W).T, "b0": L0_gnn_b,
        "ptr": _np.asarray(L1_gnn_ptr).reshape(NPTR, 1), "Wq": L1_gnn_Wq, "bq": _np.asarray(L1_gnn_bq).reshape(KD, P).T,
        "Wk": L1_gnn_Wk, "bk": _np.asarray(L1_gnn_bk).reshape(KD, P).T,
        "WvT": _np.asarray(L1_gnn_Wv).T, "bv": L1_gnn_bv,
    }
    nc = _bacc.Bacc("TRN2", target_bir_lowering=False, num_devices=1)
    arrays, args = {}, {}
    for name, value in ins.items():
        value = _np.ascontiguousarray(value)
        arrays[f"in_{name}_dram"] = value
        args[name] = nc.dram_tensor(f"in_{name}_dram", value.shape, _mybir.dt.from_np(value.dtype),
                                    kind="ExternalInput").ap()
    out = nc.dram_tensor("out_0_dram", (N, D), _mybir.dt.float32, kind="ExternalOutput").ap()
    gnn_kernel(nc, out=out, **args)
    r = _run(nc, [arrays], core_ids=[0])
    return r.results[0]["out_0_dram"]
```
